# Optimizing a Trainium2 kernel written in Bass

```python
import numpy as np
import jax
import jax.numpy as jnp

def _softmax(x, axis=-1):
    return jax.nn.softmax(x, axis=axis)

def _gelu(x):
    return jax.nn.gelu(x, approximate=True)

def _silu(x):
    return jax.nn.silu(x)

def _sigmoid(x):
    return jax.nn.sigmoid(x)

def _layernorm(x, axis=-1, eps=1e-05):
    m = jnp.mean(x, axis=axis, keepdims=True)
    v = jnp.var(x, axis=axis, keepdims=True)
    return (x - m) / jnp.sqrt(v + eps)

def _scatter_add(tgt, idx, src, axis=0):
    return tgt.at[idx].add(src)

def _segment_sum(src, seg, n):
    return jax.ops.segment_sum(src, seg, n)
kernel_name = 'mk_xattn_ffn_d4_seqx_r4_09db22'

def setup_inputs(seed: int=0):
    np.random.seed(seed)
    _w = jnp.asarray

    def _rec_inputs():
        import jax
        import jax.numpy as jnp
        _rk = jax.random.key(seed)
        x = -0.0002928 + 1 * jax.random.normal(jax.random.fold_in(_rk, 1), (4, 512, 256), jnp.float32)
        _lenS = 512 - jax.random.randint(jax.random.fold_in(_rk, 7), (4,), 0, max(1, 512 // 4) + 1, jnp.int32)
        _lenS2 = 64 - jax.random.randint(jax.random.fold_in(_rk, 8), (4,), 0, max(1, 64 // 4) + 1, jnp.int32)
        _ctx_1024P = jax.random.normal(jax.random.fold_in(_rk, 11), (4, 16, 256), jnp.float32)
        _ctx_1024c = jax.random.dirichlet(jax.random.fold_in(_rk, 511), 0.3 * jnp.ones((16,), jnp.float32), (4, 64))
        _ctx_1024t = jnp.einsum('bsk,bkd->bsd', _ctx_1024c, _ctx_1024P)
        _ctx_1024t = _ctx_1024t * jax.lax.rsqrt(jnp.mean(jnp.square(_ctx_1024t)) + 1e-12) * 0.953939
        ctx_1024 = -1.39393e-06 + 0.999914 * (_ctx_1024t + 0.3 * jax.random.normal(jax.random.fold_in(_rk, 611), (4, 64, 256), jnp.float32))
        return (x, ctx_1024)
    x, ctx_1024 = _rec_inputs()

    def _L0_xattn_setup():
        import jax, jax.numpy as jnp
        import numpy as np
        E = 256
        H = 16
        D = E // H
        key = jax.random.key(seed)
        ks = jax.random.split(key, 8)
        s = 0.02
        return {'layer_input': jax.random.normal(ks[0], (2, 512, E), jnp.float32), 'cross_attn_input': jax.random.normal(ks[1], (2, 512, E), jnp.float32), 'Wq': jax.random.normal(ks[2], (E, E), jnp.float32) * s, 'bq': jnp.zeros((E,), jnp.float32), 'Wkv': jax.random.normal(ks[3], (E, 2 * E), jnp.float32) * s, 'bkv': jnp.zeros((2 * E,), jnp.float32), 'Wo': jax.random.normal(ks[4], (E, E), jnp.float32) * s, 'bo': jnp.zeros((E,), jnp.float32)}
    _L0_xattn_all = _L0_xattn_setup()
    _L0_xattn_in = {k: v for k, v in _L0_xattn_all.items() if k in ('Wq', 'bq', 'Wkv', 'bkv', 'Wo', 'bo')}
    del _L0_xattn_all

    def _L0_ffn_setup():
        import jax, jax.numpy as jnp
        import numpy as np
        NUM_EXPERTS = 8
        TOP_K = 2
        B, T, D, F = (4, 512, 256, 704)
        key = jax.random.key(seed)
        ks = jax.random.split(key, 5)
        return {'x': jax.random.normal(ks[0], (B, T, D), dtype=jnp.float32), 'router_w': jax.random.normal(ks[1], (D, NUM_EXPERTS), dtype=jnp.float32) * 0.02, 'gate_proj': jax.random.normal(ks[2], (NUM_EXPERTS, D, F), dtype=jnp.float32) * 0.02, 'up_proj': jax.random.normal(ks[3], (NUM_EXPERTS, D, F), dtype=jnp.float32) * 0.02, 'down_proj': jax.random.normal(ks[4], (NUM_EXPERTS, F, D), dtype=jnp.float32) * 0.02}
    _L0_ffn_all = _L0_ffn_setup()
    _L0_ffn_in = {k: v for k, v in _L0_ffn_all.items() if k in ('router_w', 'gate_proj', 'up_proj', 'down_proj')}
    del _L0_ffn_all

    def _L1_xattn_setup():
        import jax, jax.numpy as jnp
        import numpy as np
        EMBED = 256
        HEADS = 16
        HEAD_DIM = EMBED // HEADS
        EXP_DIM = 2 * HEAD_DIM

        def _feature_map(x, fm_w, fm_b):
            z = jnp.einsum('nshd,ed->nshe', x, fm_w) + fm_b
            return jnp.concatenate([jnp.exp(z), jnp.exp(-z)], axis=-1)
        key = jax.random.key(seed)
        ks = jax.random.split(key, 7)
        N, S = (4, 512)
        values = jax.random.normal(ks[0], (N, S, EMBED), dtype=jnp.float32)
        keys_ = jax.random.normal(ks[1], (N, S, EMBED), dtype=jnp.float32)
        query = jax.random.normal(ks[2], (N, S, EMBED), dtype=jnp.float32)
        fm_w = jnp.eye(HEAD_DIM, dtype=jnp.float32) + 0.02 * jax.random.normal(ks[3], (HEAD_DIM, HEAD_DIM), dtype=jnp.float32)
        fm_b = 0.02 * jax.random.normal(ks[4], (HEAD_DIM,), dtype=jnp.float32)
        fc_w = jax.random.normal(ks[5], (EMBED, HEADS * EXP_DIM), dtype=jnp.float32) * (1.0 / np.sqrt(HEADS * EXP_DIM))
        fc_b = jnp.zeros((EMBED,), dtype=jnp.float32)
        return {'values': values, 'keys': keys_, 'query': query, 'fm_w': fm_w, 'fm_b': fm_b, 'fc_w': fc_w, 'fc_b': fc_b}
    _L1_xattn_all = _L1_xattn_setup()
    _L1_xattn_in = {k: v for k, v in _L1_xattn_all.items() if k in ('fm_w', 'fm_b', 'fc_w', 'fc_b')}
    del _L1_xattn_all

    def _L1_ffn_setup():
        import jax, jax.numpy as jnp
        import numpy as np
        H = 256
        NH = 16
        HD = H // NH
        HH = HD // 2
        L = H // 4
        I = int(H * 1.0)
        ER = 7
        TOPK = 2
        BASE = 10000.0
        EPS = 1e-05

        def rmsnorm(x, w):
            norm = jnp.sqrt(jnp.mean(x * x, axis=-1, keepdims=True)) + EPS
            return x / norm * w

        def rope_tables(seq_len):
            inv_freq = 1.0 / BASE ** (jnp.arange(0, HH, 2, dtype=jnp.float32) / HH)
            t = jnp.arange(seq_len, dtype=jnp.float32)
            freqs = jnp.einsum('i,j->ij', t, inv_freq)
            emb = jnp.concatenate([freqs, freqs], axis=-1)
            cos = jnp.cos(emb)[None, :, None, :]
            sin = jnp.sin(emb)[None, :, None, :]
            return (cos, sin)

        def rotate_half(x):
            x1, x2 = jnp.split(x, 2, axis=-1)
            return jnp.concatenate([-x2, x1], axis=-1)

        def silu(x):
            return x * jax.nn.sigmoid(x)

        def mla(xn, W_kvd, W_qd, W_ku, W_qu, W_vu, W_ropeq, W_ropek, W_o):
            B, S, _ = xn.shape
            kv_lat = xn @ W_kvd
            q_lat = xn @ W_qd
            k = (kv_lat @ W_ku).reshape(B, S, NH, HH)
            q = (q_lat @ W_qu).reshape(B, S, NH, HH)
            v = (kv_lat @ W_vu).reshape(B, S, NH, HD)
            q_rope = (q_lat @ W_ropeq).reshape(B, S, NH, HH)
            k_rope = (xn @ W_ropek).reshape(B, S, NH, HH)
            cos, sin = rope_tables(S)
            k_rope = k_rope * cos + rotate_half(k_rope) * sin
            q_rope = q_rope * cos + rotate_half(q_rope) * sin
            kk = jnp.concatenate([k, k_rope], axis=-1)
            qq = jnp.concatenate([q, q_rope], axis=-1)
            scale = 1.0 / jnp.sqrt(jnp.float32(HD))
            scores = jnp.einsum('bqhd,bkhd->bhqk', qq, kk) * scale
            causal = jnp.tril(jnp.ones((S, S), dtype=bool))
            scores = jnp.where(causal[None, None], scores, jnp.finfo(scores.dtype).min)
            probs = jax.nn.softmax(scores, axis=-1)
            y = jnp.einsum('bhqk,bkhd->bqhd', probs, v).reshape(B, S, H)
            return y @ W_o

        def moe(xn, Wg_s, Wu_s, Wd_s, Wg_r, Wu_r, Wd_r, W_router, routing_bias):
            B, S, _ = xn.shape
            xt = xn.reshape(B * S, H)
            shared = silu(xt @ Wg_s) * (xt @ Wu_s) @ Wd_s
            logits = xt @ W_router + routing_bias
            probs = jax.nn.sigmoid(logits)
            scores, idx = jax.lax.top_k(probs, TOPK)
            scores = scores / jnp.sum(scores, axis=-1, keepdims=True)
            wts = jnp.sum(jax.nn.one_hot(idx, ER, dtype=xt.dtype) * scores[..., None], axis=1)
            g = jnp.einsum('th,ehi->tei', xt, Wg_r)
            u = jnp.einsum('th,ehi->tei', xt, Wu_r)
            hmid = silu(g) * u
            combined = jnp.einsum('tei,eih,te->th', hmid, Wd_r, wts)
            return (shared + combined).reshape(B, S, H)
        key = jax.random.key(seed)
        ks = jax.random.split(key, 20)
        s = 0.02
        r = lambda k, shp: jax.random.normal(k, shp, dtype=jnp.float32) * s
        return {'x': jax.random.normal(ks[0], (4, 256, H), dtype=jnp.float32), 'w_ln1': jnp.ones((H,), jnp.float32), 'w_ln2': jnp.ones((H,), jnp.float32), 'W_kvd': r(ks[1], (H, L)), 'W_qd': r(ks[2], (H, L)), 'W_ku': r(ks[3], (L, NH * HH)), 'W_qu': r(ks[4], (L, NH * HH)), 'W_vu': r(ks[5], (L, H)), 'W_ropeq': r(ks[6], (L, H // 2)), 'W_ropek': r(ks[7], (H, H // 2)), 'W_o': r(ks[8], (H, H)), 'Wg_s': r(ks[9], (H, I)), 'Wu_s': r(ks[10], (H, I)), 'Wd_s': r(ks[11], (I, H)), 'Wg_r': r(ks[12], (ER, H, I)), 'Wu_r': r(ks[13], (ER, H, I)), 'Wd_r': r(ks[14], (ER, I, H)), 'W_router': r(ks[15], (H, ER)), 'routing_bias': jnp.zeros((ER,), jnp.float32)}
    _L1_ffn_all = _L1_ffn_setup()
    _L1_ffn_in = {k: v for k, v in _L1_ffn_all.items() if k in ('w_ln1', 'w_ln2', 'W_kvd', 'W_qd', 'W_ku', 'W_qu', 'W_vu', 'W_ropeq', 'W_ropek', 'W_o', 'Wg_s', 'Wu_s', 'Wd_s', 'Wg_r', 'Wu_r', 'Wd_r', 'W_router', 'routing_bias')}
    del _L1_ffn_all

    def _L2_xattn_setup():
        import jax, jax.numpy as jnp
        import numpy as np
        EPS = 1e-12

        def _l2norm(x):
            n = jnp.linalg.norm(x, axis=-1, keepdims=True)
            return x / jnp.maximum(n, EPS)
        key = jax.random.key(seed)
        k1, k2 = jax.random.split(key)
        img_feat = jax.random.normal(k1, (8, 1024, 256), dtype=jnp.float32)
        text_feat = jax.random.normal(k2, (8, 128, 256), dtype=jnp.float32)
        return {'img_feat': img_feat, 'text_feat': text_feat}
    _L2_xattn_all = _L2_xattn_setup()
    _L2_xattn_in = {k: v for k, v in _L2_xattn_all.items() if k in ()}
    del _L2_xattn_all

    def _L2_ffn_setup():
        import jax, jax.numpy as jnp
        import numpy as np
        BLOCK = 16
        _GRID = jnp.array([0.0, 0.5, 1.0, 1.5, 2.0, 3.0, 4.0, 6.0], dtype=jnp.float32)
        _MID = jnp.array([0.25, 0.75, 1.25, 1.75, 2.5, 3.5, 5.0], dtype=jnp.float32)

        def fp4_quant_dequant(x):
            shape = x.shape
            xb = x.reshape(shape[:-1] + (shape[-1] // BLOCK, BLOCK))
            scale = jnp.max(jnp.abs(xb), axis=-1, keepdims=True) / 6.0
            scale = jnp.maximum(scale, jnp.float32(1e-12))
            xn = xb / scale
            idx = jnp.searchsorted(_MID, jnp.abs(xn))
            q = _GRID[idx] * jnp.sign(xn) * scale
            return q.reshape(shape)

        def fp4_linear(x, w):
            xq = fp4_quant_dequant(x)
            wq = fp4_quant_dequant(w)
            return jnp.einsum('bsk,nk->bsn', xq, wq)
        key = jax.random.key(seed)
        k1, k2, k3, k4 = jax.random.split(key, 4)
        H, I = (256, 704)
        x = jax.random.normal(k1, (4, 1024, H), dtype=jnp.float32)
        w_gate = jax.random.normal(k2, (I, H), dtype=jnp.float32) * 0.02
        w_up = jax.random.normal(k3, (I, H), dtype=jnp.float32) * 0.02
        w_down = jax.random.normal(k4, (H, I), dtype=jnp.float32) * 0.02
        return {'x': x, 'w_gate': w_gate, 'w_up': w_up, 'w_down': w_down}
    _L2_ffn_all = _L2_ffn_setup()
    _L2_ffn_in = {k: v for k, v in _L2_ffn_all.items() if k in ('w_gate', 'w_up', 'w_down')}
    del _L2_ffn_all

    def _L3_xattn_setup():
        import jax, jax.numpy as jnp
        import numpy as np
        D_MODEL = 256
        N_HEAD = 16

        def _split_heads(x, n_head):
            b, s, d = x.shape
            return x.reshape(b, s, n_head, d // n_head).transpose(0, 2, 1, 3)
        key = jax.random.key(seed)
        ks = jax.random.split(key, 11)
        b, s, d = (4, 512, D_MODEL)
        scale = 1.0 / np.sqrt(d)
        inp = {'q': jax.random.normal(ks[0], (b, s, d), dtype=jnp.float32), 'k': jax.random.normal(ks[1], (b, s, d), dtype=jnp.float32), 'v': jax.random.normal(ks[2], (b, s, d), dtype=jnp.float32), 'w_q': jax.random.normal(ks[3], (d, d), dtype=jnp.float32) * scale, 'b_q': jnp.zeros((d,), dtype=jnp.float32), 'w_k': jax.random.normal(ks[4], (d, d), dtype=jnp.float32) * scale, 'b_k': jnp.zeros((d,), dtype=jnp.float32), 'w_v': jax.random.normal(ks[5], (d, d), dtype=jnp.float32) * scale, 'b_v': jnp.zeros((d,), dtype=jnp.float32), 'w_o': jax.random.normal(ks[6], (d, d), dtype=jnp.float32) * scale, 'b_o': jnp.zeros((d,), dtype=jnp.float32)}
        return inp
    _L3_xattn_all = _L3_xattn_setup()
    _L3_xattn_in = {k: v for k, v in _L3_xattn_all.items() if k in ('w_q', 'b_q', 'w_k', 'b_k', 'w_v', 'b_v', 'w_o', 'b_o')}
    del _L3_xattn_all

    def _L3_ffn_setup():
        import jax, jax.numpy as jnp
        import numpy as np
        E = 8
        TOP_K = 2
        DIM = 256
        HID = 512
        key = jax.random.key(seed)
        k1, k2, k3, k4, k5 = jax.random.split(key, 5)
        s = 0.02
        x = jax.random.normal(k1, (2, 512, DIM), dtype=jnp.float32)
        Wg = jax.random.normal(k2, (DIM, E), dtype=jnp.float32) * s
        W1 = jax.random.normal(k3, (E, DIM, HID), dtype=jnp.float32) * s
        W2 = jax.random.normal(k4, (E, DIM, HID), dtype=jnp.float32) * s
        W3 = jax.random.normal(k5, (E, HID, DIM), dtype=jnp.float32) * s
        return {'x': x, 'Wg': Wg, 'W1': W1, 'W2': W2, 'W3': W3}
    _L3_ffn_all = _L3_ffn_setup()
    _L3_ffn_in = {k: v for k, v in _L3_ffn_all.items() if k in ('Wg', 'W1', 'W2', 'W3')}
    del _L3_ffn_all
    return {'x': x, 'ctx_1024': ctx_1024, 'L0_xattn_Wq': _L0_xattn_in['Wq'], 'L0_xattn_bq': _L0_xattn_in['bq'], 'L0_xattn_Wkv': _L0_xattn_in['Wkv'], 'L0_xattn_bkv': _L0_xattn_in['bkv'], 'L0_xattn_Wo': _L0_xattn_in['Wo'], 'L0_xattn_bo': _L0_xattn_in['bo'], 'L0_ffn_router_w': _L0_ffn_in['router_w'], 'L0_ffn_gate_proj': _L0_ffn_in['gate_proj'], 'L0_ffn_up_proj': _L0_ffn_in['up_proj'], 'L0_ffn_down_proj': _L0_ffn_in['down_proj'], 'L1_xattn_fm_w': _L1_xattn_in['fm_w'], 'L1_xattn_fm_b': _L1_xattn_in['fm_b'], 'L1_xattn_fc_w': _L1_xattn_in['fc_w'], 'L1_xattn_fc_b': _L1_xattn_in['fc_b'], 'L1_ffn_w_ln1': _L1_ffn_in['w_ln1'], 'L1_ffn_w_ln2': _L1_ffn_in['w_ln2'], 'L1_ffn_W_kvd': _L1_ffn_in['W_kvd'], 'L1_ffn_W_qd': _L1_ffn_in['W_qd'], 'L1_ffn_W_ku': _L1_ffn_in['W_ku'], 'L1_ffn_W_qu': _L1_ffn_in['W_qu'], 'L1_ffn_W_vu': _L1_ffn_in['W_vu'], 'L1_ffn_W_ropeq': _L1_ffn_in['W_ropeq'], 'L1_ffn_W_ropek': _L1_ffn_in['W_ropek'], 'L1_ffn_W_o': _L1_ffn_in['W_o'], 'L1_ffn_Wg_s': _L1_ffn_in['Wg_s'], 'L1_ffn_Wu_s': _L1_ffn_in['Wu_s'], 'L1_ffn_Wd_s': _L1_ffn_in['Wd_s'], 'L1_ffn_Wg_r': _L1_ffn_in['Wg_r'], 'L1_ffn_Wu_r': _L1_ffn_in['Wu_r'], 'L1_ffn_Wd_r': _L1_ffn_in['Wd_r'], 'L1_ffn_W_router': _L1_ffn_in['W_router'], 'L1_ffn_routing_bias': _L1_ffn_in['routing_bias'], 'L2_ffn_w_gate': _L2_ffn_in['w_gate'], 'L2_ffn_w_up': _L2_ffn_in['w_up'], 'L2_ffn_w_down': _L2_ffn_in['w_down'], 'L3_xattn_w_q': _L3_xattn_in['w_q'], 'L3_xattn_b_q': _L3_xattn_in['b_q'], 'L3_xattn_w_k': _L3_xattn_in['w_k'], 'L3_xattn_b_k': _L3_xattn_in['b_k'], 'L3_xattn_w_v': _L3_xattn_in['w_v'], 'L3_xattn_b_v': _L3_xattn_in['b_v'], 'L3_xattn_w_o': _L3_xattn_in['w_o'], 'L3_xattn_b_o': _L3_xattn_in['b_o'], 'L3_ffn_Wg': _L3_ffn_in['Wg'], 'L3_ffn_W1': _L3_ffn_in['W1'], 'L3_ffn_W2': _L3_ffn_in['W2'], 'L3_ffn_W3': _L3_ffn_in['W3']}

def reference(x, ctx_1024, L0_xattn_Wq, L0_xattn_bq, L0_xattn_Wkv, L0_xattn_bkv, L0_xattn_Wo, L0_xattn_bo, L0_ffn_router_w, L0_ffn_gate_proj, L0_ffn_up_proj, L0_ffn_down_proj, L1_xattn_fm_w, L1_xattn_fm_b, L1_xattn_fc_w, L1_xattn_fc_b, L1_ffn_w_ln1, L1_ffn_w_ln2, L1_ffn_W_kvd, L1_ffn_W_qd, L1_ffn_W_ku, L1_ffn_W_qu, L1_ffn_W_vu, L1_ffn_W_ropeq, L1_ffn_W_ropek, L1_ffn_W_o, L1_ffn_Wg_s, L1_ffn_Wu_s, L1_ffn_Wd_s, L1_ffn_Wg_r, L1_ffn_Wu_r, L1_ffn_Wd_r, L1_ffn_W_router, L1_ffn_routing_bias, L2_ffn_w_gate, L2_ffn_w_up, L2_ffn_w_down, L3_xattn_w_q, L3_xattn_b_q, L3_xattn_w_k, L3_xattn_b_k, L3_xattn_w_v, L3_xattn_b_v, L3_xattn_w_o, L3_xattn_b_o, L3_ffn_Wg, L3_ffn_W1, L3_ffn_W2, L3_ffn_W3):
    import jax
    import jax.numpy as jnp

    def _L0_xattn_ref(layer_input, cross_attn_input, Wq, bq, Wkv, bkv, Wo, bo):
        import jax, jax.numpy as jnp
        import numpy as np
        E = 256
        H = 16
        D = E // H
        scale = D ** (-0.5)
        q = layer_input @ Wq + bq
        kv = cross_attn_input @ Wkv + bkv
        k, v = jnp.split(kv, 2, axis=-1)

        def split_heads(x):
            b, s, _ = x.shape
            return x.reshape(b, s, H, D).transpose(0, 2, 1, 3)
        q, k, v = map(split_heads, (q, k, v))
        scores = jnp.einsum('bhqd,bhkd->bhqk', q, k) * scale
        weights = jax.nn.softmax(scores, axis=-1)
        out = jnp.einsum('bhqk,bhkd->bhqd', weights, v)
        b, h, sq, d = out.shape
        out = out.transpose(0, 2, 1, 3).reshape(b, sq, E)
        return out @ Wo + bo

    def _L0_ffn_ref(x, router_w, gate_proj, up_proj, down_proj):
        import jax, jax.numpy as jnp
        import numpy as np
        NUM_EXPERTS = 8
        TOP_K = 2
        B, T, D, F = (4, 512, 256, 704)
        scores = jnp.einsum('btd,de->bte', x, router_w).astype(jnp.float32)
        probs = jax.nn.softmax(scores, axis=-1)
        routing_weights, routing_idx = jax.lax.top_k(probs, TOP_K)
        routing_weights = (routing_weights / jnp.sum(routing_weights, axis=-1, keepdims=True)).astype(x.dtype)
        one_hot = jax.nn.one_hot(routing_idx, NUM_EXPERTS, dtype=x.dtype)
        expert_w = jnp.einsum('btke,btk->bte', one_hot, routing_weights)
        dispatched = jnp.einsum('btd,btke->bted', x, one_hot)
        gate = jnp.einsum('bted,edf->btef', dispatched, gate_proj)
        up = jnp.einsum('bted,edf->btef', dispatched, up_proj)
        acts = jax.nn.silu(gate) * up
        expert_out = jnp.einsum('btef,efd->bted', acts, down_proj)
        return jnp.einsum('bted,bte->btd', expert_out, expert_w)

    def _L1_xattn_ref(values, keys, query, fm_w, fm_b, fc_w, fc_b):
        import jax, jax.numpy as jnp
        import numpy as np
        EMBED = 256
        HEADS = 16
        HEAD_DIM = EMBED // HEADS
        EXP_DIM = 2 * HEAD_DIM

        def _feature_map(x, fm_w, fm_b):
            z = jnp.einsum('nshd,ed->nshe', x, fm_w) + fm_b
            return jnp.concatenate([jnp.exp(z), jnp.exp(-z)], axis=-1)
        N, S, _ = query.shape
        v = values.reshape(N, -1, HEADS, HEAD_DIM)
        k = keys.reshape(N, -1, HEADS, HEAD_DIM)
        q = query.reshape(N, -1, HEADS, HEAD_DIM)
        v, k, q = (_feature_map(x, fm_w, fm_b) for x in (v, k, q))
        scores = jnp.einsum('nqhd,nkhd->nhqk', q, k) / jnp.sqrt(jnp.float32(EMBED))
        attn = jax.nn.softmax(scores, axis=-1)
        out = jnp.einsum('nhql,nlhd->nqhd', attn, v)
        out = out.reshape(N, S, HEADS * EXP_DIM)
        return out @ fc_w.T + fc_b

    def _L1_ffn_ref(x, w_ln1, w_ln2, W_kvd, W_qd, W_ku, W_qu, W_vu, W_ropeq, W_ropek, W_o, Wg_s, Wu_s, Wd_s, Wg_r, Wu_r, Wd_r, W_router, routing_bias):
        import jax, jax.numpy as jnp
        import numpy as np
        H = 256
        NH = 16
        HD = H // NH
        HH = HD // 2
        L = H // 4
        I = int(H * 1.0)
        ER = 7
        TOPK = 2
        BASE = 10000.0
        EPS = 1e-05

        def rmsnorm(x, w):
            norm = jnp.sqrt(jnp.mean(x * x, axis=-1, keepdims=True)) + EPS
            return x / norm * w

        def rope_tables(seq_len):
            inv_freq = 1.0 / BASE ** (jnp.arange(0, HH, 2, dtype=jnp.float32) / HH)
            t = jnp.arange(seq_len, dtype=jnp.float32)
            freqs = jnp.einsum('i,j->ij', t, inv_freq)
            emb = jnp.concatenate([freqs, freqs], axis=-1)
            cos = jnp.cos(emb)[None, :, None, :]
            sin = jnp.sin(emb)[None, :, None, :]
            return (cos, sin)

        def rotate_half(x):
            x1, x2 = jnp.split(x, 2, axis=-1)
            return jnp.concatenate([-x2, x1], axis=-1)

        def silu(x):
            return x * jax.nn.sigmoid(x)

        def mla(xn, W_kvd, W_qd, W_ku, W_qu, W_vu, W_ropeq, W_ropek, W_o):
            B, S, _ = xn.shape
            kv_lat = xn @ W_kvd
            q_lat = xn @ W_qd
            k = (kv_lat @ W_ku).reshape(B, S, NH, HH)
            q = (q_lat @ W_qu).reshape(B, S, NH, HH)
            v = (kv_lat @ W_vu).reshape(B, S, NH, HD)
            q_rope = (q_lat @ W_ropeq).reshape(B, S, NH, HH)
            k_rope = (xn @ W_ropek).reshape(B, S, NH, HH)
            cos, sin = rope_tables(S)
            k_rope = k_rope * cos + rotate_half(k_rope) * sin
            q_rope = q_rope * cos + rotate_half(q_rope) * sin
            kk = jnp.concatenate([k, k_rope], axis=-1)
            qq = jnp.concatenate([q, q_rope], axis=-1)
            scale = 1.0 / jnp.sqrt(jnp.float32(HD))
            scores = jnp.einsum('bqhd,bkhd->bhqk', qq, kk) * scale
            causal = jnp.tril(jnp.ones((S, S), dtype=bool))
            scores = jnp.where(causal[None, None], scores, jnp.finfo(scores.dtype).min)
            probs = jax.nn.softmax(scores, axis=-1)
            y = jnp.einsum('bhqk,bkhd->bqhd', probs, v).reshape(B, S, H)
            return y @ W_o

        def moe(xn, Wg_s, Wu_s, Wd_s, Wg_r, Wu_r, Wd_r, W_router, routing_bias):
            B, S, _ = xn.shape
            xt = xn.reshape(B * S, H)
            shared = silu(xt @ Wg_s) * (xt @ Wu_s) @ Wd_s
            logits = xt @ W_router + routing_bias
            probs = jax.nn.sigmoid(logits)
            scores, idx = jax.lax.top_k(probs, TOPK)
            scores = scores / jnp.sum(scores, axis=-1, keepdims=True)
            wts = jnp.sum(jax.nn.one_hot(idx, ER, dtype=xt.dtype) * scores[..., None], axis=1)
            g = jnp.einsum('th,ehi->tei', xt, Wg_r)
            u = jnp.einsum('th,ehi->tei', xt, Wu_r)
            hmid = silu(g) * u
            combined = jnp.einsum('tei,eih,te->th', hmid, Wd_r, wts)
            return (shared + combined).reshape(B, S, H)
        x = x + mla(rmsnorm(x, w_ln1), W_kvd, W_qd, W_ku, W_qu, W_vu, W_ropeq, W_ropek, W_o)
        x = x + moe(rmsnorm(x, w_ln2), Wg_s, Wu_s, Wd_s, Wg_r, Wu_r, Wd_r, W_router, routing_bias)
        return x

    def _L2_xattn_ref(img_feat, text_feat):
        import jax, jax.numpy as jnp
        import numpy as np
        EPS = 1e-12

        def _l2norm(x):
            n = jnp.linalg.norm(x, axis=-1, keepdims=True)
            return x / jnp.maximum(n, EPS)
        img_norm = _l2norm(img_feat)
        text_norm = _l2norm(text_feat)
        sim = jnp.einsum('bic,btc->bit', img_norm, text_norm)
        min_idx = jnp.argmax(sim, axis=-1)
        text_aligned = jnp.take_along_axis(text_feat, min_idx[..., None], axis=1)
        return text_aligned

    def _L2_ffn_ref(x, w_gate, w_up, w_down):
        import jax, jax.numpy as jnp
        import numpy as np
        BLOCK = 16
        _GRID = jnp.array([0.0, 0.5, 1.0, 1.5, 2.0, 3.0, 4.0, 6.0], dtype=jnp.float32)
        _MID = jnp.array([0.25, 0.75, 1.25, 1.75, 2.5, 3.5, 5.0], dtype=jnp.float32)

        def fp4_quant_dequant(x):
            shape = x.shape
            xb = x.reshape(shape[:-1] + (shape[-1] // BLOCK, BLOCK))
            scale = jnp.max(jnp.abs(xb), axis=-1, keepdims=True) / 6.0
            scale = jnp.maximum(scale, jnp.float32(1e-12))
            xn = xb / scale
            idx = jnp.searchsorted(_MID, jnp.abs(xn))
            q = _GRID[idx] * jnp.sign(xn) * scale
            return q.reshape(shape)

        def fp4_linear(x, w):
            xq = fp4_quant_dequant(x)
            wq = fp4_quant_dequant(w)
            return jnp.einsum('bsk,nk->bsn', xq, wq)
        gate = fp4_linear(x, w_gate)
        y = fp4_linear(x, w_up)
        h = jax.nn.silu(gate) * y
        return fp4_linear(h, w_down)

    def _L3_xattn_ref(q, k, v, w_q, b_q, w_k, b_k, w_v, b_v, w_o, b_o):
        import jax, jax.numpy as jnp
        import numpy as np
        D_MODEL = 256
        N_HEAD = 16

        def _split_heads(x, n_head):
            b, s, d = x.shape
            return x.reshape(b, s, n_head, d // n_head).transpose(0, 2, 1, 3)
        qp = q @ w_q.T + b_q
        kp = k @ w_k.T + b_k
        vp = v @ w_v.T + b_v
        qh = _split_heads(qp, N_HEAD)
        kh = _split_heads(kp, N_HEAD)
        vh = _split_heads(vp, N_HEAD)
        d_k = kh.shape[-1]
        scores = jnp.einsum('bhqd,bhkd->bhqk', qh, kh) / jnp.sqrt(jnp.float32(d_k))
        attn = jax.nn.softmax(scores, axis=-1)
        out = jnp.einsum('bhqk,bhkd->bhqd', attn, vh)
        b, h, s, dk = out.shape
        out = out.transpose(0, 2, 1, 3).reshape(b, s, h * dk)
        return out @ w_o.T + b_o

    def _L3_ffn_ref(x, Wg, W1, W2, W3):
        import jax, jax.numpy as jnp
        import numpy as np
        E = 8
        TOP_K = 2
        DIM = 256
        HID = 512
        B, T, C = x.shape
        xf = x.reshape(-1, C)
        logits = xf @ Wg
        top_w, top_i = jax.lax.top_k(logits, TOP_K)
        top_w = jax.nn.softmax(top_w, axis=-1)
        one_hot = jax.nn.one_hot(top_i, E, dtype=xf.dtype)
        combine = jnp.einsum('nk,nke->ne', top_w, one_hot)
        h = jnp.einsum('nc,ech->enh', xf, W1)
        g = jnp.einsum('nc,ech->enh', xf, W2)
        y = jnp.einsum('enh,ehc->enc', jax.nn.silu(h) * g, W3)
        out = jnp.einsum('enc,ne->nc', y, combine)
        return out.reshape(B, T, C)
    x = x + _L0_xattn_ref(_layernorm(x, axis=-1), ctx_1024, L0_xattn_Wq, L0_xattn_bq, L0_xattn_Wkv, L0_xattn_bkv, L0_xattn_Wo, L0_xattn_bo)
    x = x + _L0_ffn_ref(_layernorm(x, axis=-1), L0_ffn_router_w, L0_ffn_gate_proj, L0_ffn_up_proj, L0_ffn_down_proj)
    x = x + _L1_xattn_ref(ctx_1024, ctx_1024, _layernorm(x, axis=-1), L1_xattn_fm_w, L1_xattn_fm_b, L1_xattn_fc_w, L1_xattn_fc_b)
    x = x + _L1_ffn_ref(_layernorm(x, axis=-1), L1_ffn_w_ln1, L1_ffn_w_ln2, L1_ffn_W_kvd, L1_ffn_W_qd, L1_ffn_W_ku, L1_ffn_W_qu, L1_ffn_W_vu, L1_ffn_W_ropeq, L1_ffn_W_ropek, L1_ffn_W_o, L1_ffn_Wg_s, L1_ffn_Wu_s, L1_ffn_Wd_s, L1_ffn_Wg_r, L1_ffn_Wu_r, L1_ffn_Wd_r, L1_ffn_W_router, L1_ffn_routing_bias)
    x = x + _L2_xattn_ref(_layernorm(x, axis=-1), ctx_1024)
    x = x + _L2_ffn_ref(_layernorm(x, axis=-1), L2_ffn_w_gate, L2_ffn_w_up, L2_ffn_w_down)
    x = x + _L3_xattn_ref(_layernorm(x, axis=-1), ctx_1024, ctx_1024, L3_xattn_w_q, L3_xattn_b_q, L3_xattn_w_k, L3_xattn_b_k, L3_xattn_w_v, L3_xattn_b_v, L3_xattn_w_o, L3_xattn_b_o)
    x = x + _L3_ffn_ref(_layernorm(x, axis=-1), L3_ffn_Wg, L3_ffn_W1, L3_ffn_W2, L3_ffn_W3)
    return x

_drawn_inputs = setup_inputs


def setup_inputs(seed=0):
    import zlib

    import numpy as np

    out = dict(_drawn_inputs(seed))
    spreads = {'L0_xattn_bq': (0.0, 0.8),
     'L0_xattn_bkv': (0.0, 0.1),
     'L0_xattn_bo': (0.0, 0.1),
     'L1_xattn_fc_b': (0.0, 0.443),
     'L1_ffn_w_ln1': (1.0, 0.6),
     'L1_ffn_w_ln2': (1.0, 0.6),
     'L1_ffn_routing_bias': (0.0, 0.8),
     'L3_xattn_b_q': (0.0, 2.0),
     'L3_xattn_b_k': (0.0, 2.0),
     'L3_xattn_b_v': (0.0, 2.0),
     'L3_xattn_b_o': (0.0, 2.0)}
    factors = {'L0_xattn_Wq': 8.0,
     'L0_ffn_router_w': 3.071,
     'L0_ffn_gate_proj': 2.668,
     'L0_ffn_up_proj': 2.668,
     'L0_ffn_down_proj': 2.707,
     'L1_ffn_W_kvd': 8.0,
     'L1_ffn_W_qd': 8.0,
     'L1_ffn_W_ku': 8.0,
     'L1_ffn_W_qu': 8.0,
     'L1_ffn_W_vu': 8.0,
     'L1_ffn_W_ropeq': 8.0,
     'L1_ffn_W_ropek': 8.0,
     'L1_ffn_W_o': 8.0,
     'L1_ffn_Wg_s': 8.0,
     'L1_ffn_Wu_s': 8.0,
     'L1_ffn_Wd_s': 8.0,
     'L1_ffn_Wg_r': 8.0,
     'L1_ffn_Wu_r': 8.0,
     'L1_ffn_Wd_r': 8.0,
     'L1_ffn_W_router': 8.0,
     'L2_ffn_w_gate': 8.0,
     'L2_ffn_w_up': 8.0,
     'L2_ffn_w_down': 8.0,
     'L3_xattn_w_k': 2.922,
     'L3_ffn_Wg': 8.0,
     'L3_ffn_W1': 8.0,
     'L3_ffn_W2': 8.0,
     'L3_ffn_W3': 8.0}
    for name, (base, spread) in spreads.items():
        noise = np.random.default_rng([zlib.crc32(name.encode()), seed]).standard_normal(out[name].shape)
        drawn = base * np.exp(spread * noise) if base else spread * noise
        out[name] = jnp.asarray(drawn.astype(out[name].dtype))
    for name, factor in factors.items():
        out[name] = (out[name] * factor).astype(out[name].dtype)
    return out
```

```python
from contextlib import ExitStack

import numpy as np
import concourse.bass as bass
from concourse import mybir

ALU = mybir.AluOpType
ACT = mybir.ActivationFunctionType
F32 = mybir.dt.float32
BF16 = mybir.dt.bfloat16
I32 = mybir.dt.int32
U32 = mybir.dt.uint32
AX_X = mybir.AxisListType.X

P = 128
B, S, D = 4, 512, 256
T = B * S // P
TB = S // P
KC = D // P
L = 64
H, HD = 16, 16
HC = H // KC
SCALE = HD ** -0.5
LAT = 64
HH = HD // 2
NE = 8
TOP = 2
LN_EPS, RMS_EPS, L2_EPS = 1e-5, 1e-5, 1e-12
ROUTED = (TOP * B * S + NE * (P - 1)) // P
SHARED = T
SLOTS = (ROUTED + SHARED) * P
NEG = -1.0e30
FP4_BLOCK = 16

CONST = {}


def _constants():
    p = np.arange(P)
    parts = {
        "ident": np.eye(P),
        "before": (p[:, None] < p[None, :]),
        "ones": np.ones((P, P)),
        "causal": np.where(p[:, None] >= p[None, :], 0.0, NEG),
        "head8": (p[:, None] // HD == np.arange(HC)[None, :]),
        "parity": (p[:, None] // L == np.arange(2)[None, :]),
        "iota8": np.tile(np.arange(NE), (P, 1)),
        "full": np.tile(np.arange(T) * P, (P, 1)),
        "iotab": np.tile(np.arange(ROUTED + SHARED), (P, 1)),
        "tri8": np.tile((np.arange(NE)[None, :] < np.arange(NE)[:, None]).ravel(), (P, 1)),
        "iota64": np.tile(np.arange(L), (P, 1)),
    }
    r = p % HD - HH
    inv = np.float32(1.0) / np.float32(10000.0) ** (np.arange(0, HH, 2, dtype=np.float32) / np.float32(HH))
    freqs = np.arange(S, dtype=np.float32)[None, :] * inv[r % (HH // 2)][:, None].astype(np.float32)
    parts["cos"] = np.where((r >= 0)[:, None], np.cos(freqs), 1.0)
    parts["sin"] = np.where((r >= 0)[:, None], np.sin(freqs), 0.0)
    at = 0
    for k, v in parts.items():
        CONST[k] = (at, at + v.shape[1])
        at += v.shape[1]
    return np.concatenate([np.asarray(v, np.float32) for v in parts.values()], axis=1)


def positive(n):
    return not isinstance(n, int) or n > 0


class Semaphores:

    def __init__(self, nc, stage, tag):
        self.nc, self.tag, self.made = nc, tag, []
        stage.callback(self.clear)

    def clear(self):
        for s in self.made:
            self.nc.gpsimd.sem_clear(s)
            self.nc.release_semaphore(s)

    def __call__(self, name):
        self.made.append(self.nc.alloc_semaphore(f"{self.tag}_{name}"))
        return self.made[-1]


def bcast(ap, axis, n):
    ap = ap.unsqueeze(axis)
    shape = list(ap.shape)
    shape[axis] = n
    return ap.broadcast_to(shape)


def program(nc, ins, out):
    ctx = ExitStack()
    with ctx:
        build(nc, ctx, ins, out)


def build(nc, ctx, ins, out):
    def sb(name, shape, dt=F32):
        return ctx.enter_context(nc.sbuf_tensor(name, shape, dt))

    consts = sb("consts", [P, ins["consts"].shape[1]])

    def const(k):
        return consts[:, CONST[k][0]:CONST[k][1]]

    ident, ones = const("ident"), const("ones")

    x = sb("x", [P, T, D])
    inner = sb("inner", [P, T, D])
    xn = sb("xn", [P, T, D])
    xnT = sb("xnT", [P, KC, T * P])
    ctx_tok = sb("ctx_tok", [L, B, D])
    ctxT = sb("ctxT", [P, KC, B, L])
    ctxT2 = sb("ctxT2", [P, KC, B, 2, L])
    ident_h = sb("ident_h", [P, P], BF16)
    causal_h = sb("causal_h", [P, P], BF16)
    x_slots = nc.dram_tensor("x_slots", [SLOTS, D], F32, kind="Internal").ap()
    y_slots = nc.dram_tensor("y_slots", [SLOTS, D], F32, kind="Internal").ap()

    RING = 8
    pool_sem = lambda n: ctx.enter_context(nc.semaphore(n))
    diag, rows_put = pool_sem("diag_loaded"), pool_sem("rows_put")
    rows_got = [pool_sem(f"rows_got{r}") for r in range(RING)]
    rows_out = [pool_sem(f"rows_out{j}") for j in range(2)]
    stored_before = [0, 0]

    class Small:
        pass
    w = Small()
    loads = []

    def matrix(name, n_in, n_out):
        t = sb(f"w_{name}", [P, n_in // P, n_out])
        loads.append((t[:], ins[name].rearrange("(k p) n -> p k n", p=P)))
        return t

    def rows(name, n_in, n_out):
        t = sb(f"w_{name}", [n_in, n_out])
        loads.append((t[:], ins[name]))
        return t

    def column(name, n):
        t = sb(f"c_{name}", [P, n // P])
        for k in range(n // P):
            loads.append((t[:, k:k + 1], ins[name][k * P:(k + 1) * P].rearrange("(p a) -> p a", a=1)))
        return t

    def row(name, n):
        t = sb(f"r_{name}", [1, n])
        loads.append((t[:], ins[name].rearrange("(a n) -> a n", a=1)))
        return t

    def spread(name, n):
        t = sb(f"s_{name}", [P, n])
        loads.append((t[:], ins[name].partition_broadcast(P)))
        return t

    w.q0, w.kv0, w.o0 = matrix("L0_xattn_Wq", D, D), matrix("L0_xattn_Wkv", D, 2 * D), matrix("L0_xattn_Wo", D, D)
    w.bq0, w.bk0 = column("L0_xattn_bq", D), column("L0_xattn_bk", D)
    w.bv0, w.bo0 = spread("L0_xattn_bv", D), row("L0_xattn_bo", D)
    w.q3, w.k3, w.v3, w.o3 = (matrix(f"L3_xattn_w_{k}T", D, D) for k in "qkvo")
    w.bq3, w.bk3 = column("L3_xattn_b_q", D), column("L3_xattn_b_k", D)
    w.bv3, w.bo3 = spread("L3_xattn_b_v", D), row("L3_xattn_b_o", D)
    w.fc1, w.bo1 = matrix("L1_xattn_fc_wT", 2 * D, D), row("L1_xattn_fc_b", D)
    w.ln1, w.ln2 = spread("L1_ffn_w_ln1", D), spread("L1_ffn_w_ln2", D)
    w.kvd, w.qd = matrix("L1_ffn_W_kvd", D, LAT), matrix("L1_ffn_W_qd", D, LAT)
    w.ku, w.qu, w.vu = rows("L1_ffn_W_ku", LAT, H * HH), rows("L1_ffn_W_qu", LAT, H * HH), rows("L1_ffn_W_vu", LAT, D)
    w.ropeq, w.ropek = rows("L1_ffn_W_ropeq", LAT, H * HH), matrix("L1_ffn_W_ropek", D, H * HH)
    w.o1 = matrix("L1_ffn_W_o", D, D)
    w.router = [matrix("L0_ffn_router_w", D, NE), matrix("L1_ffn_W_router", D, NE - 1), matrix("L3_ffn_Wg", D, NE)]
    w.rbias = spread("L1_ffn_routing_bias", NE - 1)
    w.fm = sb("fm_diag", [P, P])
    w.fmb = sb("fm_bias", [P, 1])
    w.fmb_neg = sb("fm_bias_neg", [P, 1])
    w.fmb_row = sb("fm_bias_row", [P, HD])

    with ExitStack() as st:
        sem = Semaphores(nc, st, "p")
        loaded, zeroed, tr_done, tr_copied, prep, x_zero = (sem(n) for n in (
            "loaded", "zeroed", "tr", "trc", "prep", "xzero"))
        tp = st.enter_context(nc.psum_tensor("ctx_tp", [P, KC, B * L], F32))
        ctx_load = st.enter_context(nc.sbuf_tensor("ctx_load", [P, B * L // P, D], F32))
        with nc.Block() as block:
            n_first = 5 + len(loads)

            @block.sync
            def _(sp):
                sp.dma_start(consts[:], ins["consts"]).then_inc(loaded, 16)
                sp.dma_start(x[:], ins["x"].rearrange("b (t p) d -> p (b t) d", p=P)).then_inc(loaded, 16)
                sp.dma_start(ctx_load[:], ins["ctx_1024"].rearrange("b l d -> (b l) d")
                             .rearrange("(k p) d -> p k d", p=P)).then_inc(loaded, 16)
                sp.dma_start(ctx_tok[:], ins["ctx_1024"].rearrange("b l d -> l b d")).then_inc(loaded, 16)
                sp.dma_start(w.fmb_row[:], ins["L1_xattn_fm_b"].partition_broadcast(P)).then_inc(loaded, 16)
                for dst, src in loads:
                    sp.dma_start(dst, src).then_inc(loaded, 16)
                sp.wait_ge(zeroed, 1)
                slots = x_slots.rearrange("(k p) d -> p k d", p=P)
                for k in range(0, SLOTS // P, T):
                    n = min(T, SLOTS // P - k)
                    sp.dma_start(slots[:, k:k + n, :], xn[:, 0:n, :]).then_inc(x_zero, 16)
                sp.wait_ge(x_zero, 16 * (-(-SLOTS // P // T)))

            @block.gpsimd
            def _(pool):
                pool.wait_ge(zeroed, 2)
                for h in range(HC):
                    pool.dma_start(w.fm[h * HD:(h + 1) * HD, h * HD:(h + 1) * HD],
                                   ins["L1_xattn_fm_wT"]).then_inc(diag, 16)
                    pool.dma_start(w.fmb[h * HD:(h + 1) * HD, :],
                                   ins["L1_xattn_fm_b"].rearrange("(p a) -> p a", a=1)).then_inc(diag, 16)
                pool.wait_ge(diag, 32 * HC)

            @block.vector
            def _(dve):
                nc.vector.memset(xn[:], 0.0).then_inc(zeroed, 1)
                nc.vector.memset(w.fm[:], 0.0).then_inc(zeroed, 1)
                dve.wait_ge(loaded, 16 * n_first)
                nc.vector.tensor_copy(ident_h[:], ident).then_inc(prep, 1)
                nc.vector.tensor_copy(causal_h[:], const("causal")).then_inc(prep, 1)
                dve.wait_ge(diag, 32 * HC)
                nc.vector.tensor_scalar(w.fmb_neg[:], w.fmb[:], -1.0, None, ALU.mult).then_inc(prep, 1)
                dve.wait_ge(tr_done, 1)
                nc.vector.tensor_copy(ctxT[:].rearrange("p k b l -> p k (b l)"), tp[:]).then_inc(prep, 1)
                for k in range(KC):
                    nc.vector.tensor_copy(ctxT2[:, k], bcast(tp[:, k, :].rearrange("p (b l) -> p b l", b=B), 2, 2))\
                        .then_inc(prep, 1)

            @block.tensor
            def _(pe):
                pe.wait_ge(loaded, 16 * n_first)
                for t in range(B * L // P):
                    for k in range(KC):
                        last = nc.tensor.transpose(tp[:, k, t * P:(t + 1) * P], ctx_load[:, t, k * P:(k + 1) * P], ident)
                last.then_inc(tr_done, 1)

    def normalise(tag, x, xn, rms_weight=None):
        with ExitStack() as st:
            sem = Semaphores(nc, st, tag)
            tmp = lambda n, s: st.enter_context(nc.sbuf_tensor(f"{tag}_{n}", s, F32))
            stats_done, step, rooted, xn_ready, turned = (sem(n) for n in ("stats", "step", "root", "xn", "turned"))
            copied, kept = ([sem(f"{n}{j}") for j in range(2)] for n in ("copied", "kept"))
            stage = [tmp(f"stage{j}", [P, D]) for j in range(2)]
            st6, mean, var, dif = tmp("st6", [P, T, 6]), tmp("mean", [P, T]), tmp("var", [P, T]), tmp("dif", [P, T])
            m2, root, rstd = tmp("m2", [P, T]), tmp("root", [P, T]), tmp("rstd", [P, T])
            tp = [st.enter_context(nc.psum_tensor(f"{tag}_tp{j}", [P, KC, P], F32)) for j in range(2)]
            with nc.Block() as block:
                @block.vector
                def _(dve):
                    with dve.Fori(0, T) as t:
                        nc.vector.bn_stats(st6[:, t, :], x[:, t, :]).then_inc(stats_done, 1)
                    dve.wait_ge(stats_done, T)
                    nc.vector.tensor_tensor(mean[:], st6[:, :, 1], st6[:, :, 4], ALU.add).then_inc(step, 1)
                    nc.vector.tensor_tensor(dif[:], st6[:, :, 1], st6[:, :, 4], ALU.subtract).then_inc(step, 1)
                    nc.vector.tensor_tensor(m2[:], st6[:, :, 2], st6[:, :, 5], ALU.add).then_inc(step, 1)
                    dve.wait_ge(step, 3)
                    nc.vector.tensor_scalar(mean[:], mean[:], 0.5, None, ALU.mult).then_inc(step, 1)
                    nc.vector.tensor_tensor(dif[:], dif[:], dif[:], ALU.mult).then_inc(step, 1)
                    dve.wait_ge(step, 5)
                    nc.vector.tensor_scalar(dif[:], dif[:], 0.25, None, ALU.mult).then_inc(step, 1)
                    dve.wait_ge(step, 6)
                    nc.vector.scalar_tensor_tensor(var[:], m2[:], 1.0 / D, dif[:], ALU.mult, ALU.add).then_inc(step, 1)
                    dve.wait_ge(step, 7)
                    if rms_weight is None:
                        nc.vector.tensor_scalar(var[:], var[:], LN_EPS, None, ALU.add).then_inc(step, 1)
                    else:
                        nc.vector.tensor_tensor(dif[:], mean[:], mean[:], ALU.mult).then_inc(step, 1)
                        dve.wait_ge(step, 8)
                        nc.vector.tensor_tensor(var[:], var[:], dif[:], ALU.add).then_inc(step, 1)
                    dve.wait_ge(rooted, 1)
                    if rms_weight is not None:
                        nc.vector.tensor_scalar(root[:], root[:], RMS_EPS, None, ALU.add).then_inc(step, 1)
                        dve.wait_ge(step, 10)
                    for j in range(2):
                        dve.sem_inc(copied[j], 1)
                        dve.sem_inc(kept[j], 1)
                    nc.vector.reciprocal(rstd[:], root[:]).then_inc(step, 1)
                    dve.wait_ge(step, 9 if rms_weight is None else 11)
                    with dve.Fori(0, T // 2) as i:
                        for j in range(2):
                            t = i * 2 + j
                            dve.wait_ge(copied[j], i + 1)
                            dve.wait_ge(kept[j], i + 1)
                            if rms_weight is None:
                                nc.vector.tensor_scalar(stage[j][:], x[:, t, :], mean[:, bass.ds(t, 1)],
                                                        rstd[:, bass.ds(t, 1)], ALU.subtract, ALU.mult)\
                                    .then_inc(xn_ready, 1)
                            else:
                                nc.vector.scalar_tensor_tensor(stage[j][:], x[:, t, :], rstd[:, bass.ds(t, 1)],
                                                               rms_weight, ALU.mult, ALU.mult).then_inc(xn_ready, 1)

                @block.gpsimd
                def _(pool):
                    with pool.Fori(0, T // 2) as i:
                        for j in range(2):
                            pool.wait_ge(xn_ready, i * 2 + j + 1)
                            nc.gpsimd.tensor_copy(xn[:, i * 2 + j, :], stage[j][:]).then_inc(kept[j], 1)

                @block.scalar
                def _(act):
                    act.wait_ge(step, 8 if rms_weight is None else 9)
                    nc.scalar.activation(root[:], var[:], ACT.Sqrt).then_inc(rooted, 1)
                    with act.Fori(0, T // 2) as i:
                        for j in range(2):
                            act.wait_ge(turned, i * 2 + j + 1)
                            nc.scalar.copy(xnT[:, :, bass.ts(i * 2 + j, P)], tp[j][:]).then_inc(copied[j], 1)

                @block.tensor
                def _(pe):
                    with pe.Fori(0, T // 2) as i:
                        for j in range(2):
                            pe.wait_ge(xn_ready, i * 2 + j + 1)
                            pe.wait_ge(copied[j], i + 1)
                            for k in range(KC):
                                last = nc.tensor.transpose(tp[j][:, k, :], stage[j][:, k * P:(k + 1) * P], ident)
                            last.then_inc(turned, 1)

    def cross_attention(tag, wq, wk, wv, wo, bq, bk, bv, bo, features=False):
        SG = 2 if features else 1
        VD = HD * SG
        OC = H * VD // P
        PAIRS = H // 2
        with ExitStack() as st:
            sem = Semaphores(nc, st, tag)
            tmp = lambda n, s: st.enter_context(nc.sbuf_tensor(f"{tag}_{n}", s, F32))
            ps = lambda n, s: st.enter_context(nc.psum_tensor(f"{tag}_{n}", s, F32))
            kd = tmp("kd", [P, B, SG, KC, HC, L])
            vd = tmp("vd", [P, B, PAIRS, 2, VD])
            kT = tmp("kT", [P, SG, KC, B, L])
            vt = tmp("vt", [P, B, H, VD])
            vz = tmp("vz", [P, B, D])
            qT = tmp("qT", [P, SG, KC, 2 * P])
            pr = [tmp(f"pr{j}", [P, H, L]) for j in range(2)]
            pT = [tmp(f"pT{j}", [P, PAIRS, P]) for j in range(2)]
            ho = [tmp(f"ho{j}", [P, H, VD]) for j in range(2)]
            hoT = [tmp(f"hoT{j}", [P, OC, P]) for j in range(2)]
            mx = [tmp(f"mx{j}", [P, H]) for j in range(2)]
            sm = [tmp(f"sm{j}", [P, H]) for j in range(2)]
            rs = [tmp(f"rs{j}", [P, H]) for j in range(2)]
            sc = [ps(f"sc{j}", [P, KC, HC * L]) for j in range(2)]
            ob = [ps(f"ob{j}", [P, H * VD]) for j in range(2)]
            qb = ps("qb", [P, KC, 2 * P])

            k_made, k_done, k_spread, v_made, v_done, v_exp, v_spread = (sem(n) for n in (
                "kmade", "kdone", "kspread", "vmade", "vdone", "vexp", "vspread"))
            with nc.Block() as block:
                @block.tensor
                def _(pe):
                    for c in range(KC):
                        if features:
                            last = nc.tensor.matmul(qb[:, c, :], w.fm[:], ctxT[:, c].rearrange("p b l -> p (b l)"),
                                                    start=True, stop=True)
                        else:
                            for k in range(KC):
                                last = nc.tensor.matmul(qb[:, c, :], wk[:, k, c * P:(c + 1) * P],
                                                        ctxT[:, k].rearrange("p b l -> p (b l)"),
                                                        start=(k == 0), stop=(k == KC - 1))
                    last.then_inc(k_made, 1)
                    for b in range(B):
                        for k in range(KC):
                            lhs = ctxT2[:, k, b].rearrange("p a l -> p (a l)")
                            dst = sc[b // 2][:, b % 2, 0:D]
                            if features:
                                last = nc.tensor.matmul(dst[:, k * P:(k + 1) * P], lhs, w.fm[:], start=True, stop=True)
                            else:
                                last = nc.tensor.matmul(dst, lhs, wv[:, k, :], start=(k == 0), stop=(k == KC - 1))
                        last.then_inc(v_made, 1)

                @block.scalar
                def _(act):
                    if features:
                        act.wait_ge(k_made, 1)
                        for s in range(SG):
                            nc.scalar.activation(kT[:, s].rearrange("p c b l -> p c (b l)"), qb[:], ACT.Exp,
                                                 bias=(w.fmb, w.fmb_neg)[s][:, 0:1], scale=(1.0, -1.0)[s])\
                                .then_inc(k_done, 1)
                        for b in range(B):
                            act.wait_ge(v_done, b + 1)
                            for s in range(SG):
                                nc.scalar.activation(vt[:, b, :, s * HD:(s + 1) * HD],
                                                     vz[:, b, :].rearrange("p (h d) -> p h d", d=HD), ACT.Exp,
                                                     scale=(1.0, -1.0)[s]).then_inc(v_exp, 1)

                @block.vector
                def _(dve):
                    if not features:
                        dve.wait_ge(k_made, 1)
                        for c in range(KC):
                            nc.vector.tensor_scalar(kT[:, 0, c].rearrange("p b l -> p (b l)"), qb[:, c, :],
                                                    bk[:, c:c + 1], SCALE, ALU.add, ALU.mult).then_inc(k_done, 1)
                    for b in range(B):
                        dve.wait_ge(v_made, b + 1)
                        src = sc[b // 2][:, b % 2, 0:D]
                        if features:
                            nc.vector.tensor_tensor(vz[:, b, :].rearrange("p (h d) -> p h d", d=HD),
                                                    src.rearrange("p (h d) -> p h d", d=HD),
                                                    bcast(w.fmb_row[:], 1, H), ALU.add).then_inc(v_done, 1)
                        else:
                            nc.vector.tensor_tensor(vt[:, b].rearrange("p h d -> p (h d)"), src, bv[:],
                                                    ALU.add).then_inc(v_done, 1)
                    dve.wait_ge(k_done, KC)
                    for b in range(B):
                        for s in range(SG):
                            for c in range(KC):
                                key = bcast(kT[:, s, c, b, :], 1, HC)
                                mask = bcast(const("head8"), 2, L)
                                nc.vector.tensor_tensor(kd[:, b, s, c], key, mask, ALU.mult).then_inc(k_spread, 1)
                    if features:
                        dve.wait_ge(k_spread, B * SG * KC)
                        nc.vector.tensor_scalar(kd[:].rearrange("p b s c h l -> p (b s c h l)"),
                                                kd[:].rearrange("p b s c h l -> p (b s c h l)"), D ** -0.5, None,
                                                ALU.mult).then_inc(k_spread, 1)
                        dve.wait_ge(v_exp, SG * B)
                    else:
                        dve.wait_ge(v_done, B)
                    for b in range(B):
                        nc.vector.tensor_tensor(vd[:, b], vt[:, b].rearrange("p (r a) d -> p r a d", a=2),
                                                bcast(bcast(const("parity"), 1, PAIRS), 3, VD), ALU.mult)\
                            .then_inc(v_spread, 1)

            q_made, q_done, sc_made, max_done, less_done, exp_done, sum_done, rec_done, pt_made, pt_half, o_made, \
                o_done, ot_made, ot_done, y_made = (sem(n) for n in (
                    "q", "qd", "sc", "max", "less", "exp", "sum", "rec", "pt", "ptd", "o", "od", "ot", "otd", "y"))
            added = [sem(f"added{j}") for j in range(2)]
            with nc.Block() as block:
                @block.tensor
                def _(pe):
                    for j in range(2):
                        pe.sem_inc(added[j], 1)
                    with pe.Fori(0, B) as b:
                        with pe.Fori(0, TB // 2) as p2:
                            i = b * (TB // 2) + p2
                            for c in range(KC):
                                if features:
                                    last = nc.tensor.matmul(qb[:, c, :], w.fm[:], xnT[:, c, bass.ts(i, 2 * P)],
                                                            start=True, stop=True)
                                else:
                                    for k in range(KC):
                                        last = nc.tensor.matmul(qb[:, c, :], wq[:, k, c * P:(c + 1) * P],
                                                                xnT[:, k, bass.ts(i, 2 * P)],
                                                                start=(k == 0), stop=(k == KC - 1))
                            last.then_inc(q_made, 1)
                            for j in range(2):
                                pe.wait_ge(q_done, (i + 1) * SG * KC)
                                pe.wait_ge(added[j], i + 1)
                                for c in range(KC):
                                    for s in range(SG):
                                        last = nc.tensor.matmul(sc[j][:, c, :], qT[:, s, c, j * P:(j + 1) * P],
                                                                kd[:, b, s, c].rearrange("p h l -> p (h l)"),
                                                                start=(s == 0), stop=(s == SG - 1))
                                last.then_inc(sc_made, 1)
                            for j in range(2):
                                pe.wait_ge(exp_done, i * 2 + j + 1)
                                for r in range(PAIRS):
                                    last = nc.tensor.transpose(sc[j][:, r // 4, (r % 4) * P:(r % 4 + 1) * P],
                                                               pr[j][:, 2 * r:2 * r + 2, :].rearrange("p h l -> p (h l)"),
                                                               ident)
                                    if r % 4 == 3:
                                        last.then_inc(pt_made, 1)
                            for j in range(2):
                                pe.wait_ge(pt_half, (i * 2 + j + 1) * 2)
                                for r in range(PAIRS):
                                    last = nc.tensor.matmul(ob[j][:, r * 2 * VD:(r + 1) * 2 * VD], pT[j][:, r, :],
                                                            vd[:, b, r].rearrange("p a d -> p (a d)"),
                                                            start=True, stop=True)
                                last.then_inc(o_made, 1)
                            for j in range(2):
                                pe.wait_ge(o_done, i * 2 + j + 1)
                                for c in range(OC):
                                    last = nc.tensor.transpose(ob[j][:, c * P:(c + 1) * P],
                                                               ho[j][:].rearrange("p h d -> p (h d)")[:, c * P:(c + 1) * P],
                                                               ident)
                                last.then_inc(ot_made, 1)
                            for j in range(2):
                                pe.wait_ge(ot_done, i * 2 + j + 1)
                                for c in range(OC):
                                    nc.tensor.matmul(sc[j][:, 0, 0:D], hoT[j][:, c, :], wo[:, c, :],
                                                     start=(c == 0), stop=False)
                                nc.tensor.matmul(sc[j][:, 0, 0:D], ones[0:1, :], bo[0:1, :], start=False,
                                                 stop=True).then_inc(y_made, 1)

                @block.scalar
                def _(act):
                    with act.Fori(0, T // 2) as i:
                        act.wait_ge(q_made, i + 1)
                        for c in range(KC):
                            for s in range(SG):
                                nc.scalar.activation(qT[:, s, c, :], qb[:, c, :], ACT.Exp if features else ACT.Identity,
                                                     bias=(w.fmb, w.fmb_neg)[s][:, 0:1] if features else bq[:, c:c + 1],
                                                     scale=(1.0, -1.0)[s]).then_inc(q_done, 1)
                        for j in range(2):
                            act.wait_ge(less_done, i * 2 + j + 1)
                            nc.scalar.activation(pr[j][:], pr[j][:], ACT.Exp).then_inc(exp_done, 1)
                        for j in range(2):
                            act.wait_ge(pt_made, (i * 2 + j) * 2 + 1)
                            nc.scalar.copy(pT[j][:, 0:4, :].rearrange("p r q -> p (r q)"), sc[j][:, 0, :])\
                                .then_inc(pt_half, 1)
                            act.wait_ge(pt_made, (i * 2 + j) * 2 + 2)
                            nc.scalar.copy(pT[j][:, 4:8, :].rearrange("p r q -> p (r q)"), sc[j][:, 1, :])\
                                .then_inc(pt_half, 1)
                        for j in range(2):
                            act.wait_ge(ot_made, i * 2 + j + 1)
                            nc.scalar.copy(hoT[j][:].rearrange("p c q -> p (c q)"), ob[j][:]).then_inc(ot_done, 1)

                @block.vector
                def _(dve):
                    with dve.Fori(0, T // 2) as i:
                        for j in range(2):
                            s3 = sc[j][:].rearrange("p c (h l) -> p (c h) l", l=L)
                            dve.wait_ge(sc_made, i * 2 + j + 1)
                            nc.vector.tensor_reduce(mx[j][:], s3, AX_X, ALU.max).then_inc(max_done, 1)
                            dve.wait_ge(max_done, i * 2 + j + 1)
                            nc.vector.tensor_tensor(pr[j][:], s3, bcast(mx[j][:], 2, L), ALU.subtract)\
                                .then_inc(less_done, 1)
                        for j in range(2):
                            dve.wait_ge(exp_done, i * 2 + j + 1)
                            nc.vector.tensor_reduce(sm[j][:], pr[j][:], AX_X, ALU.add).then_inc(sum_done, 1)
                            dve.wait_ge(sum_done, i * 2 + j + 1)
                            nc.vector.reciprocal(rs[j][:], sm[j][:]).then_inc(rec_done, 1)
                        for j in range(2):
                            dve.wait_ge(rec_done, i * 2 + j + 1)
                            dve.wait_ge(o_made, i * 2 + j + 1)
                            nc.vector.tensor_tensor(ho[j][:], ob[j][:].rearrange("p (h d) -> p h d", d=VD),
                                                    bcast(rs[j][:], 2, VD), ALU.mult).then_inc(o_done, 1)
                        for j in range(2):
                            dve.wait_ge(y_made, i * 2 + j + 1)
                            nc.vector.tensor_tensor(x[:, i * 2 + j, :], sc[j][:, 0, 0:D], x[:, i * 2 + j, :],
                                                    ALU.add).then_inc(added[j], 1)

    def latent_attention(tag, x):
        with ExitStack() as st:
            sem = Semaphores(nc, st, tag)
            tmp = lambda n, s: st.enter_context(nc.sbuf_tensor(f"{tag}_{n}", s, F32))
            ps = lambda n, s: st.enter_context(nc.psum_tensor(f"{tag}_{n}", s, F32))
            qa, qr, ka = (tmp(n, [LAT, KC, HC, HD]) for n in ("qa", "qr", "ka"))
            kx, kr = (tmp(n, [P, KC, KC, HC, HD]) for n in ("kx", "kr"))
            qT, kT = tmp("qT", [P, B, KC, S]), tmp("kT", [P, B, KC, S])
            va = tmp("va", [P, T, H, HD + 1])
            laid = sem("laid")
            with nc.Block() as block:
                @block.gpsimd
                def _(pool):
                    for t in (qa, qr, ka, kx, kr):
                        nc.gpsimd.memset(t[:], 0.0).then_inc(laid, 1)
                    nc.gpsimd.memset(va[:], 1.0).then_inc(laid, 1)

                @block.vector
                def _(dve):
                    heads = lambda m: m.rearrange("p (c h d) -> p c h d", c=KC, d=HH)
                    dve.wait_ge(laid, 6)
                    nc.vector.tensor_copy(qa[:, :, :, 0:HH], heads(w.qu[:]))
                    nc.vector.tensor_copy(qa[:, :, :, HH:HD], heads(w.ropeq[:]))
                    nc.vector.tensor_copy(ka[:, :, :, 0:HH], heads(w.ku[:]))
                    q = HH // 2
                    nc.vector.tensor_scalar(qr[:, :, :, HH:HH + q], heads(w.ropeq[:])[:, :, :, q:HH], -1.0, None, ALU.mult)
                    nc.vector.tensor_copy(qr[:, :, :, HH + q:HD], heads(w.ropeq[:])[:, :, :, 0:q])
                    for k in range(KC):
                        rk = heads(w.ropek[:, k, :])
                        nc.vector.tensor_copy(kx[:, k, :, :, HH:HD], rk)
                        nc.vector.tensor_scalar(kr[:, k, :, :, HH:HH + q], rk[:, :, :, q:HH], -1.0, None, ALU.mult)
                        nc.vector.tensor_copy(kr[:, k, :, :, HH + q:HD], rk[:, :, :, 0:q])

            with ExitStack() as s2:
                sem2 = Semaphores(nc, s2, f"{tag}p")
                ps2 = lambda n, s: s2.enter_context(nc.psum_tensor(f"{tag}p_{n}", s, F32))
                tmp2 = lambda n, s: s2.enter_context(nc.sbuf_tensor(f"{tag}p_{n}", s, F32))
                lat = [tmp2(f"lat{n}", [LAT, S]) for n in range(2)]
                t1 = [tmp2(f"t1{n}", [P, S]) for n in range(2)]
                t2 = [tmp2(f"t2{n}", [P, S]) for n in range(2)]
                lp = [ps2(f"lp{n}", [LAT, S]) for n in range(2)]
                pa, pr_ = [ps2(f"pa{n}", [P, S]) for n in range(2)], [ps2(f"pr{n}", [P, S]) for n in range(2)]
                vp = ps2("vp", [P, TB, D])
                lat_made, lat_done, ka_made, kr_made, qa_made, qr_made, cos_k, sin_k, cos_q, sin_q, k_done, q_done, \
                    v_made, v_done = (sem2(n) for n in ("lat", "latd", "ka", "kr", "qa", "qr", "ck", "sk", "cq", "sq",
                                                        "k", "q", "v", "vd"))
                with nc.Block() as block:
                    @block.tensor
                    def _(pe):
                        for bank_read in (cos_k, sin_k, cos_q, sin_q, v_done):
                            pe.sem_inc(bank_read, 1)
                        with pe.Fori(0, B) as b:
                            tokens = lambda k: xnT[:, k, bass.ts(b, S)]
                            for n, wd in ((0, w.kvd), (1, w.qd)):
                                for k in range(KC):
                                    last = nc.tensor.matmul(lp[n][:], wd[:, k, :], tokens(k), start=(k == 0),
                                                            stop=(k == KC - 1))
                                last.then_inc(lat_made, 1)
                            pe.wait_ge(lat_done, b * 2 + 2)
                            for c in range(KC):
                                flat = lambda m: m.rearrange("p h d -> p (h d)")
                                pe.wait_ge(cos_k, b * KC + c + 1)
                                nc.tensor.matmul(pa[0][:], flat(ka[:, c]), lat[0][:], start=True, stop=False)
                                for k in range(KC):
                                    last = nc.tensor.matmul(pa[0][:], flat(kx[:, k, c]), tokens(k), start=False,
                                                            stop=(k == KC - 1))
                                last.then_inc(ka_made, 1)
                                pe.wait_ge(sin_k, b * KC + c + 1)
                                for k in range(KC):
                                    last = nc.tensor.matmul(pr_[0][:], flat(kr[:, k, c]), tokens(k), start=(k == 0),
                                                            stop=(k == KC - 1))
                                last.then_inc(kr_made, 1)
                                pe.wait_ge(cos_q, b * KC + c + 1)
                                nc.tensor.matmul(pa[1][:], flat(qa[:, c]), lat[1][:], start=True, stop=True)\
                                    .then_inc(qa_made, 1)
                                pe.wait_ge(sin_q, b * KC + c + 1)
                                nc.tensor.matmul(pr_[1][:], flat(qr[:, c]), lat[1][:], start=True, stop=True)\
                                    .then_inc(qr_made, 1)
                            pe.wait_ge(v_done, b + 1)
                            for t in range(TB):
                                last = nc.tensor.matmul(vp[:, t, :], lat[0][:, t * P:(t + 1) * P], w.vu[:],
                                                        start=True, stop=True)
                            last.then_inc(v_made, 1)

                    @block.scalar
                    def _(act):
                        with act.Fori(0, B) as b:
                            for n in range(2):
                                act.wait_ge(lat_made, b * 2 + n + 1)
                                nc.scalar.copy(lat[n][:], lp[n][:]).then_inc(lat_done, 1)
                            act.wait_ge(v_made, b + 1)
                            nc.scalar.copy(va[:, bass.ts(b, TB), :, 0:HD].rearrange("p t h d -> p (t h) d"),
                                           vp[:].rearrange("p t (h d) -> p (t h) d", d=HD)).then_inc(v_done, 1)

                    @block.vector
                    def _(dve):
                        for summed in (k_done, q_done):
                            dve.sem_inc(summed, 1)
                        with dve.Fori(0, B * KC) as o:
                            dve.wait_ge(ka_made, o + 1)
                            dve.wait_ge(k_done, o + 1)
                            nc.vector.tensor_tensor(t1[0][:], pa[0][:], const("cos"), ALU.mult).then_inc(cos_k, 1)
                            dve.wait_ge(kr_made, o + 1)
                            nc.vector.tensor_tensor(t2[0][:], pr_[0][:], const("sin"), ALU.mult).then_inc(sin_k, 1)
                            dve.wait_ge(qa_made, o + 1)
                            dve.wait_ge(q_done, o + 1)
                            nc.vector.tensor_tensor(t1[1][:], pa[1][:], const("cos"), ALU.mult).then_inc(cos_q, 1)
                            dve.wait_ge(qr_made, o + 1)
                            nc.vector.tensor_tensor(t2[1][:], pr_[1][:], const("sin"), ALU.mult).then_inc(sin_q, 1)

                    @block.gpsimd
                    def _(pool):
                        with pool.Fori(0, B * KC) as o:
                            pool.wait_ge(sin_k, o + 2)
                            nc.gpsimd.tensor_tensor(kT[:].rearrange("p b c s -> p (b c) s")[:, o, :], t1[0][:], t2[0][:],
                                                    ALU.add).then_inc(k_done, 1)
                            pool.wait_ge(sin_q, o + 2)
                            nc.gpsimd.tensor_tensor(qT[:].rearrange("p b c s -> p (b c) s")[:, o, :], t1[1][:], t2[1][:],
                                                    ALU.add).then_inc(q_done, 1)

            y = xn
            with ExitStack() as s2:
                sem2 = Semaphores(nc, s2, f"{tag}a")
                ps2 = lambda n, s: s2.enter_context(nc.psum_tensor(f"{tag}a_{n}", s, F32))
                tmp2 = lambda n, s: s2.enter_context(nc.sbuf_tensor(f"{tag}a_{n}", s, F32))
                qm = tmp2("qm", [P, S])
                pr = tmp2("pr", [P, TB, S])
                nm, rc = tmp2("nm", [P, TB]), tmp2("rc", [P, TB])
                pT = tmp2("pT", [P, 12, P])
                sc = [ps2(f"sc{q}", [P, S]) for q in range(TB)]
                tp = [ps2(f"tp{n}", [P, TB, P]) for n in range(3)]
                ob = ps2("ob", [P, TB, HD + 1])
                GROUPS = [[(3, k) for k in range(4)], [(2, k) for k in range(3)], [(1, 0), (1, 1), (0, 0)]]
                place = {qk: (n, m) for n, g in enumerate(GROUPS) for m, qk in enumerate(g)}
                q_masked, sc_made, max_done, exp_done, t_made, t_copied, o_made, rec_done, y_done = (sem2(n) for n in (
                    "qm", "sc", "max", "exp", "t", "tc", "o", "rec", "y"))
                hs = const("head8")
                with nc.Block() as block:
                    @block.vector
                    def _(dve):
                        with dve.Fori(0, B) as b:
                            with dve.Fori(0, KC) as c:
                                with dve.Fori(0, HC) as hh:
                                    n = b * H + c * HC + hh
                                    nc.vector.tensor_scalar(qm[:], qT[:].rearrange("p b c s -> p (b c) s")[:, b * KC + c, :],
                                                            hs[:, bass.ds(hh, 1)], SCALE, ALU.mult, ALU.mult).then_inc(q_masked, 1)
                                    for m, q in enumerate(reversed(range(TB))):
                                        dve.wait_ge(sc_made, n * TB + m + 1)
                                        nc.vector.tensor_reduce(nm[:, q:q + 1], sc[q][:, 0:(q + 1) * P], AX_X, ALU.max,
                                                                negate=True).then_inc(max_done, 1)
                                    dve.wait_ge(t_made, n * 3 + 2)
                                    nc.vector.tensor_copy(pT[:, 4:7, :], tp[1][:, 0:3, :]).then_inc(t_copied, 1)
                                    dve.wait_ge(o_made, n + 1)
                                    nc.vector.reciprocal(rc[:], ob[:, :, HD]).then_inc(rec_done, 1)
                                    dve.wait_ge(rec_done, n + 1)
                                    nc.vector.tensor_tensor(
                                        y[:, bass.ts(b, TB), :].rearrange("p t (h d) -> p t h d", d=HD)[:, :, c * HC + hh, :],
                                        ob[:, :, 0:HD], bcast(rc[:], 2, HD), ALU.mult).then_inc(y_done, 1)

                    @block.scalar
                    def _(act):
                        with act.Fori(0, B * H) as n:
                            for m, q in enumerate(reversed(range(TB))):
                                act.wait_ge(max_done, n * TB + m + 1)
                                nc.scalar.activation(pr[:, q, 0:(q + 1) * P], sc[q][:, 0:(q + 1) * P], ACT.Exp,
                                                     bias=nm[:, q:q + 1]).then_inc(exp_done, 1)
                            for g in (0, 2):
                                act.wait_ge(t_made, n * 3 + g + 1)
                                k = len(GROUPS[g])
                                nc.scalar.copy(pT[:, 4 * g:4 * g + k, :] if g < 2 else pT[:, 7:10, :], tp[g][:, 0:k, :])\
                                    .then_inc(t_copied, 1)

                    @block.tensor
                    def _(pe):
                        pe.sem_inc(y_done, 1)
                        with pe.Fori(0, B) as b:
                            with pe.Fori(0, KC) as c:
                                with pe.Fori(0, HC) as hh:
                                    n = b * H + c * HC + hh
                                    pe.wait_ge(q_masked, n + 1)
                                    for q in reversed(range(TB)):
                                        nc.tensor.matmul(sc[q][:, 0:(q + 1) * P], qm[:, q * P:(q + 1) * P],
                                                         kT[:].rearrange("p b c s -> p (b c) s")[:, b * KC + c, 0:(q + 1) * P],
                                                         start=True, stop=False)
                                        nc.tensor.matmul(sc[q][:, q * P:(q + 1) * P], ident_h[:], causal_h[:], start=False,
                                                         stop=True).then_inc(sc_made, 1)
                                    for g, blocks in enumerate(GROUPS):
                                        pe.wait_ge(exp_done, n * TB + (1, 2, 4)[g])
                                        for q, k in blocks:
                                            last = nc.tensor.transpose(tp[g][:, place[q, k][1], :],
                                                                       pr[:, q, k * P:(k + 1) * P], ident)
                                        last.then_inc(t_made, 1)
                                    pe.wait_ge(t_copied, n * 3 + 3)
                                    pe.wait_ge(y_done, n + 1)
                                    for q in range(TB):
                                        for k in range(q + 1):
                                            g, m = place[q, k]
                                            last = nc.tensor.matmul(ob[:, q, :], pT[:, (0, 4, 7)[g] + m, :],
                                                                    va[:, b * TB + k, c * HC + hh, :],
                                                                    start=(k == 0), stop=(k == q))
                                    last.then_inc(o_made, 1)

            project_tokens(f"{tag}o", y, w.o1, x)

    def project_tokens(tag, y, wo, x):
        with ExitStack() as st:
            sem = Semaphores(nc, st, tag)
            yT = [st.enter_context(nc.sbuf_tensor(f"{tag}_yT{j}", [P, KC, P], F32)) for j in range(2)]
            tp = [st.enter_context(nc.psum_tensor(f"{tag}_tp{j}", [P, KC, P], F32)) for j in range(2)]
            op = [st.enter_context(nc.psum_tensor(f"{tag}_op{j}", [P, D], F32)) for j in range(2)]
            staged, turned, copied, made = sem("staged"), sem("turned"), sem("copied"), sem("made")
            ys = [st.enter_context(nc.sbuf_tensor(f"{tag}_ys{j}", [P, D], F32)) for j in range(2)]
            added = [sem(f"added{j}") for j in range(2)]
            with nc.Block() as block:
                @block.tensor
                def _(pe):
                    with pe.Fori(0, T // 2) as i:
                        for j in range(2):
                            pe.wait_ge(staged, i * 2 + j + 1)
                            for k in range(KC):
                                last = nc.tensor.transpose(tp[j][:, k, :], ys[j][:, k * P:(k + 1) * P], ident)
                            last.then_inc(turned, 1)
                        for j in range(2):
                            pe.wait_ge(copied, i * 2 + j + 1)
                            for k in range(KC):
                                last = nc.tensor.matmul(op[j][:], yT[j][:, k, :], wo[:, k, :], start=(k == 0),
                                                        stop=(k == KC - 1))
                            last.then_inc(made, 1)

                @block.gpsimd
                def _(pool):
                    for j in range(2):
                        pool.sem_inc(added[j], 1)
                    with pool.Fori(0, T // 2) as i:
                        for j in range(2):
                            pool.wait_ge(added[j], i + 1)
                            nc.gpsimd.tensor_copy(ys[j][:], y[:, i * 2 + j, :]).then_inc(staged, 1)

                @block.scalar
                def _(act):
                    with act.Fori(0, T // 2) as i:
                        for j in range(2):
                            act.wait_ge(turned, i * 2 + j + 1)
                            nc.scalar.copy(yT[j][:], tp[j][:]).then_inc(copied, 1)

                @block.vector
                def _(dve):
                    with dve.Fori(0, T // 2) as i:
                        for j in range(2):
                            dve.wait_ge(made, i * 2 + j + 1)
                            nc.vector.tensor_tensor(x[:, i * 2 + j, :], op[j][:], x[:, i * 2 + j, :], ALU.add)\
                                .then_inc(added[j], 1)

    def experts(tag, layer, x, wr, w_gate, w_up, w_down, F, shared=False, bias=None, outer=None):
        E = NE - 1 if shared else NE
        NB = ROUTED + (SHARED if shared else 0)
        FC = -(-F // P)
        FW = [min(P, F - f * P) for f in range(FC)]
        HALVES = -(-F // 512)
        FH = F // HALVES
        assert NB % 2 == 1
        with ExitStack() as st:
            tmp = lambda n, s, dt=F32: st.enter_context(nc.sbuf_tensor(f"{tag}_{n}", s, dt))
            wt = [tmp(f"wt{k}", [P, T]) for k in range(TOP)]
            slot = [tmp(f"slot{k}", [P, T], U32) for k in range(TOP)]
            owner = tmp("owner", [P, ROUTED + SHARED], I32)
            route(tag, wr, E, NB, wt, slot, owner, bias)

            with ExitStack() as s2:
                sem = Semaphores(nc, s2, tag)
                shared_put = sem("shared_put")
                with nc.Block() as block:
                    @block.gpsimd
                    def _(pool):
                        for t in range(T):
                            for k in range(TOP):
                                pool.indirect_dma_start(x_slots[0:ROUTED * P, :], bass.IndirectOffsetOnAxis(ap=slot[k][:, t:t + 1], axis=0),
                                                        xn[:, t, :], None).then_inc(rows_put, 16)
                        pool.wait_ge(rows_put, 16 * TOP * T * (layer + 1))

                    @block.sync
                    def _(sp):
                        if shared:
                            sp.dma_start(x_slots[ROUTED * P:SLOTS, :].rearrange("(t p) d -> p t d", p=P), xn[:])\
                                .then_inc(shared_put, 16)
                            sp.wait_ge(shared_put, 16)

            blocks(tag, w_gate, w_up, w_down, F, NB, E if not shared else NE, owner)

            with ExitStack() as s2:
                sem = Semaphores(nc, s2, tag)
                got = s2.enter_context(nc.sbuf_tensor(f"{tag}_got", [P, RING, D], F32))
                shr = s2.enter_context(nc.sbuf_tensor(f"{tag}_shr", [P, T, D], F32)) if shared else None
                used, shr_got = sem("used"), sem("shr")
                with nc.Block() as block:
                    @block.gpsimd
                    def _(pool):
                        for n in range(T * TOP):
                            if n >= RING:
                                pool.wait_ge(used, n - RING + 1)
                            pool.indirect_dma_start(got[:, n % RING, :], None, y_slots[0:ROUTED * P, :], bass.IndirectOffsetOnAxis(
                                ap=slot[n % TOP][:, n // TOP:n // TOP + 1], axis=0)).then_inc(rows_got[n % RING], 16)

                    @block.sync
                    def _(sp):
                        if shared:
                            sp.dma_start(shr[:], y_slots[ROUTED * P:SLOTS, :].rearrange("(t p) d -> p t d", p=P))\
                                .then_inc(shr_got, 16)

                    @block.vector
                    def _(dve):
                        for n in range(T * TOP):
                            t, k = n // TOP, n % TOP
                            dve.wait_ge(rows_got[n % RING], 16 * (layer * T * TOP // RING + n // RING + 1))
                            if n:
                                dve.wait_ge(used, n)
                            nc.vector.scalar_tensor_tensor(x[:, t, :], got[:, n % RING, :], wt[k][:, t:t + 1], x[:, t, :],
                                                           ALU.mult, ALU.add).then_inc(used, 1)
                        if shared:
                            dve.wait_ge(used, T * TOP)
                            dve.wait_ge(shr_got, 16)
                            nc.vector.tensor_tensor(x[:], shr[:], x[:], ALU.add).then_inc(used, 1)

                        if outer is not None:
                            dve.wait_ge(used, T * TOP + (1 if shared else 0))
                            nc.vector.tensor_tensor(outer[:], outer[:], x[:], ALU.add)

    def route(tag, wr, E, NB, wt, slot, owner, bias):
        with ExitStack() as st:
            sem = Semaphores(nc, st, f"{tag}r")
            tmp = lambda n, s, dt=F32: st.enter_context(nc.sbuf_tensor(f"{tag}r_{n}", s, dt))
            ps = lambda n, s: st.enter_context(nc.psum_tensor(f"{tag}r_{n}", s, F32))
            lg, lb = tmp("lg", [P, T, NE]), tmp("lb", [P, T, NE])
            m8, i8, i8f = tmp("m8", [P, T, 8]), tmp("i8", [P, T, 8], U32), tmp("i8f", [P, T, 8])
            oh = [tmp(f"oh{k}", [P, T, NE]) for k in range(TOP)]
            both, base, pick = tmp("both", [P, T, NE]), tmp("base", [P, T, NE]), [tmp(f"pick{k}", [P, T, NE]) for k in range(TOP)]
            sf = [tmp(f"sf{k}", [P, T]) for k in range(TOP)]
            cnt, over, nb, part, first = tmp("cnt", [P, NE]), tmp("over", [P, NE, T]), tmp("nb", [P, NE]), \
                tmp("part", [P, NE, NE]), tmp("first", [P, NE])
            past, own = tmp("past", [P, ROUTED + SHARED, NE - 1]), tmp("own", [P, ROUTED + SHARED])
            diff, tot = tmp("diff", [P, T]), tmp("tot", [P, T])
            lp, rank, count = ps("lp", [P, T, NE]), ps("rank", [P, T, NE]), ps("count", [P, NE])
            lg_made, lg_done, prob_done, max_done, idx_done, step, ranked, counted, weighed = (sem(n) for n in (
                "lg", "lgd", "prob", "max", "idx", "step", "rank", "count", "wt"))
            with nc.Block() as block:
                @block.tensor
                def _(pe):
                    for t in range(T):
                        for k in range(KC):
                            last = nc.tensor.matmul(lp[:, t, 0:E], xnT[:, k, t * P:(t + 1) * P], wr[:, k, :],
                                                    start=(k == 0), stop=(k == KC - 1))
                    last.then_inc(lg_made, 1)
                    pe.wait_ge(step, 4)
                    nc.tensor.matmul(rank[:], const("before"), both[:], start=True, stop=False)
                    for t in range(T - 1):
                        last = nc.tensor.matmul(rank[:, t + 1:T, :], ones, bcast(both[:, t, :], 1, T - 1 - t), start=False,
                                                stop=(t == T - 2))
                    last.then_inc(ranked, 1)
                    for t in range(T):
                        last = nc.tensor.matmul(count[:], ones, both[:, t, :], start=(t == 0), stop=(t == T - 1))
                    last.then_inc(counted, 1)

                @block.scalar
                def _(act):
                    if bias is not None:
                        act.wait_ge(lg_done, 2)
                        nc.scalar.activation(lg[:, :, 0:E], lb[:, :, 0:E], ACT.Sigmoid).then_inc(prob_done, 1)
                    else:
                        act.wait_ge(weighed, 1)
                        for k in range(TOP):
                            nc.scalar.activation(wt[k][:], diff[:], ACT.Sigmoid, scale=(1.0, -1.0)[k]).then_inc(weighed, 1)

                @block.vector
                def _(dve):
                    if E < NE:
                        nc.vector.memset(lg[:], NEG).then_inc(lg_done, 1)
                    dve.wait_ge(lg_made, 1)
                    if bias is not None:
                        nc.vector.tensor_tensor(lb[:, :, 0:E], lp[:, :, 0:E], bcast(bias[:], 1, T), ALU.add).then_inc(lg_done, 1)
                        dve.wait_ge(prob_done, 1)
                    else:
                        nc.vector.tensor_copy(lg[:], lp[:]).then_inc(lg_done, 1)
                        dve.wait_ge(lg_done, 1)
                    for t in range(T):
                        nc.vector.max(m8[:, t, :], lg[:, t, :]).then_inc(max_done, 1)
                    for t in range(T):
                        dve.wait_ge(max_done, t + 1)
                        nc.vector.max_index(i8[:, t, :], m8[:, t, :], lg[:, t, :]).then_inc(idx_done, 1)
                    dve.wait_ge(idx_done, T)
                    nc.vector.tensor_copy(i8f[:], i8[:]).then_inc(step, 1)
                    dve.wait_ge(step, 1)
                    for k in range(TOP):
                        nc.vector.tensor_tensor(oh[k][:], bcast(i8f[:, :, k], 2, NE), bcast(const("iota8"), 1, T),
                                                ALU.is_equal).then_inc(step, 1)
                    dve.wait_ge(step, 3)
                    nc.vector.tensor_tensor(both[:], oh[0][:], oh[1][:], ALU.add).then_inc(step, 1)
                    if bias is None:
                        nc.vector.tensor_tensor(diff[:], m8[:, :, 0], m8[:, :, 1], ALU.subtract).then_inc(weighed, 1)
                    else:
                        nc.vector.tensor_tensor(diff[:], m8[:, :, 0], m8[:, :, 1], ALU.add).then_inc(weighed, 1)
                        dve.wait_ge(weighed, 1)
                        nc.vector.reciprocal(tot[:], diff[:]).then_inc(weighed, 1)
                        dve.wait_ge(weighed, 2)
                        for k in range(TOP):
                            nc.vector.tensor_tensor(wt[k][:], m8[:, :, k], tot[:], ALU.mult)
                    dve.wait_ge(counted, 1)
                    nc.vector.tensor_copy(cnt[:], count[:]).then_inc(step, 1)
                    dve.wait_ge(step, 5)
                    nc.vector.tensor_tensor(over[:], bcast(cnt[:], 2, T), bcast(const("full"), 1, NE), ALU.is_gt).then_inc(step, 1)
                    dve.wait_ge(step, 6)
                    nc.vector.tensor_reduce(nb[:], over[:], AX_X, ALU.add).then_inc(step, 1)
                    dve.wait_ge(step, 7)
                    nc.vector.tensor_tensor(part[:], bcast(nb[:], 1, NE), const("tri8").rearrange("p (e f) -> p e f", e=NE),
                                            ALU.mult).then_inc(step, 1)
                    dve.wait_ge(step, 8)
                    nc.vector.tensor_reduce(first[:], part[:], AX_X, ALU.add).then_inc(step, 1)
                    dve.wait_ge(step, 9)
                    nc.vector.tensor_tensor(past[:, :, 0:E - 1], bcast(const("iotab"), 2, E - 1),
                                            bcast(first[:, 1:E], 1, ROUTED + SHARED), ALU.is_ge).then_inc(step, 1)
                    dve.wait_ge(step, 10)
                    nc.vector.tensor_reduce(own[:], past[:, :, 0:E - 1], AX_X, ALU.add).then_inc(step, 1)
                    dve.wait_ge(step, 11)
                    if E < NE:
                        nc.vector.memset(own[:, ROUTED:], float(E)).then_inc(step, 1)
                    else:
                        nc.vector.tensor_copy(own[:, ROUTED:], own[:, ROUTED:]).then_inc(step, 1)
                    dve.wait_ge(step, 12)
                    nc.vector.tensor_copy(owner[:], own[:]).then_inc(step, 1)
                    dve.wait_ge(ranked, 1)
                    nc.vector.scalar_tensor_tensor(base[:], bcast(first[:], 1, T), float(P), rank[:], ALU.mult, ALU.add)\
                        .then_inc(step, 1)
                    dve.wait_ge(step, 14)
                    for k in range(TOP):
                        nc.vector.tensor_tensor(pick[k][:], oh[k][:], base[:], ALU.mult).then_inc(step, 1)
                    dve.wait_ge(step, 16)
                    for k in range(TOP):
                        nc.vector.tensor_reduce(sf[k][:], pick[k][:], AX_X, ALU.add).then_inc(step, 1)
                    dve.wait_ge(step, 18)
                    for k in range(TOP):
                        nc.vector.tensor_copy(slot[k][:], sf[k][:])

    def blocks(tag, w_gate, w_up, w_down, F, NB, experts_n, owner):
        FC = -(-F // P)
        FW = [min(P, F - f * P) for f in range(FC)]
        HALVES = -(-F // 512)
        FH = F // HALVES
        FULL = F // P
        with ExitStack() as st:
            sem = Semaphores(nc, st, f"{tag}b")
            tmp = lambda n, s: st.enter_context(nc.sbuf_tensor(f"{tag}b_{n}", s, F32))
            ps = lambda n, s: st.enter_context(nc.psum_tensor(f"{tag}b_{n}", s, F32))
            xb = [tmp(f"xb{j}", [P, D]) for j in range(2)]
            wg, wu = ([tmp(f"{n}{j}", [P, KC, F]) for j in range(2)] for n in ("wg", "wu"))
            wd = [tmp(f"wd{j}", [P, FC, D]) for j in range(2)]
            xT, sg, hT = tmp("xT", [P, KC, P]), tmp("sg", [P, F]), tmp("hT", [P, FC, P])
            h, yb = ([tmp(f"{n}{j}", [P, m]) for j in range(2)] for n, m in (("h", F), ("yb", D)))
            gp, up = ([ps(f"{n}{k}", [P, FH]) for k in range(HALVES)] for n in ("gp", "up"))
            hp = [ps(f"hp{k}", [P, 4, P]) for k in range(-(-FC // 4))]
            xp, yp = ps("xp", [P, KC, P]), ps("yp", [P, D])
            x_in, gu_in, d_in = ([sem(f"{n}{j}") for j in range(2)] for n in ("xin", "guin", "din"))
            before = list(stored_before)
            stored_before[0] += NB // 2 + 1
            stored_before[1] += NB // 2
            x_turned, x_copied, gate_made, up_made, sg_done, h_done, h_turned, h_copied, y_made, y_copied = (
                sem(n) for n in ("xt", "xc", "gate", "up", "sg", "h", "ht", "hc", "ymade", "yc"))
            DN = 16 if F % P == 0 else 32
            groups = [list(range(g, min(g + 4, FC))) for g in range(0, FC, 4)]
            NG = len(groups)

            with nc.Block() as block:
                @block.sync
                def _(sp):
                    def load(n, j, e, peeled):
                        if not peeled:
                            sp.wait_ge(x_turned, n)
                        sp.dma_start(xb[j][:], x_slots[n * P:n * P + P, :] if peeled else
                                     x_slots.rearrange("(n p) d -> n p d", p=P)[n]).then_inc(x_in[j], 16)
                        if not peeled:
                            sp.wait_ge(up_made, n)
                        sp.dma_start(wg[j][:], w_gate[e].rearrange("(k p) f -> p k f", p=P)).then_inc(gu_in[j], 16)
                        sp.dma_start(wu[j][:], w_up[e].rearrange("(k p) f -> p k f", p=P)).then_inc(gu_in[j], 16)
                        if not peeled:
                            sp.wait_ge(y_made, n)
                        sp.dma_start(wd[j][:, 0:FULL, :],
                                     w_down[e, 0:FULL * P, :].rearrange("(f p) d -> p f d", p=P)).then_inc(d_in[j], 16)
                        if F % P:
                            sp.dma_start(wd[j][0:F % P, FULL, :], w_down[e, FULL * P:F, :]).then_inc(d_in[j], 16)

                    for used in (x_turned, up_made, y_made):
                        sp.sem_inc(used, 1)
                    load(0, 0, sp.value_load(owner[0:1, 0:1], min_val=0, max_val=experts_n - 1), True)
                    with sp.Fori(0, NB // 2) as i:
                        for j in (1, 0):
                            n = i * 2 + 2 - j
                            load(n, j, sp.value_load(owner[0:1, bass.ds(n, 1)], min_val=0, max_val=experts_n - 1), False)

                @block.gpsimd
                def _(pool):
                    def store(n, j):
                        pool.wait_ge(y_copied, n + 2)
                        pool.dma_start(y_slots.rearrange("(n p) d -> n p d", p=P)[n], yb[j][:]).then_inc(rows_out[j], 16)
                    pool.sem_inc(y_copied, 1)
                    store(0, 0)
                    with pool.Fori(0, NB // 2) as i:
                        for j in (1, 0):
                            store(i * 2 + 2 - j, j)
                    pool.wait_ge(rows_out[0], 16 * (before[0] + NB // 2 + 1))
                    pool.wait_ge(rows_out[1], 16 * (before[1] + NB // 2))

                @block.tensor
                def _(pe):
                    def turn_rows(n, j, count):
                        pe.wait_ge(x_in[j], 16 * count)
                        for k in range(KC):
                            last = nc.tensor.transpose(xp[:, k, :], xb[j][:, k * P:(k + 1) * P], ident)
                        last.then_inc(x_turned, 1)

                    def gate_up(n, j, count, peeled=False):
                        pe.wait_ge(x_copied, n + 1)
                        pe.wait_ge(gu_in[j], 32 * count)
                        if not peeled:
                            pe.wait_ge(h_done, n)
                        for wm, dst, done in ((wg, gp, gate_made), (wu, up, up_made)):
                            for v in range(HALVES):
                                for k in range(KC):
                                    last = nc.tensor.matmul(dst[v][:], xT[:, k, :], wm[j][:, k, v * FH:(v + 1) * FH],
                                                            start=(k == 0), stop=(k == KC - 1))
                            last.then_inc(done, 1)

                    def turn_hidden(n, j):
                        pe.wait_ge(h_done, n + 1)
                        for g, chunks in enumerate(groups):
                            for f in chunks:
                                last = nc.tensor.transpose(hp[g][0:FW[f], f % 4, :], h[j][:, f * P:f * P + FW[f]], ident)
                            last.then_inc(h_turned, 1)

                    def down(n, j, count):
                        pe.wait_ge(d_in[j], DN * count)
                        pe.wait_ge(y_copied, n + 1)
                        for g, chunks in enumerate(groups):
                            pe.wait_ge(h_copied, n * NG + g + 1)
                            for f in chunks:
                                last = nc.tensor.matmul(yp[:], hT[0:FW[f], f, :], wd[j][0:FW[f], f, :], start=(f == 0),
                                                        stop=(f == FC - 1))
                        last.then_inc(y_made, 1)

                    turn_rows(0, 0, 1)
                    gate_up(0, 0, 1, peeled=True)
                    turn_rows(1, 1, 1)
                    def body(i, last_block=False):
                        for j in (1, 0):
                            n = i * 2 + 2 - j
                            gate_up(n, j, i + 2 - j)
                            turn_hidden(n - 1, 1 - j)
                            if not (last_block and j == 0):
                                turn_rows(n + 1, 1 - j, i + 2)
                            down(n - 1, 1 - j, i + 1)
                    with pe.Fori(0, NB // 2 - 1) as i:
                        body(i)
                    body(NB // 2 - 1, last_block=True)
                    turn_hidden(NB - 1, 0)
                    down(NB - 1, 0, NB // 2 + 1)

                @block.scalar
                def _(act):
                    def silu(n, peeled=False):
                        act.wait_ge(gate_made, n + 1)
                        if not peeled:
                            act.wait_ge(h_done, n)
                        for v in range(HALVES):
                            last = nc.scalar.activation(sg[:, v * FH:(v + 1) * FH], gp[v][:], ACT.Silu)
                        last.then_inc(sg_done, 1)

                    def copy_hidden(n):
                        act.wait_ge(y_made, n + 1)
                        for g, chunks in enumerate(groups):
                            act.wait_ge(h_turned, n * NG + g + 1)
                            full = [f for f in chunks if FW[f] == P]
                            last = nc.scalar.copy(hT[:, full[0]:full[-1] + 1, :], hp[g][:, 0:len(full), :])
                            for f in chunks:
                                if FW[f] < P:
                                    last = nc.scalar.copy(hT[0:FW[f], f, :], hp[g][0:FW[f], f % 4, :])
                            last.then_inc(h_copied, 1)

                    silu(0, peeled=True)
                    with act.Fori(1, NB) as n:
                        silu(n)
                        copy_hidden(n - 1)
                    copy_hidden(NB - 1)

                @block.vector
                def _(dve):
                    def copy_rows(n):
                        dve.wait_ge(x_turned, n + 2)
                        dve.wait_ge(up_made, n + 1)
                        nc.vector.tensor_copy(xT[:], xp[:]).then_inc(x_copied, 1)

                    def hidden(n, j):
                        dve.wait_ge(sg_done, n + 1)
                        dve.wait_ge(up_made, n + 2)
                        for v in range(HALVES):
                            last = nc.vector.tensor_tensor(h[j][:, v * FH:(v + 1) * FH], up[v][:],
                                                           sg[:, v * FH:(v + 1) * FH], ALU.mult)
                        last.then_inc(h_done, 1)

                    def copy_out(n, j, count):
                        dve.wait_ge(y_made, n + 2)
                        if positive(count):
                            dve.wait_ge(rows_out[j], 16 * before[j] + 16 * count)
                        nc.vector.tensor_copy(yb[j][:], yp[:]).then_inc(y_copied, 1)

                    copy_rows(0)
                    copy_rows(1)
                    hidden(0, 0)
                    def body(i, last_block=False):
                        for j in (1, 0):
                            n = i * 2 + 2 - j
                            if not (last_block and j == 0):
                                copy_rows(n + 1)
                            hidden(n, j)
                            copy_out(n - 1, 1 - j, i)
                    body(0)
                    with dve.Fori(1, NB // 2 - 1) as i:
                        body(i)
                    body(NB // 2 - 1, last_block=True)
                    copy_out(NB - 1, 0, NB // 2)

    def nearest_context(tag):
        with ExitStack() as st:
            sem = Semaphores(nc, st, tag)
            tmp = lambda n, s, dt=F32: st.enter_context(nc.sbuf_tensor(f"{tag}_{n}", s, dt))
            ps = lambda n, s: st.enter_context(nc.psum_tensor(f"{tag}_{n}", s, F32))
            sq, sqc = tmp("sq", [P, T, D]), tmp("sqc", [L, B, D])
            ss, rt, ri = tmp("ss", [P, T]), tmp("rt", [P, T]), tmp("ri", [P, T])
            ssc, rtc, ric = tmp("ssc", [L, B]), tmp("rtc", [L, B]), tmp("ric", [L, B])
            cn, cnT = tmp("cn", [L, B, D]), tmp("cnT", [P, KC, B, L])
            xs, sim = ([tmp(f"{n}{j}", s) for j in range(2)] for n, s in (("xs", [P, KC, P]), ("sim", [P, L])))
            m8, i8, i8f = [tmp(f"m8{j}", [P, 8]) for j in range(2)], [tmp(f"i8{j}", [P, 8], U32) for j in range(2)], \
                [tmp(f"if{j}", [P, 8]) for j in range(2)]
            oh, ohT = [tmp(f"oh{j}", [P, L]) for j in range(2)], [tmp(f"ohT{j}", [L, P]) for j in range(2)]
            sp_, tp_, yp = ([ps(f"{n}{j}", s) for j in range(2)] for n, s in
                            (("sp", [P, L]), ("tp", [L, P]), ("yp", [P, D])))
            cp = ps("cp", [P, KC, B, L])
            squared, summed, rooted, ready, c_turned, c_copied, staged, sim_made, scaled, max_done, idx_done, num_done, \
                hot, hot_turned, hot_copied, picked = (sem(n) for n in (
                    "sq", "sum", "root", "ready", "ct", "cc", "st", "sim", "sc", "max", "idx", "num", "hot", "ht", "hc", "p"))
            added = [sem(f"added{j}") for j in range(2)]
            with nc.Block() as block:
                @block.gpsimd
                def _(pool):
                    nc.gpsimd.tensor_tensor(sqc[:], ctx_tok[:], ctx_tok[:], ALU.mult).then_inc(squared, 1)

                @block.scalar
                def _(act):
                    act.wait_ge(summed, 2)
                    nc.scalar.activation(rt[:], ss[:], ACT.Sqrt).then_inc(rooted, 1)
                    nc.scalar.activation(rtc[:], ssc[:], ACT.Sqrt).then_inc(rooted, 1)
                    act.wait_ge(c_turned, 1)
                    nc.scalar.copy(cnT[:], cp[:]).then_inc(c_copied, 1)
                    for j in range(2):
                        act.sem_inc(added[j], 1)
                    with act.Fori(0, T // 2) as i:
                        for j in range(2):
                            act.wait_ge(added[j], i + 1)
                            nc.scalar.copy(xs[j][:], xnT[:, :, bass.ts(i * 2 + j, P)]).then_inc(staged, 1)
                        for j in range(2):
                            act.wait_ge(hot_turned, i * 2 + j + 1)
                            nc.scalar.copy(ohT[j][:], tp_[j][:]).then_inc(hot_copied, 1)

                @block.vector
                def _(dve):
                    nc.vector.tensor_tensor(sq[:], xn[:], xn[:], ALU.mult).then_inc(squared, 1)
                    dve.wait_ge(squared, 2)
                    nc.vector.tensor_reduce(ss[:], sq[:], AX_X, ALU.add).then_inc(summed, 1)
                    nc.vector.tensor_reduce(ssc[:], sqc[:], AX_X, ALU.add).then_inc(summed, 1)
                    dve.wait_ge(rooted, 2)
                    nc.vector.tensor_scalar(rt[:], rt[:], L2_EPS, None, ALU.max).then_inc(ready, 1)
                    nc.vector.tensor_scalar(rtc[:], rtc[:], L2_EPS, None, ALU.max).then_inc(ready, 1)
                    dve.wait_ge(ready, 2)
                    nc.vector.reciprocal(ri[:], rt[:]).then_inc(ready, 1)
                    nc.vector.reciprocal(ric[:], rtc[:]).then_inc(ready, 1)
                    dve.wait_ge(ready, 4)
                    nc.vector.tensor_tensor(cn[:], ctx_tok[:], bcast(ric[:], 2, D), ALU.mult).then_inc(ready, 1)
                    with dve.Fori(0, T // 2) as i:
                        for j in range(2):
                            t = i * 2 + j
                            dve.wait_ge(sim_made, t + 1)
                            nc.vector.tensor_scalar(sim[j][:], sp_[j][:], ri[:, bass.ds(t, 1)], None, ALU.mult).then_inc(scaled, 1)
                            dve.wait_ge(ready, 5)
                            dve.wait_ge(scaled, t + 1)
                            nc.vector.max(m8[j][:], sim[j][:]).then_inc(max_done, 1)
                            dve.wait_ge(ready, 5)
                            dve.wait_ge(max_done, t + 1)
                            nc.vector.max_index(i8[j][:], m8[j][:], sim[j][:]).then_inc(idx_done, 1)
                            dve.wait_ge(idx_done, t + 1)
                            nc.vector.tensor_copy(i8f[j][:], i8[j][:]).then_inc(num_done, 1)
                            dve.wait_ge(num_done, t + 1)
                            nc.vector.tensor_scalar(oh[j][:], const("iota64"), i8f[j][:, 0:1], None, ALU.is_equal)\
                                .then_inc(hot, 1)
                        for j in range(2):
                            dve.wait_ge(picked, i * 2 + j + 1)
                            nc.vector.tensor_tensor(x[:, i * 2 + j, :], yp[j][:], x[:, i * 2 + j, :], ALU.add)\
                                .then_inc(added[j], 1)

                @block.tensor
                def _(pe):
                    pe.wait_ge(ready, 5)
                    for b in range(B):
                        for k in range(KC):
                            last = nc.tensor.transpose(cp[:, k, b, :], cn[:, b, k * P:(k + 1) * P], ident[0:L, 0:L])
                    last.then_inc(c_turned, 1)
                    pe.wait_ge(c_copied, 1)
                    with pe.Fori(0, B) as b:
                        with pe.Fori(0, TB // 2) as p2:
                            i = b * (TB // 2) + p2
                            for j in range(2):
                                pe.wait_ge(staged, i * 2 + j + 1)
                                for k in range(KC):
                                    last = nc.tensor.matmul(sp_[j][:], xs[j][:, k, :], cnT[:, k, b, :], start=(k == 0),
                                                            stop=(k == KC - 1))
                                last.then_inc(sim_made, 1)
                            for j in range(2):
                                pe.wait_ge(c_copied, 1)
                                pe.wait_ge(hot, i * 2 + j + 1)
                                nc.tensor.transpose(tp_[j][:], oh[j][:], ident).then_inc(hot_turned, 1)
                            for j in range(2):
                                pe.wait_ge(c_copied, 1)
                                pe.wait_ge(hot_copied, i * 2 + j + 1)
                                nc.tensor.matmul(yp[j][:], ohT[j][:], ctx_tok[:, b, :], start=True, stop=True)\
                                    .then_inc(picked, 1)

    C_HALF, C_ONE, C_TWO = 1.5 * 2.0 ** 22, 1.5 * 2.0 ** 23, 1.5 * 2.0 ** 24
    QUANT_STEPS = 14

    def quantise(dve, dst, src, n, bufs, done, base, free=None):
        am, sc, a, m, u1, u2, u3 = bufs
        nb = n // FP4_BLOCK
        v3 = lambda ap: ap.rearrange("p (b i) -> p b i", i=FP4_BLOCK)
        am, sc, a, m, u1, u2, u3 = am[:, 0:nb], sc[:, 0:nb], a[:, 0:n], m[:, 0:n], u1[:, 0:n], u2[:, 0:n], u3[:, 0:n]
        after = lambda k: dve.wait_ge(done, base + k)
        nc.vector.tensor_reduce(am, v3(src), AX_X, ALU.max, apply_absolute_value=True).then_inc(done, 1)
        after(1)
        nc.vector.tensor_scalar(sc, am, 1.0 / 6.0, 1e-12, ALU.mult, ALU.max).then_inc(done, 1)
        after(2)
        nc.vector.reciprocal(am, sc).then_inc(done, 1)
        after(3)
        nc.vector.tensor_scalar(am, am, 1.0 - 2.0 ** -23, None, ALU.mult).then_inc(done, 1)
        after(4)
        nc.vector.tensor_tensor(v3(a), v3(src), bcast(am, 2, FP4_BLOCK), ALU.mult).then_inc(done, 1)
        after(5)
        nc.vector.tensor_scalar(m.bitcast(U32), a.bitcast(U32), 0x7FFFFFFF, None, ALU.bitwise_and).then_inc(done, 1)
        after(6)
        nc.vector.tensor_scalar(u1, m, 2.0, C_HALF, ALU.min, ALU.add).then_inc(done, 1)
        nc.vector.tensor_scalar(u2, m, 2.0, 4.0, ALU.max, ALU.min).then_inc(done, 1)
        nc.vector.tensor_scalar(u3, m, 4.0, C_TWO, ALU.max, ALU.add).then_inc(done, 1)
        after(8)
        nc.vector.tensor_scalar(u2, u2, C_ONE, C_ONE + 2.0, ALU.add, ALU.subtract).then_inc(done, 1)
        after(10)
        nc.vector.scalar_tensor_tensor(u1, u1, C_HALF, u2, ALU.subtract, ALU.add).then_inc(done, 1)
        after(11)
        nc.vector.scalar_tensor_tensor(u1, u3, C_TWO + 4.0, u1, ALU.subtract, ALU.add).then_inc(done, 1)
        after(12)
        nc.vector.scalar_tensor_tensor(u2.bitcast(U32), a.bitcast(U32), 0x80000000, u1.bitcast(U32), ALU.bitwise_and,
                                       ALU.bitwise_or).then_inc(done, 1)
        after(13)
        if free is not None:
            dve.wait_ge(*free)
        return nc.vector.tensor_tensor(v3(dst), v3(u2), bcast(sc, 2, FP4_BLOCK), ALU.mult)

    def fp4_feed_forward(tag, F):
        FC = -(-F // P)
        FW = [min(P, F - f * P) for f in range(FC)]
        FULL = F // P
        HALVES, FH = 2, F // 2
        with ExitStack() as st:
            tmp = lambda n, s: st.enter_context(nc.sbuf_tensor(f"{tag}_{n}", s, F32))
            bufs = [tmp(f"qb{k}", [P, FC * D if k > 1 else FC * D // FP4_BLOCK]) for k in range(7)]
            gT, uT, dT = tmp("gT", [P, KC, F]), tmp("uT", [P, KC, F]), tmp("dT", [P, FC, D])
            with ExitStack() as s2:
                sem = Semaphores(nc, s2, f"{tag}w")
                wn = [s2.enter_context(nc.sbuf_tensor(f"{tag}w_{n}", s, F32)) for n, s in
                      (("gate", [P, FC, D]), ("up", [P, FC, D]), ("down", [P, KC, F]))]
                tp = [s2.enter_context(nc.psum_tensor(f"{tag}w_tp{k}", [P, 512], F32)) for k in range(2)]
                cleared, loaded, steps, quantised, turned, copied = (sem(n) for n in ("clr", "ld", "q", "qd", "t", "tc"))
                jobs = []
                for m, dst in ((0, gT), (1, uT)):
                    for k in range(KC):
                        jobs.append((m, [(f, k) for f in range(4)], dst[:, k, 0:4 * P]))
                        jobs.append((m, [(f, k) for f in range(4, FC)], dst[:, k, 4 * P:F]))
                for f in range(0, FULL, 2):
                    fs = range(f, min(f + 2, FULL))
                    jobs.append((2, [(k, g) for g in fs for k in range(KC)],
                                 dT[:, fs[0]:fs[-1] + 1, :].rearrange("p f d -> p (f d)")))
                jobs.append((2, [(k, FULL) for k in range(KC)], dT[0:FW[FULL], FULL, :]))
                with nc.Block() as block:
                    @block.sync
                    def _(sp):
                        sp.wait_ge(cleared, 2)
                        for m, name in ((0, "L2_ffn_w_gate"), (1, "L2_ffn_w_up")):
                            sp.dma_start(wn[m][:, 0:FULL, :], ins[name][0:FULL * P, :].rearrange("(f p) k -> p f k", p=P))\
                                .then_inc(loaded, 16)
                            sp.dma_start(wn[m][0:F % P, FULL, :], ins[name][FULL * P:F, :]).then_inc(loaded, 16)
                        sp.dma_start(wn[2][:], ins["L2_ffn_w_down"].rearrange("(k p) f -> p k f", p=P)).then_inc(loaded, 16)

                    @block.vector
                    def _(dve):
                        for m in range(2):
                            nc.vector.memset(wn[m][:, FULL, :], 0.0).then_inc(cleared, 1)
                        dve.wait_ge(loaded, 16 * 5)
                        for m in range(3):
                            flat = wn[m][:].rearrange("p a b -> p (a b)")
                            quantise(dve, flat, flat, flat.shape[1], bufs, steps, m * (QUANT_STEPS - 1)).then_inc(quantised, 1)

                    @block.tensor
                    def _(pe):
                        for n, (m, parts, dst) in enumerate(jobs):
                            pe.wait_ge(quantised, m + 1)
                            if n >= 2:
                                pe.wait_ge(copied, n - 1)
                            at = 0
                            for r, c in parts:
                                if m < 2:
                                    last = nc.tensor.transpose(tp[n % 2][:, at:at + FW[r]],
                                                               wn[m][0:FW[r], r, c * P:(c + 1) * P], ident[0:FW[r], 0:FW[r]])
                                    at += FW[r]
                                else:
                                    last = nc.tensor.transpose(tp[n % 2][0:FW[c], at:at + P],
                                                               wn[m][:, r, c * P:c * P + FW[c]], ident)
                                    at += P
                            last.then_inc(turned, 1)

                    @block.scalar
                    def _(act):
                        for n, (m, parts, dst) in enumerate(jobs):
                            act.wait_ge(turned, n + 1)
                            nc.scalar.copy(dst, tp[n % 2][0:dst.shape[0], 0:dst.shape[1]]).then_inc(copied, 1)

            with ExitStack() as s2:
                sem = Semaphores(nc, s2, tag)
                tmp2 = lambda n, s: s2.enter_context(nc.sbuf_tensor(f"{tag}_{n}", s, F32))
                ps = lambda n, s: s2.enter_context(nc.psum_tensor(f"{tag}_{n}", s, F32))
                xq, xT, sg, h, hq, hT = tmp2("xq", [P, D]), tmp2("xT", [P, KC, P]), tmp2("sg", [P, F]), tmp2("h", [P, F]), \
                    tmp2("hq", [P, F]), tmp2("hT", [P, FC, P])
                gp, up = ([ps(f"{n}{k}", [P, FH]) for k in range(HALVES)] for n in ("gp", "up"))
                hp = [ps(f"hp{k}", [P, 4, P]) for k in range(2)]
                xp, yp = ps("xp", [P, KC, P]), ps("yp", [P, D])
                groups = [list(range(g, min(g + 4, FC))) for g in range(0, FC, 4)]
                NG = len(groups)
                xsteps, hsteps, x_quant, x_turned, x_copied, gate_made, up_made, sg_done, h_done, h_quant, h_turned, h_copied, \
                    y_made, added = (sem(n) for n in ("xs", "hs", "xq", "xt", "xc", "gate", "up", "sg", "h", "hq", "ht", "hc",
                                                      "y", "added"))
                with nc.Block() as block:
                    @block.vector
                    def _(dve):
                        def rows(n):
                            quantise(dve, xq[:], xn[:, n, :], D, bufs, xsteps, n * (QUANT_STEPS - 1),
                                     (x_turned, n) if positive(n) else None).then_inc(x_quant, 1)

                        def hidden(n):
                            dve.wait_ge(sg_done, n + 1)
                            dve.wait_ge(up_made, n + 1)
                            for v in range(HALVES):
                                last = nc.vector.tensor_tensor(h[:, v * FH:(v + 1) * FH], up[v][:], sg[:, v * FH:(v + 1) * FH],
                                                               ALU.mult)
                            last.then_inc(h_done, 1)
                            dve.wait_ge(h_done, n + 1)
                            quantise(dve, hq[:], h[:], F, bufs, hsteps, n * (QUANT_STEPS - 1),
                                     (h_turned, n * NG) if positive(n) else None).then_inc(h_quant, 1)

                        def add(n):
                            dve.wait_ge(y_made, n + 2)
                            nc.vector.tensor_tensor(x[:, n, :], yp[:], x[:, n, :], ALU.add).then_inc(added, 1)

                        rows(0)
                        rows(1)
                        hidden(0)
                        with dve.Fori(1, T - 1) as n:
                            rows(n + 1)
                            hidden(n)
                            add(n - 1)
                        hidden(T - 1)
                        add(T - 2)
                        add(T - 1)

                    @block.scalar
                    def _(act):
                        def copy_rows(n):
                            act.wait_ge(x_turned, n + 1)
                            if positive(n):
                                act.wait_ge(up_made, n)
                            nc.scalar.copy(xT[:], xp[:]).then_inc(x_copied, 1)

                        def silu(n):
                            act.wait_ge(gate_made, n + 1)
                            if positive(n):
                                act.wait_ge(h_done, n)
                            for v in range(HALVES):
                                last = nc.scalar.activation(sg[:, v * FH:(v + 1) * FH], gp[v][:], ACT.Silu)
                            last.then_inc(sg_done, 1)

                        def copy_hidden(n):
                            act.wait_ge(y_made, n + 1)
                            for g, chunks in enumerate(groups):
                                act.wait_ge(h_turned, n * NG + g + 1)
                                full = [f for f in chunks if FW[f] == P]
                                last = nc.scalar.copy(hT[:, full[0]:full[-1] + 1, :], hp[g][:, 0:len(full), :])
                                for f in chunks:
                                    if FW[f] < P:
                                        last = nc.scalar.copy(hT[0:FW[f], f, :], hp[g][0:FW[f], f % 4, :])
                                last.then_inc(h_copied, 1)

                        copy_rows(0)
                        silu(0)
                        copy_rows(1)
                        with act.Fori(1, T - 1) as n:
                            silu(n)
                            copy_rows(n + 1)
                            copy_hidden(n - 1)
                        silu(T - 1)
                        copy_hidden(T - 2)
                        copy_hidden(T - 1)

                    @block.tensor
                    def _(pe):
                        def turn_rows(n):
                            pe.wait_ge(x_quant, n + 1)
                            if positive(n):
                                pe.wait_ge(x_copied, n)
                            for k in range(KC):
                                last = nc.tensor.transpose(xp[:, k, :], xq[:, k * P:(k + 1) * P], ident)
                            last.then_inc(x_turned, 1)

                        def gate_up(n):
                            pe.wait_ge(x_copied, n + 1)
                            if positive(n):
                                pe.wait_ge(h_done, n)
                            for wm, dst, done in ((gT, gp, gate_made), (uT, up, up_made)):
                                for v in range(HALVES):
                                    for k in range(KC):
                                        last = nc.tensor.matmul(dst[v][:], xT[:, k, :], wm[:, k, v * FH:(v + 1) * FH],
                                                                start=(k == 0), stop=(k == KC - 1))
                                last.then_inc(done, 1)

                        def turn_hidden(n):
                            pe.wait_ge(h_quant, n + 1)
                            for g, chunks in enumerate(groups):
                                for f in chunks:
                                    last = nc.tensor.transpose(hp[g][0:FW[f], f % 4, :], hq[:, f * P:f * P + FW[f]], ident)
                                last.then_inc(h_turned, 1)

                        def down(n):
                            pe.wait_ge(added, n + 1)
                            for g, chunks in enumerate(groups):
                                pe.wait_ge(h_copied, n * NG + g + 1)
                                for f in chunks:
                                    last = nc.tensor.matmul(yp[:], hT[0:FW[f], f, :], dT[0:FW[f], f, :], start=(f == 0),
                                                            stop=(f == FC - 1))
                            last.then_inc(y_made, 1)

                        pe.sem_inc(added, 1)
                        pe.sem_inc(y_made, 1)
                        turn_rows(0)
                        gate_up(0)
                        turn_rows(1)
                        with pe.Fori(1, T - 1) as n:
                            gate_up(n)
                            turn_rows(n + 1)
                            turn_hidden(n - 1)
                            down(n - 1)
                        gate_up(T - 1)
                        turn_hidden(T - 2)
                        down(T - 2)
                        turn_hidden(T - 1)
                        down(T - 1)

    stages = [
        lambda: (normalise("n0", x, xn),
                 cross_attention("a0", w.q0, w.kv0[:, :, 0:D], w.kv0[:, :, D:2 * D], w.o0, w.bq0, w.bk0, w.bv0, w.bo0)),
        lambda: (normalise("n1", x, xn),
                 experts("e0", 0, x, w.router[0], ins["L0_ffn_gate_proj"], ins["L0_ffn_up_proj"], ins["L0_ffn_down_proj"], 704)),
        lambda: (normalise("n2", x, xn), cross_attention("a1", None, None, None, w.fc1, None, None, None, w.bo1, features=True)),
        lambda: (normalise("n3", x, inner), normalise("r3", inner, xn, w.ln1[:]), latent_attention("l1", inner)),
        lambda: (normalise("n4", inner, xn, w.ln2[:]),
                 experts("e1", 1, inner, w.router[1], ins["L1_ffn_Wg"], ins["L1_ffn_Wu"], ins["L1_ffn_Wd"], 256, shared=True,
                         bias=w.rbias, outer=x)),
        lambda: (normalise("n5", x, xn), nearest_context("c2")),
        lambda: (normalise("n6", x, xn), fp4_feed_forward("f2", 704)),
        lambda: (normalise("n7", x, xn), cross_attention("a3", w.q3, w.k3, w.v3, w.o3, w.bq3, w.bk3, w.bv3, w.bo3)),
        lambda: (normalise("n8", x, xn),
                 experts("e3", 2, x, w.router[2], ins["L3_ffn_W1"], ins["L3_ffn_W2"], ins["L3_ffn_W3"], 512)),
    ]
    for stage in stages:
        stage()

    with ExitStack() as st:
        stored = st.enter_context(nc.semaphore("stored"))
        with nc.Block() as block:
            @block.sync
            def _(sp):
                sp.dma_start(out.rearrange("b (t p) d -> p (b t) d", p=P), x[:]).then_inc(stored, 16)
                sp.wait_ge(stored, 16)


def kernel(**inputs):
    import numpy as _np
    import concourse.bacc as _bacc
    from concourse import mybir as _mybir
    from concourse.bass_utils import run_bass_kernel_spmd as _run

    a = {k: _np.asarray(v) for k, v in inputs.items()}
    D_ = a["x"].shape[-1]
    bkv = a.pop("L0_xattn_bkv")
    a["L0_xattn_bk"], a["L0_xattn_bv"] = bkv[:D_], bkv[D_:]
    for k in ("w_q", "w_k", "w_v", "w_o"):
        a[f"L3_xattn_{k}T"] = a.pop(f"L3_xattn_{k}").T
    a["L1_xattn_fm_wT"] = a.pop("L1_xattn_fm_w").T
    a["L1_xattn_fc_wT"] = a.pop("L1_xattn_fc_w").T
    for k in "gud":
        a[f"L1_ffn_W{k}"] = _np.concatenate([a.pop(f"L1_ffn_W{k}_r"), a.pop(f"L1_ffn_W{k}_s")[None]], axis=0)
    a["consts"] = _constants()

    nc = _bacc.Bacc("TRN2", target_bir_lowering=False, num_devices=1)
    arrays, ins = {}, {}
    for name, v in a.items():
        v = _np.ascontiguousarray(v)
        arrays[f"in_{name}"] = v
        ins[name] = nc.dram_tensor(f"in_{name}", v.shape, _mybir.dt.from_np(v.dtype), kind="ExternalInput").ap()
    out = nc.dram_tensor("out_x", a["x"].shape, F32, kind="ExternalOutput").ap()
    program(nc, ins, out)
    r = _run(nc, [arrays], core_ids=[0])
    return r.results[0]["out_x"]
```

```python
from contextlib import ExitStack

import numpy as np
import concourse.bass as bass
from concourse import mybir

ALU = mybir.AluOpType
ACT = mybir.ActivationFunctionType
F32 = mybir.dt.float32
BF16 = mybir.dt.bfloat16
I32 = mybir.dt.int32
U32 = mybir.dt.uint32
AX_X = mybir.AxisListType.X

P = 128
B, S, D = 4, 512, 256
T = B * S // P
TB = S // P
KC = D // P
L = 64
H, HD = 16, 16
HC = H // KC
SCALE = HD ** -0.5
LAT = 64
HH = HD // 2
NE = 8
TOP = 2
LN_EPS, RMS_EPS, L2_EPS = 1e-5, 1e-5, 1e-12
ROUTED = (TOP * B * S + NE * (P - 1)) // P
SHARED = T
SLOTS = (ROUTED + SHARED) * P
NEG = -1.0e30
FP4_BLOCK = 16

CONST = {}


def _constants():
    p = np.arange(P)
    parts = {
        "ident": np.eye(P),
        "before": (p[:, None] < p[None, :]),
        "ones": np.ones((P, P)),
        "causal": np.where(p[:, None] >= p[None, :], 0.0, NEG),
        "head8": (p[:, None] // HD == np.arange(HC)[None, :]),
        "parity": (p[:, None] // L == np.arange(2)[None, :]),
        "iota8": np.tile(np.arange(NE), (P, 1)),
        "full": np.tile(np.arange(T) * P, (P, 1)),
        "iotab": np.tile(np.arange(ROUTED + SHARED), (P, 1)),
        "tri8": np.tile((np.arange(NE)[None, :] < np.arange(NE)[:, None]).ravel(), (P, 1)),
        "iota64": np.tile(np.arange(L), (P, 1)),
    }
    r = p % HD - HH
    inv = np.float32(1.0) / np.float32(10000.0) ** (np.arange(0, HH, 2, dtype=np.float32) / np.float32(HH))
    freqs = np.arange(S, dtype=np.float32)[None, :] * inv[r % (HH // 2)][:, None].astype(np.float32)
    parts["cos"] = np.where((r >= 0)[:, None], np.cos(freqs), 1.0)
    parts["sin"] = np.where((r >= 0)[:, None], np.sin(freqs), 0.0)
    at = 0
    for k, v in parts.items():
        CONST[k] = (at, at + v.shape[1])
        at += v.shape[1]
    return np.concatenate([np.asarray(v, np.float32) for v in parts.values()], axis=1)


def positive(n):
    return not isinstance(n, int) or n > 0


def within(n, count):
    return n if isinstance(n, int) else n.with_bounds(min_val=0, max_val=count - 1)


class Semaphores:

    def __init__(self, nc, stage, tag):
        self.nc, self.tag, self.made = nc, tag, []
        stage.callback(self.clear)

    def clear(self):
        for s in self.made:
            self.nc.gpsimd.sem_clear(s)
            self.nc.release_semaphore(s)

    def __call__(self, name):
        self.made.append(self.nc.alloc_semaphore(f"{self.tag}_{name}"))
        return self.made[-1]


def bcast(ap, axis, n):
    ap = ap.unsqueeze(axis)
    shape = list(ap.shape)
    shape[axis] = n
    return ap.broadcast_to(shape)


def program(nc, ins, out):
    ctx = ExitStack()
    with ctx:
        build(nc, ctx, ins, out)


def build(nc, ctx, ins, out):
    def sb(name, shape, dt=F32):
        return ctx.enter_context(nc.sbuf_tensor(name, shape, dt))

    consts = sb("consts", [P, ins["consts"].shape[1]])

    def const(k):
        return consts[:, CONST[k][0]:CONST[k][1]]

    ident, ones = const("ident"), const("ones")

    x = sb("x", [P, T, D])
    inner = sb("inner", [P, T, D])
    xn = sb("xn", [P, T, D])
    xnT = sb("xnT", [P, KC, T * P])
    ctx_tok = sb("ctx_tok", [L, B, D])
    ctxT = sb("ctxT", [P, KC, B, L])
    ctxT2 = sb("ctxT2", [P, KC, B, 2, L])
    ident_h = sb("ident_h", [P, P], BF16)
    causal_h = sb("causal_h", [P, P], BF16)
    x_slots = nc.dram_tensor("x_slots", [SLOTS, D], F32, kind="Internal").ap()
    y_slots = nc.dram_tensor("y_slots", [SLOTS, D], F32, kind="Internal").ap()

    RING = 8
    pool_sem = lambda n: ctx.enter_context(nc.semaphore(n))
    diag, rows_put = pool_sem("diag_loaded"), pool_sem("rows_put")
    rows_got = [pool_sem(f"rows_got{r}") for r in range(RING)]
    rows_out = [pool_sem(f"rows_out{j}") for j in range(2)]
    stored_before = [0, 0]

    class Small:
        pass
    w = Small()
    loads = []

    def matrix(name, n_in, n_out):
        t = sb(f"w_{name}", [P, n_in // P, n_out])
        loads.append((t[:], ins[name].rearrange("(k p) n -> p k n", p=P)))
        return t

    def rows(name, n_in, n_out):
        t = sb(f"w_{name}", [n_in, n_out])
        loads.append((t[:], ins[name]))
        return t

    def column(name, n):
        t = sb(f"c_{name}", [P, n // P])
        for k in range(n // P):
            loads.append((t[:, k:k + 1], ins[name][k * P:(k + 1) * P].rearrange("(p a) -> p a", a=1)))
        return t

    def spread(name, n):
        t = sb(f"s_{name}", [P, n])
        loads.append((t[:], ins[name].partition_broadcast(P)))
        return t

    w.q0, w.kv0, w.o0 = matrix("L0_xattn_Wq", D, D), matrix("L0_xattn_Wkv", D, 2 * D), matrix("L0_xattn_Wo", D, D)
    w.bq0, w.bk0 = column("L0_xattn_bq", D), column("L0_xattn_bk", D)
    w.bv0, w.bo0 = spread("L0_xattn_bv", D), spread("L0_xattn_bo", D)
    w.q3, w.k3, w.v3, w.o3 = (matrix(f"L3_xattn_w_{k}T", D, D) for k in "qkvo")
    w.bq3, w.bk3 = column("L3_xattn_b_q", D), column("L3_xattn_b_k", D)
    w.bv3, w.bo3 = spread("L3_xattn_b_v", D), spread("L3_xattn_b_o", D)
    w.fc1, w.bo1 = matrix("L1_xattn_fc_wT", 2 * D, D), spread("L1_xattn_fc_b", D)
    w.ln1, w.ln2 = spread("L1_ffn_w_ln1", D), spread("L1_ffn_w_ln2", D)
    w.kvd, w.qd = matrix("L1_ffn_W_kvd", D, LAT), matrix("L1_ffn_W_qd", D, LAT)
    w.ku, w.qu, w.vu = rows("L1_ffn_W_ku", LAT, H * HH), rows("L1_ffn_W_qu", LAT, H * HH), rows("L1_ffn_W_vu", LAT, D)
    w.ropeq, w.ropek = rows("L1_ffn_W_ropeq", LAT, H * HH), matrix("L1_ffn_W_ropek", D, H * HH)
    w.o1 = matrix("L1_ffn_W_o", D, D)
    w.router = [matrix("L0_ffn_router_w", D, NE), matrix("L1_ffn_W_router", D, NE - 1), matrix("L3_ffn_Wg", D, NE)]
    w.rbias = spread("L1_ffn_routing_bias", NE - 1)
    w.fm = sb("fm_diag", [P, P])
    w.fmb = sb("fm_bias", [P, 1])
    w.fmb_neg = sb("fm_bias_neg", [P, 1])
    w.fmb_row = sb("fm_bias_row", [P, HD])

    with ExitStack() as st:
        sem = Semaphores(nc, st, "p")
        loaded, zeroed, tr_done, tr_copied, prep, x_zero = (sem(n) for n in (
            "loaded", "zeroed", "tr", "trc", "prep", "xzero"))
        tp = st.enter_context(nc.psum_tensor("ctx_tp", [P, KC, B * L], F32))
        ctx_load = st.enter_context(nc.sbuf_tensor("ctx_load", [P, B * L // P, D], F32))
        with nc.Block() as block:
            n_first = 5 + len(loads)

            @block.sync
            def _(sp):
                sp.dma_start(consts[:], ins["consts"]).then_inc(loaded, 16)
                sp.dma_start(x[:], ins["x"].rearrange("b (t p) d -> p (b t) d", p=P)).then_inc(loaded, 16)
                sp.dma_start(ctx_load[:], ins["ctx_1024"].rearrange("b l d -> (b l) d")
                             .rearrange("(k p) d -> p k d", p=P)).then_inc(loaded, 16)
                sp.dma_start(ctx_tok[:], ins["ctx_1024"].rearrange("b l d -> l b d")).then_inc(loaded, 16)
                sp.dma_start(w.fmb_row[:], ins["L1_xattn_fm_b"].partition_broadcast(P)).then_inc(loaded, 16)
                for dst, src in loads:
                    sp.dma_start(dst, src).then_inc(loaded, 16)
                sp.wait_ge(zeroed, 1)
                slots = x_slots.rearrange("(k p) d -> p k d", p=P)
                for k in range(0, SLOTS // P, T):
                    n = min(T, SLOTS // P - k)
                    sp.dma_start(slots[:, k:k + n, :], xn[:, 0:n, :]).then_inc(x_zero, 16)
                sp.wait_ge(x_zero, 16 * (-(-SLOTS // P // T)))

            @block.gpsimd
            def _(pool):
                pool.wait_ge(zeroed, 2)
                for h in range(HC):
                    pool.dma_start(w.fm[h * HD:(h + 1) * HD, h * HD:(h + 1) * HD],
                                   ins["L1_xattn_fm_wT"]).then_inc(diag, 16)
                    pool.dma_start(w.fmb[h * HD:(h + 1) * HD, :],
                                   ins["L1_xattn_fm_b"].rearrange("(p a) -> p a", a=1)).then_inc(diag, 16)
                pool.wait_ge(diag, 32 * HC)

            @block.vector
            def _(dve):
                nc.vector.memset(xn[:], 0.0).then_inc(zeroed, 1)
                nc.vector.memset(w.fm[:], 0.0).then_inc(zeroed, 1)
                dve.wait_ge(loaded, 16 * n_first)
                nc.vector.tensor_copy(ident_h[:], ident).then_inc(prep, 1)
                nc.vector.tensor_copy(causal_h[:], const("causal")).then_inc(prep, 1)
                dve.wait_ge(diag, 32 * HC)
                nc.vector.tensor_scalar(w.fmb_neg[:], w.fmb[:], -1.0, None, ALU.mult).then_inc(prep, 1)
                dve.wait_ge(tr_done, 1)
                nc.vector.tensor_copy(ctxT[:].rearrange("p k b l -> p k (b l)"), tp[:]).then_inc(prep, 1)
                for k in range(KC):
                    nc.vector.tensor_copy(ctxT2[:, k], bcast(tp[:, k, :].rearrange("p (b l) -> p b l", b=B), 2, 2))\
                        .then_inc(prep, 1)

            @block.tensor
            def _(pe):
                pe.wait_ge(loaded, 16 * n_first)
                for t in range(B * L // P):
                    for k in range(KC):
                        last = nc.tensor.transpose(tp[:, k, t * P:(t + 1) * P], ctx_load[:, t, k * P:(k + 1) * P], ident)
                last.then_inc(tr_done, 1)

    def normalise(tag, x, xn, rms_weight=None):
        with ExitStack() as st:
            sem = Semaphores(nc, st, tag)
            tmp = lambda n, s: st.enter_context(nc.sbuf_tensor(f"{tag}_{n}", s, F32))
            stats_done, step, rooted, xn_ready, turned, copied = (sem(n) for n in (
                "stats", "step", "root", "xn", "turned", "copied"))
            st6, mean, var, dif = tmp("st6", [P, T, 6]), tmp("mean", [P, T]), tmp("var", [P, T]), tmp("dif", [P, T])
            m2, root, rstd = tmp("m2", [P, T]), tmp("root", [P, T]), tmp("rstd", [P, T])
            tp = [st.enter_context(nc.psum_tensor(f"{tag}_tp{j}", [P, KC, P], F32)) for j in range(4)]
            with nc.Block() as block:
                @block.vector
                def _(dve):
                    for t in range(T):
                        nc.vector.bn_stats(st6[:, t, :], x[:, t, :]).then_inc(stats_done, 1)
                    dve.wait_ge(stats_done, T)
                    nc.vector.tensor_tensor(mean[:], st6[:, :, 1], st6[:, :, 4], ALU.add).then_inc(step, 1)
                    nc.vector.tensor_tensor(dif[:], st6[:, :, 1], st6[:, :, 4], ALU.subtract).then_inc(step, 1)
                    nc.vector.tensor_tensor(m2[:], st6[:, :, 2], st6[:, :, 5], ALU.add).then_inc(step, 1)
                    dve.wait_ge(step, 3)
                    nc.vector.tensor_scalar(mean[:], mean[:], 0.5, None, ALU.mult).then_inc(step, 1)
                    nc.vector.tensor_tensor(dif[:], dif[:], dif[:], ALU.mult).then_inc(step, 1)
                    dve.wait_ge(step, 5)
                    nc.vector.tensor_scalar(dif[:], dif[:], 0.25, None, ALU.mult).then_inc(step, 1)
                    dve.wait_ge(step, 6)
                    nc.vector.scalar_tensor_tensor(var[:], m2[:], 1.0 / D, dif[:], ALU.mult, ALU.add).then_inc(step, 1)
                    dve.wait_ge(step, 7)
                    if rms_weight is None:
                        nc.vector.tensor_scalar(var[:], var[:], LN_EPS, None, ALU.add).then_inc(step, 1)
                    else:
                        nc.vector.tensor_tensor(dif[:], mean[:], mean[:], ALU.mult).then_inc(step, 1)
                        dve.wait_ge(step, 8)
                        nc.vector.tensor_tensor(var[:], var[:], dif[:], ALU.add).then_inc(step, 1)
                    dve.wait_ge(rooted, 1)
                    if rms_weight is not None:
                        nc.vector.tensor_scalar(root[:], root[:], RMS_EPS, None, ALU.add).then_inc(step, 1)
                        dve.wait_ge(step, 10)
                    nc.vector.reciprocal(rstd[:], root[:]).then_inc(step, 1)
                    dve.wait_ge(step, 9 if rms_weight is None else 11)
                    for t in range(T):
                        if rms_weight is None:
                            nc.vector.tensor_scalar(xn[:, t, :], x[:, t, :], mean[:, t:t + 1], rstd[:, t:t + 1],
                                                    ALU.subtract, ALU.mult).then_inc(xn_ready, 1)
                        else:
                            nc.vector.scalar_tensor_tensor(xn[:, t, :], x[:, t, :], rstd[:, t:t + 1], rms_weight,
                                                           ALU.mult, ALU.mult).then_inc(xn_ready, 1)

                @block.scalar
                def _(act):
                    act.preload_act_table(ACT.Sqrt)
                    act.wait_ge(step, 8 if rms_weight is None else 9)
                    nc.scalar.activation(root[:], var[:], ACT.Sqrt).then_inc(rooted, 1)
                    for t in range(T):
                        act.wait_ge(turned, t + 1)
                        nc.scalar.copy(xnT[:, :, t * P:(t + 1) * P], tp[t % 4][:]).then_inc(copied, 1)

                @block.tensor
                def _(pe):
                    for t in range(T):
                        if t >= 4:
                            pe.wait_ge(copied, t - 3)
                        pe.wait_ge(xn_ready, t + 1)
                        for k in range(KC):
                            last = nc.tensor.transpose(tp[t % 4][:, k, :], xn[:, t, k * P:(k + 1) * P], ident)
                        last.then_inc(turned, 1)

    def cross_attention(tag, wq, wk, wv, wo, bq, bk, bv, bo, features=False):
        SG = 2 if features else 1
        VD = HD * SG
        OC = H * VD // P
        PAIRS = H // 2
        with ExitStack() as st:
            sem = Semaphores(nc, st, tag)
            tmp = lambda n, s: st.enter_context(nc.sbuf_tensor(f"{tag}_{n}", s, F32))
            ps = lambda n, s: st.enter_context(nc.psum_tensor(f"{tag}_{n}", s, F32))
            kd = tmp("kd", [P, B, SG, KC, HC, L])
            vd = tmp("vd", [P, B, PAIRS, 2, VD])
            kT = tmp("kT", [P, SG, KC, B, L])
            vt = tmp("vt", [P, B, H, VD])
            vz = tmp("vz", [P, B, D])
            qT = tmp("qT", [P, SG, KC, 2 * P])
            pr = [tmp(f"pr{j}", [P, H, L]) for j in range(2)]
            pT, ho, hoT = tmp("pT", [P, PAIRS, P]), tmp("ho", [P, H, VD]), tmp("hoT", [P, OC, P])
            mx, sm = tmp("mx", [P, H]), tmp("sm", [P, H])
            rs = [tmp(f"rs{j}", [P, H]) for j in range(2)]
            sc = [ps(f"sc{j}", [P, KC, HC * L]) for j in range(2)]
            ob = [ps(f"ob{j}", [P, H * VD]) for j in range(2)]
            qb, yb = ps("qb", [P, KC, 2 * P]), ps("yb", [P, D])

            k_made, k_done, k_spread, v_made, v_done, v_exp, v_spread = (sem(n) for n in (
                "kmade", "kdone", "kspread", "vmade", "vdone", "vexp", "vspread"))
            with nc.Block() as block:
                @block.tensor
                def _(pe):
                    for c in range(KC):
                        if features:
                            last = nc.tensor.matmul(qb[:, c, :], w.fm[:], ctxT[:, c].rearrange("p b l -> p (b l)"),
                                                    start=True, stop=True)
                        else:
                            for k in range(KC):
                                last = nc.tensor.matmul(qb[:, c, :], wk[:, k, c * P:(c + 1) * P],
                                                        ctxT[:, k].rearrange("p b l -> p (b l)"),
                                                        start=(k == 0), stop=(k == KC - 1))
                    last.then_inc(k_made, 1)
                    for b in range(B):
                        for k in range(KC):
                            lhs = ctxT2[:, k, b].rearrange("p a l -> p (a l)")
                            dst = sc[b // 2][:, b % 2, 0:D]
                            if features:
                                last = nc.tensor.matmul(dst[:, k * P:(k + 1) * P], lhs, w.fm[:], start=True, stop=True)
                            else:
                                last = nc.tensor.matmul(dst, lhs, wv[:, k, :], start=(k == 0), stop=(k == KC - 1))
                        last.then_inc(v_made, 1)

                @block.scalar
                def _(act):
                    if features:
                        act.wait_ge(k_made, 1)
                        for s in range(SG):
                            nc.scalar.activation(kT[:, s].rearrange("p c b l -> p c (b l)"), qb[:], ACT.Exp,
                                                 bias=(w.fmb, w.fmb_neg)[s][:, 0:1], scale=(1.0, -1.0)[s])\
                                .then_inc(k_done, 1)
                        for b in range(B):
                            act.wait_ge(v_done, b + 1)
                            for s in range(SG):
                                nc.scalar.activation(vt[:, b, :, s * HD:(s + 1) * HD],
                                                     vz[:, b, :].rearrange("p (h d) -> p h d", d=HD), ACT.Exp,
                                                     scale=(1.0, -1.0)[s]).then_inc(v_exp, 1)

                @block.gpsimd
                def _(pool):
                    nc.gpsimd.tensor_tensor(x[:], x[:], bcast(bo[:], 1, T), ALU.add)

                @block.vector
                def _(dve):
                    if not features:
                        dve.wait_ge(k_made, 1)
                        for c in range(KC):
                            nc.vector.tensor_scalar(kT[:, 0, c].rearrange("p b l -> p (b l)"), qb[:, c, :],
                                                    bk[:, c:c + 1], SCALE, ALU.add, ALU.mult).then_inc(k_done, 1)
                    for b in range(B):
                        dve.wait_ge(v_made, b + 1)
                        src = sc[b // 2][:, b % 2, 0:D]
                        if features:
                            nc.vector.tensor_tensor(vz[:, b, :].rearrange("p (h d) -> p h d", d=HD),
                                                    src.rearrange("p (h d) -> p h d", d=HD),
                                                    bcast(w.fmb_row[:], 1, H), ALU.add).then_inc(v_done, 1)
                        else:
                            nc.vector.tensor_tensor(vt[:, b].rearrange("p h d -> p (h d)"), src, bv[:],
                                                    ALU.add).then_inc(v_done, 1)
                    dve.wait_ge(k_done, KC)
                    for b in range(B):
                        for s in range(SG):
                            for c in range(KC):
                                key = bcast(kT[:, s, c, b, :], 1, HC)
                                mask = bcast(const("head8"), 2, L)
                                nc.vector.tensor_tensor(kd[:, b, s, c], key, mask, ALU.mult).then_inc(k_spread, 1)
                    if features:
                        dve.wait_ge(k_spread, B * SG * KC)
                        nc.vector.tensor_scalar(kd[:].rearrange("p b s c h l -> p (b s c h l)"),
                                                kd[:].rearrange("p b s c h l -> p (b s c h l)"), D ** -0.5, None,
                                                ALU.mult).then_inc(k_spread, 1)
                        dve.wait_ge(v_exp, SG * B)
                    else:
                        dve.wait_ge(v_done, B)
                    for b in range(B):
                        nc.vector.tensor_tensor(vd[:, b], vt[:, b].rearrange("p (r a) d -> p r a d", a=2),
                                                bcast(bcast(const("parity"), 1, PAIRS), 3, VD), ALU.mult)\
                            .then_inc(v_spread, 1)

            q_made, q_done, sc_made, max_done, less_done, exp_done, sum_done, rec_done, pt_made, pt_half, o_made, \
                o_done, ot_made, ot_done, y_made, added = (sem(n) for n in (
                    "q", "qd", "sc", "max", "less", "exp", "sum", "rec", "pt", "ptd", "o", "od", "ot", "otd", "y", "added"))
            PAIR = T // 2
            with nc.Block() as block:
                @block.tensor
                def _(pe):
                    def queries(i):
                        for c in range(KC):
                            if features:
                                last = nc.tensor.matmul(qb[:, c, :], w.fm[:], xnT[:, c, bass.ts(i, 2 * P)], start=True, stop=True)
                            else:
                                for k in range(KC):
                                    last = nc.tensor.matmul(qb[:, c, :], wq[:, k, c * P:(c + 1) * P],
                                                            xnT[:, k, bass.ts(i, 2 * P)], start=(k == 0), stop=(k == KC - 1))
                        last.then_inc(q_made, 1)

                    def scores(i, j, b):
                        pe.wait_ge(q_done, (i + 1) * SG * KC)
                        for c in range(KC):
                            for s in range(SG):
                                last = nc.tensor.matmul(sc[j][:, c, :], qT[:, s, c, j * P:(j + 1) * P],
                                                        kd[:, b, s, c].rearrange("p h l -> p (h l)"),
                                                        start=(s == 0), stop=(s == SG - 1))
                        last.then_inc(sc_made, 1)

                    def turn_outputs(t, j):
                        pe.wait_ge(o_done, t + 1)
                        for c in range(OC):
                            last = nc.tensor.transpose(ob[j][:, c * P:(c + 1) * P],
                                                       ho[:].rearrange("p h d -> p (h d)")[:, c * P:(c + 1) * P], ident)
                        last.then_inc(ot_made, 1)

                    def turn_probs(t, j):
                        pe.wait_ge(exp_done, t + 1)
                        for r in range(PAIRS):
                            last = nc.tensor.transpose(sc[j][:, r // 4, (r % 4) * P:(r % 4 + 1) * P],
                                                       pr[j][:, 2 * r:2 * r + 2, :].rearrange("p h l -> p (h l)"), ident)
                            if r % 4 == 3:
                                last.then_inc(pt_made, 1)

                    def project(t):
                        pe.wait_ge(ot_done, t + 1)
                        if positive(t):
                            pe.wait_ge(added, t)
                        for c in range(OC):
                            last = nc.tensor.matmul(yb[:], hoT[:, c, :], wo[:, c, :], start=(c == 0), stop=(c == OC - 1))
                        last.then_inc(y_made, 1)

                    def values(t, j, b):
                        for half in range(2):
                            pe.wait_ge(pt_half, t * 2 + half + 1)
                            for r in range(half * 4, half * 4 + 4):
                                last = nc.tensor.matmul(ob[j][:, r * 2 * VD:(r + 1) * 2 * VD], pT[:, r, :],
                                                        vd[:, b, r].rearrange("p a d -> p (a d)"), start=True, stop=True)
                        last.then_inc(o_made, 1)

                    def body(i, first=False, last_pair=False):
                        t = i * 2
                        scores(i, 1, i >> 1)
                        if not first:
                            turn_outputs(t - 1, 1)
                        turn_probs(t, 0)
                        if not last_pair:
                            queries(i + 1)
                        if not first:
                            project(t - 1)
                        values(t, 0, i >> 1)
                        if not last_pair:
                            scores(i + 1, 0, within((i + 1) >> 1, B))
                        turn_outputs(t, 0)
                        turn_probs(t + 1, 1)
                        project(t)
                        values(t + 1, 1, i >> 1)

                    queries(0)
                    scores(0, 0, 0)
                    body(0, first=True)
                    with pe.Fori(1, PAIR - 1) as i:
                        body(i)
                    body(PAIR - 1, last_pair=True)
                    turn_outputs(T - 1, 1)
                    project(T - 1)

                @block.scalar
                def _(act):
                    def queries(i):
                        act.wait_ge(q_made, i + 1)
                        for c in range(KC):
                            for s in range(SG):
                                nc.scalar.activation(qT[:, s, c, :], qb[:, c, :], ACT.Exp if features else ACT.Identity,
                                                     bias=(w.fmb, w.fmb_neg)[s][:, 0:1] if features else bq[:, c:c + 1],
                                                     scale=(1.0, -1.0)[s]).then_inc(q_done, 1)

                    def exponentials(t, j):
                        act.wait_ge(less_done, t + 1)
                        nc.scalar.activation(pr[j][:], pr[j][:], ACT.Exp).then_inc(exp_done, 1)

                    def copy_outputs(t, j):
                        act.wait_ge(ot_made, t + 1)
                        nc.scalar.copy(hoT[:].rearrange("p c q -> p (c q)"), ob[j][:]).then_inc(ot_done, 1)

                    def copy_probs(t, j):
                        for half in range(2):
                            act.wait_ge(pt_made, t * 2 + half + 1)
                            nc.scalar.copy(pT[:, 4 * half:4 * half + 4, :].rearrange("p r q -> p (r q)"), sc[j][:, half, :])\
                                .then_inc(pt_half, 1)

                    def body(i, first=False, last_pair=False):
                        t = i * 2
                        if not first:
                            copy_outputs(t - 1, 1)
                        copy_probs(t, 0)
                        if not last_pair:
                            queries(i + 1)
                        exponentials(t + 1, 1)
                        copy_outputs(t, 0)
                        copy_probs(t + 1, 1)
                        if not last_pair:
                            exponentials(t + 2, 0)

                    act.preload_act_table(ACT.Exp)
                    queries(0)
                    exponentials(0, 0)
                    body(0, first=True)
                    with act.Fori(1, PAIR - 1) as i:
                        body(i)
                    body(PAIR - 1, last_pair=True)
                    copy_outputs(T - 1, 1)

                @block.vector
                def _(dve):
                    def less_maximum(t, j):
                        s3 = sc[j][:].rearrange("p c (h l) -> p (c h) l", l=L)
                        dve.wait_ge(sc_made, t + 1)
                        nc.vector.tensor_reduce(mx[:], s3, AX_X, ALU.max).then_inc(max_done, 1)
                        dve.wait_ge(max_done, t + 1)
                        nc.vector.tensor_tensor(pr[j][:], s3, bcast(mx[:], 2, L), ALU.subtract).then_inc(less_done, 1)

                    def sums(t, j):
                        dve.wait_ge(exp_done, t + 1)
                        nc.vector.tensor_reduce(sm[:], pr[j][:], AX_X, ALU.add).then_inc(sum_done, 1)
                        dve.wait_ge(sum_done, t + 1)
                        nc.vector.reciprocal(rs[j][:], sm[:]).then_inc(rec_done, 1)

                    def divide(t, j):
                        dve.wait_ge(rec_done, t + 1)
                        dve.wait_ge(o_made, t + 1)
                        nc.vector.tensor_tensor(ho[:], ob[j][:].rearrange("p (h d) -> p h d", d=VD),
                                                bcast(rs[j][:], 2, VD), ALU.mult).then_inc(o_done, 1)

                    def add(t):
                        dve.wait_ge(y_made, t + 1)
                        nc.vector.tensor_tensor(x[:, t, :], yb[:], x[:, t, :], ALU.add).then_inc(added, 1)

                    def body(i, first=False, last_pair=False):
                        t = i * 2
                        if not first:
                            divide(t - 1, 1)
                        sums(t, 0)
                        less_maximum(t + 1, 1)
                        if not first:
                            add(t - 1)
                        divide(t, 0)
                        sums(t + 1, 1)
                        if not last_pair:
                            less_maximum(t + 2, 0)
                        add(t)

                    less_maximum(0, 0)
                    body(0, first=True)
                    with dve.Fori(1, PAIR - 1) as i:
                        body(i)
                    body(PAIR - 1, last_pair=True)
                    divide(T - 1, 1)
                    add(T - 1)

    def latent_attention(tag, x):
        with ExitStack() as st:
            sem = Semaphores(nc, st, tag)
            tmp = lambda n, s: st.enter_context(nc.sbuf_tensor(f"{tag}_{n}", s, F32))
            ps = lambda n, s: st.enter_context(nc.psum_tensor(f"{tag}_{n}", s, F32))
            qa, qr, ka = (tmp(n, [LAT, KC, HC, HD]) for n in ("qa", "qr", "ka"))
            kx, kr = (tmp(n, [P, KC, KC, HC, HD]) for n in ("kx", "kr"))
            qT, kT = tmp("qT", [P, B, KC, S]), tmp("kT", [P, B, KC, S])
            va = tmp("va", [P, T, H, HD + 1])
            laid = sem("laid")
            with nc.Block() as block:
                @block.gpsimd
                def _(pool):
                    for t in (qa, qr, ka, kx, kr):
                        nc.gpsimd.memset(t[:], 0.0).then_inc(laid, 1)
                    nc.gpsimd.memset(va[:], 1.0).then_inc(laid, 1)

                @block.vector
                def _(dve):
                    heads = lambda m: m.rearrange("p (c h d) -> p c h d", c=KC, d=HH)
                    dve.wait_ge(laid, 6)
                    nc.vector.tensor_copy(qa[:, :, :, 0:HH], heads(w.qu[:]))
                    nc.vector.tensor_copy(qa[:, :, :, HH:HD], heads(w.ropeq[:]))
                    nc.vector.tensor_copy(ka[:, :, :, 0:HH], heads(w.ku[:]))
                    q = HH // 2
                    nc.vector.tensor_scalar(qr[:, :, :, HH:HH + q], heads(w.ropeq[:])[:, :, :, q:HH], -1.0, None, ALU.mult)
                    nc.vector.tensor_copy(qr[:, :, :, HH + q:HD], heads(w.ropeq[:])[:, :, :, 0:q])
                    for k in range(KC):
                        rk = heads(w.ropek[:, k, :])
                        nc.vector.tensor_copy(kx[:, k, :, :, HH:HD], rk)
                        nc.vector.tensor_scalar(kr[:, k, :, :, HH:HH + q], rk[:, :, :, q:HH], -1.0, None, ALU.mult)
                        nc.vector.tensor_copy(kr[:, k, :, :, HH + q:HD], rk[:, :, :, 0:q])

            with ExitStack() as s2:
                sem2 = Semaphores(nc, s2, f"{tag}p")
                ps2 = lambda n, s: s2.enter_context(nc.psum_tensor(f"{tag}p_{n}", s, F32))
                tmp2 = lambda n, s: s2.enter_context(nc.sbuf_tensor(f"{tag}p_{n}", s, F32))
                lat = [tmp2(f"lat{n}", [LAT, S]) for n in range(2)]
                t1 = [tmp2(f"t1{n}", [P, S]) for n in range(2)]
                t2 = [tmp2(f"t2{n}", [P, S]) for n in range(2)]
                lp = [ps2(f"lp{n}", [LAT, S]) for n in range(2)]
                pa, pr_ = [ps2(f"pa{n}", [P, S]) for n in range(2)], [ps2(f"pr{n}", [P, S]) for n in range(2)]
                vp = ps2("vp", [P, TB, D])
                lat_made, lat_done, ka_made, kr_made, qa_made, qr_made, cos_k, sin_k, cos_q, sin_q, k_done, q_done, \
                    v_made, v_done = (sem2(n) for n in ("lat", "latd", "ka", "kr", "qa", "qr", "ck", "sk", "cq", "sq",
                                                        "k", "q", "v", "vd"))
                with nc.Block() as block:
                    @block.tensor
                    def _(pe):
                        for bank_read in (cos_k, sin_k, cos_q, sin_q, v_done):
                            pe.sem_inc(bank_read, 1)
                        with pe.Fori(0, B) as b:
                            tokens = lambda k: xnT[:, k, bass.ts(b, S)]
                            for n, wd in ((0, w.kvd), (1, w.qd)):
                                for k in range(KC):
                                    last = nc.tensor.matmul(lp[n][:], wd[:, k, :], tokens(k), start=(k == 0),
                                                            stop=(k == KC - 1))
                                last.then_inc(lat_made, 1)
                            pe.wait_ge(lat_done, b * 2 + 2)
                            for c in range(KC):
                                flat = lambda m: m.rearrange("p h d -> p (h d)")
                                pe.wait_ge(cos_k, b * KC + c + 1)
                                nc.tensor.matmul(pa[0][:], flat(ka[:, c]), lat[0][:], start=True, stop=False)
                                for k in range(KC):
                                    last = nc.tensor.matmul(pa[0][:], flat(kx[:, k, c]), tokens(k), start=False,
                                                            stop=(k == KC - 1))
                                last.then_inc(ka_made, 1)
                                pe.wait_ge(sin_k, b * KC + c + 1)
                                for k in range(KC):
                                    last = nc.tensor.matmul(pr_[0][:], flat(kr[:, k, c]), tokens(k), start=(k == 0),
                                                            stop=(k == KC - 1))
                                last.then_inc(kr_made, 1)
                                pe.wait_ge(cos_q, b * KC + c + 1)
                                nc.tensor.matmul(pa[1][:], flat(qa[:, c]), lat[1][:], start=True, stop=True)\
                                    .then_inc(qa_made, 1)
                                pe.wait_ge(sin_q, b * KC + c + 1)
                                nc.tensor.matmul(pr_[1][:], flat(qr[:, c]), lat[1][:], start=True, stop=True)\
                                    .then_inc(qr_made, 1)
                            pe.wait_ge(v_done, b + 1)
                            for t in range(TB):
                                last = nc.tensor.matmul(vp[:, t, :], lat[0][:, t * P:(t + 1) * P], w.vu[:],
                                                        start=True, stop=True)
                            last.then_inc(v_made, 1)

                    @block.scalar
                    def _(act):
                        with act.Fori(0, B) as b:
                            for n in range(2):
                                act.wait_ge(lat_made, b * 2 + n + 1)
                                nc.scalar.copy(lat[n][:], lp[n][:]).then_inc(lat_done, 1)
                            act.wait_ge(v_made, b + 1)
                            nc.scalar.copy(va[:, bass.ts(b, TB), :, 0:HD].rearrange("p t h d -> p (t h) d"),
                                           vp[:].rearrange("p t (h d) -> p (t h) d", d=HD)).then_inc(v_done, 1)

                    @block.vector
                    def _(dve):
                        for summed in (k_done, q_done):
                            dve.sem_inc(summed, 1)
                        with dve.Fori(0, B * KC) as o:
                            dve.wait_ge(ka_made, o + 1)
                            dve.wait_ge(k_done, o + 1)
                            nc.vector.tensor_tensor(t1[0][:], pa[0][:], const("cos"), ALU.mult).then_inc(cos_k, 1)
                            dve.wait_ge(kr_made, o + 1)
                            nc.vector.tensor_tensor(t2[0][:], pr_[0][:], const("sin"), ALU.mult).then_inc(sin_k, 1)
                            dve.wait_ge(qa_made, o + 1)
                            dve.wait_ge(q_done, o + 1)
                            nc.vector.tensor_tensor(t1[1][:], pa[1][:], const("cos"), ALU.mult).then_inc(cos_q, 1)
                            dve.wait_ge(qr_made, o + 1)
                            nc.vector.tensor_tensor(t2[1][:], pr_[1][:], const("sin"), ALU.mult).then_inc(sin_q, 1)

                    @block.gpsimd
                    def _(pool):
                        with pool.Fori(0, B * KC) as o:
                            pool.wait_ge(sin_k, o + 2)
                            nc.gpsimd.tensor_tensor(kT[:].rearrange("p b c s -> p (b c) s")[:, o, :], t1[0][:], t2[0][:],
                                                    ALU.add).then_inc(k_done, 1)
                            pool.wait_ge(sin_q, o + 2)
                            nc.gpsimd.tensor_tensor(qT[:].rearrange("p b c s -> p (b c) s")[:, o, :], t1[1][:], t2[1][:],
                                                    ALU.add).then_inc(q_done, 1)

            y = xn
            with ExitStack() as s2:
                sem2 = Semaphores(nc, s2, f"{tag}a")
                ps2 = lambda n, s: s2.enter_context(nc.psum_tensor(f"{tag}a_{n}", s, F32))
                tmp2 = lambda n, s: s2.enter_context(nc.sbuf_tensor(f"{tag}a_{n}", s, F32))
                qm = tmp2("qm", [P, S])
                pr = tmp2("pr", [P, TB, S])
                nm, rc = tmp2("nm", [P, TB]), tmp2("rc", [P, TB])
                pT = tmp2("pT", [P, 12, P])
                sc = [ps2(f"sc{q}", [P, S]) for q in range(TB)]
                tp = [ps2(f"tp{n}", [P, TB, P]) for n in range(3)]
                ob = ps2("ob", [P, TB, HD + 1])
                GROUPS = [[(3, k) for k in range(4)], [(2, k) for k in range(3)], [(1, 0), (1, 1), (0, 0)]]
                place = {qk: (n, m) for n, g in enumerate(GROUPS) for m, qk in enumerate(g)}
                q_masked, sc_made, max_done, exp_done, t_made, t_copied, o_made, rec_done, y_done = (sem2(n) for n in (
                    "qm", "sc", "max", "exp", "t", "tc", "o", "rec", "y"))
                hs = const("head8")
                HEADS = B * H
                with nc.Block() as block:
                    @block.vector
                    def _(dve):
                        def queries(n):
                            nc.vector.tensor_scalar(qm[:], qT[:].rearrange("p b c s -> p (b c) s")[:, within(n >> 3, B * KC), :],
                                                    hs[:, bass.ds(n & 7, 1)], SCALE, ALU.mult, ALU.mult).then_inc(q_masked, 1)

                        def maxima(n):
                            for m, q in enumerate(reversed(range(TB))):
                                dve.wait_ge(sc_made, n * TB + m + 1)
                                nc.vector.tensor_reduce(nm[:, q:q + 1], sc[q][:, 0:(q + 1) * P], AX_X, ALU.max,
                                                        negate=True).then_inc(max_done, 1)

                        def copy(n):
                            dve.wait_ge(t_made, n * 3 + 2)
                            nc.vector.tensor_copy(pT[:, 4:7, :], tp[1][:, 0:3, :]).then_inc(t_copied, 1)

                        def divide(n):
                            dve.wait_ge(o_made, n + 1)
                            nc.vector.reciprocal(rc[:], ob[:, :, HD]).then_inc(rec_done, 1)
                            dve.wait_ge(rec_done, n + 1)
                            nc.vector.tensor_tensor(
                                y[:, bass.ts(within(n >> 4, B), TB), :].rearrange("p t (h d) -> p t h d", d=HD)[:, :, n & 15, :],
                                ob[:, :, 0:HD], bcast(rc[:], 2, HD), ALU.mult).then_inc(y_done, 1)

                        queries(0)
                        maxima(0)
                        queries(1)
                        copy(0)
                        with dve.Fori(1, HEADS - 1) as n:
                            maxima(n)
                            queries(n + 1)
                            divide(n - 1)
                            copy(n)
                        maxima(HEADS - 1)
                        divide(HEADS - 2)
                        copy(HEADS - 1)
                        divide(HEADS - 1)

                    @block.scalar
                    def _(act):
                        act.preload_act_table(ACT.Exp)
                        with act.Fori(0, HEADS) as n:
                            for m, q in enumerate(reversed(range(TB))):
                                act.wait_ge(max_done, n * TB + m + 1)
                                nc.scalar.activation(pr[:, q, 0:(q + 1) * P], sc[q][:, 0:(q + 1) * P], ACT.Exp,
                                                     bias=nm[:, q:q + 1]).then_inc(exp_done, 1)
                            for g in (0, 2):
                                act.wait_ge(t_made, n * 3 + g + 1)
                                k = len(GROUPS[g])
                                nc.scalar.copy(pT[:, 4 * g:4 * g + k, :] if g < 2 else pT[:, 7:10, :], tp[g][:, 0:k, :])\
                                    .then_inc(t_copied, 1)

                    @block.tensor
                    def _(pe):
                        def scores(n):
                            pe.wait_ge(q_masked, n + 1)
                            for q in reversed(range(TB)):
                                nc.tensor.matmul(sc[q][:, 0:(q + 1) * P], qm[:, q * P:(q + 1) * P],
                                                 kT[:].rearrange("p b c s -> p (b c) s")[:, within(n >> 3, B * KC), 0:(q + 1) * P],
                                                 start=True, stop=False)
                                nc.tensor.matmul(sc[q][:, q * P:(q + 1) * P], ident_h[:], causal_h[:], start=False,
                                                 stop=True).then_inc(sc_made, 1)

                        def turn(n):
                            for g, blocks in enumerate(GROUPS):
                                pe.wait_ge(exp_done, n * TB + (1, 2, 4)[g])
                                for q, k in blocks:
                                    last = nc.tensor.transpose(tp[g][:, place[q, k][1], :], pr[:, q, k * P:(k + 1) * P], ident)
                                last.then_inc(t_made, 1)

                        def values(n):
                            pe.wait_ge(t_copied, n * 3 + 3)
                            if positive(n):
                                pe.wait_ge(y_done, n)
                            for q in range(TB):
                                for k in range(q + 1):
                                    g, m = place[q, k]
                                    last = nc.tensor.matmul(ob[:, q, :], pT[:, (0, 4, 7)[g] + m, :],
                                                            va[:, within(n >> 4, B) * TB + k, n & 15, :], start=(k == 0), stop=(k == q))
                            last.then_inc(o_made, 1)

                        scores(0)
                        turn(0)
                        scores(1)
                        values(0)
                        with pe.Fori(1, HEADS - 1) as n:
                            turn(n)
                            scores(n + 1)
                            values(n)
                        turn(HEADS - 1)
                        values(HEADS - 1)

            project_tokens(f"{tag}o", y, w.o1, x)

    def project_tokens(tag, y, wo, x):
        with ExitStack() as st:
            sem = Semaphores(nc, st, tag)
            yT = [st.enter_context(nc.sbuf_tensor(f"{tag}_yT{j}", [P, KC, P], F32)) for j in range(2)]
            tp = [st.enter_context(nc.psum_tensor(f"{tag}_tp{j}", [P, KC, P], F32)) for j in range(2)]
            op = [st.enter_context(nc.psum_tensor(f"{tag}_op{j}", [P, D], F32)) for j in range(2)]
            staged, turned, copied, made = sem("staged"), sem("turned"), sem("copied"), sem("made")
            ys = [st.enter_context(nc.sbuf_tensor(f"{tag}_ys{j}", [P, D], F32)) for j in range(2)]
            added = [sem(f"added{j}") for j in range(2)]
            with nc.Block() as block:
                @block.tensor
                def _(pe):
                    with pe.Fori(0, T // 2) as i:
                        for j in range(2):
                            pe.wait_ge(staged, i * 2 + j + 1)
                            for k in range(KC):
                                last = nc.tensor.transpose(tp[j][:, k, :], ys[j][:, k * P:(k + 1) * P], ident)
                            last.then_inc(turned, 1)
                        for j in range(2):
                            pe.wait_ge(copied, i * 2 + j + 1)
                            for k in range(KC):
                                last = nc.tensor.matmul(op[j][:], yT[j][:, k, :], wo[:, k, :], start=(k == 0),
                                                        stop=(k == KC - 1))
                            last.then_inc(made, 1)

                @block.gpsimd
                def _(pool):
                    for j in range(2):
                        pool.sem_inc(added[j], 1)
                    with pool.Fori(0, T // 2) as i:
                        for j in range(2):
                            pool.wait_ge(added[j], i + 1)
                            nc.gpsimd.tensor_copy(ys[j][:], y[:, i * 2 + j, :]).then_inc(staged, 1)

                @block.scalar
                def _(act):
                    with act.Fori(0, T // 2) as i:
                        for j in range(2):
                            act.wait_ge(turned, i * 2 + j + 1)
                            nc.scalar.copy(yT[j][:], tp[j][:]).then_inc(copied, 1)

                @block.vector
                def _(dve):
                    with dve.Fori(0, T // 2) as i:
                        for j in range(2):
                            dve.wait_ge(made, i * 2 + j + 1)
                            nc.vector.tensor_tensor(x[:, i * 2 + j, :], op[j][:], x[:, i * 2 + j, :], ALU.add)\
                                .then_inc(added[j], 1)

    def experts(tag, layer, x, wr, w_gate, w_up, w_down, F, shared=False, bias=None, outer=None):
        E = NE - 1 if shared else NE
        NB = ROUTED + (SHARED if shared else 0)
        FC = -(-F // P)
        FW = [min(P, F - f * P) for f in range(FC)]
        HALVES = -(-F // 512)
        FH = F // HALVES
        assert NB % 2 == 1
        with ExitStack() as st:
            tmp = lambda n, s, dt=F32: st.enter_context(nc.sbuf_tensor(f"{tag}_{n}", s, dt))
            wt = [tmp(f"wt{k}", [P, T]) for k in range(TOP)]
            slot = [tmp(f"slot{k}", [P, T], U32) for k in range(TOP)]
            owner = tmp("owner", [P, ROUTED + SHARED], I32)
            route(tag, wr, E, NB, wt, slot, owner, bias)

            with ExitStack() as s2:
                sem = Semaphores(nc, s2, tag)
                shared_put = sem("shared_put")
                with nc.Block() as block:
                    @block.gpsimd
                    def _(pool):
                        for t in range(T):
                            for k in range(TOP):
                                pool.indirect_dma_start(x_slots[0:ROUTED * P, :], bass.IndirectOffsetOnAxis(ap=slot[k][:, t:t + 1], axis=0),
                                                        xn[:, t, :], None).then_inc(rows_put, 16)
                        pool.wait_ge(rows_put, 16 * TOP * T * (layer + 1))

                    @block.sync
                    def _(sp):
                        if shared:
                            sp.dma_start(x_slots[ROUTED * P:SLOTS, :].rearrange("(t p) d -> p t d", p=P), xn[:])\
                                .then_inc(shared_put, 16)
                            sp.wait_ge(shared_put, 16)

            blocks(tag, w_gate, w_up, w_down, F, NB, E if not shared else NE, owner)

            with ExitStack() as s2:
                sem = Semaphores(nc, s2, tag)
                got = s2.enter_context(nc.sbuf_tensor(f"{tag}_got", [P, RING, D], F32))
                shr = s2.enter_context(nc.sbuf_tensor(f"{tag}_shr", [P, T, D], F32)) if shared else None
                used, shr_got = sem("used"), sem("shr")
                with nc.Block() as block:
                    @block.gpsimd
                    def _(pool):
                        for n in range(T * TOP):
                            if n >= RING:
                                pool.wait_ge(used, n - RING + 1)
                            pool.indirect_dma_start(got[:, n % RING, :], None, y_slots[0:ROUTED * P, :], bass.IndirectOffsetOnAxis(
                                ap=slot[n % TOP][:, n // TOP:n // TOP + 1], axis=0)).then_inc(rows_got[n % RING], 16)

                    @block.sync
                    def _(sp):
                        if shared:
                            sp.dma_start(shr[:], y_slots[ROUTED * P:SLOTS, :].rearrange("(t p) d -> p t d", p=P))\
                                .then_inc(shr_got, 16)

                    @block.vector
                    def _(dve):
                        for n in range(T * TOP):
                            t, k = n // TOP, n % TOP
                            dve.wait_ge(rows_got[n % RING], 16 * (layer * T * TOP // RING + n // RING + 1))
                            if n:
                                dve.wait_ge(used, n)
                            nc.vector.scalar_tensor_tensor(x[:, t, :], got[:, n % RING, :], wt[k][:, t:t + 1], x[:, t, :],
                                                           ALU.mult, ALU.add).then_inc(used, 1)
                        if shared:
                            dve.wait_ge(used, T * TOP)
                            dve.wait_ge(shr_got, 16)
                            nc.vector.tensor_tensor(x[:], shr[:], x[:], ALU.add).then_inc(used, 1)

                        if outer is not None:
                            dve.wait_ge(used, T * TOP + (1 if shared else 0))
                            nc.vector.tensor_tensor(outer[:], outer[:], x[:], ALU.add)

    def route(tag, wr, E, NB, wt, slot, owner, bias):
        with ExitStack() as st:
            sem = Semaphores(nc, st, f"{tag}r")
            tmp = lambda n, s, dt=F32: st.enter_context(nc.sbuf_tensor(f"{tag}r_{n}", s, dt))
            ps = lambda n, s: st.enter_context(nc.psum_tensor(f"{tag}r_{n}", s, F32))
            lg, lb = tmp("lg", [P, T, NE]), tmp("lb", [P, T, NE])
            m8, i8, i8f = tmp("m8", [P, T, 8]), tmp("i8", [P, T, 8], U32), tmp("i8f", [P, T, 8])
            oh = [tmp(f"oh{k}", [P, T, NE]) for k in range(TOP)]
            both, base, pick = tmp("both", [P, T, NE]), tmp("base", [P, T, NE]), [tmp(f"pick{k}", [P, T, NE]) for k in range(TOP)]
            sf = [tmp(f"sf{k}", [P, T]) for k in range(TOP)]
            cnt, over, nb, part, first = tmp("cnt", [P, NE]), tmp("over", [P, NE, T]), tmp("nb", [P, NE]), \
                tmp("part", [P, NE, NE]), tmp("first", [P, NE])
            past, own = tmp("past", [P, ROUTED + SHARED, NE - 1]), tmp("own", [P, ROUTED + SHARED])
            diff, tot = tmp("diff", [P, T]), tmp("tot", [P, T])
            lp, rank, count = ps("lp", [P, T, NE]), ps("rank", [P, T, NE]), ps("count", [P, NE])
            lg_made, lg_done, prob_done, max_done, idx_done, step, ranked, counted, weighed = (sem(n) for n in (
                "lg", "lgd", "prob", "max", "idx", "step", "rank", "count", "wt"))
            with nc.Block() as block:
                @block.tensor
                def _(pe):
                    for t in range(T):
                        for k in range(KC):
                            last = nc.tensor.matmul(lp[:, t, 0:E], xnT[:, k, t * P:(t + 1) * P], wr[:, k, :],
                                                    start=(k == 0), stop=(k == KC - 1))
                    last.then_inc(lg_made, 1)
                    pe.wait_ge(step, 4)
                    nc.tensor.matmul(rank[:], const("before"), both[:], start=True, stop=False)
                    for t in range(T - 1):
                        last = nc.tensor.matmul(rank[:, t + 1:T, :], ones, bcast(both[:, t, :], 1, T - 1 - t), start=False,
                                                stop=(t == T - 2))
                    last.then_inc(ranked, 1)
                    for t in range(T):
                        last = nc.tensor.matmul(count[:], ones, both[:, t, :], start=(t == 0), stop=(t == T - 1))
                    last.then_inc(counted, 1)

                @block.scalar
                def _(act):
                    if bias is not None:
                        act.wait_ge(lg_done, 2)
                        nc.scalar.activation(lg[:, :, 0:E], lb[:, :, 0:E], ACT.Sigmoid).then_inc(prob_done, 1)
                    else:
                        act.wait_ge(weighed, 1)
                        for k in range(TOP):
                            nc.scalar.activation(wt[k][:], diff[:], ACT.Sigmoid, scale=(1.0, -1.0)[k]).then_inc(weighed, 1)

                @block.vector
                def _(dve):
                    if E < NE:
                        nc.vector.memset(lg[:], NEG).then_inc(lg_done, 1)
                    dve.wait_ge(lg_made, 1)
                    if bias is not None:
                        nc.vector.tensor_tensor(lb[:, :, 0:E], lp[:, :, 0:E], bcast(bias[:], 1, T), ALU.add).then_inc(lg_done, 1)
                        dve.wait_ge(prob_done, 1)
                    else:
                        nc.vector.tensor_copy(lg[:], lp[:]).then_inc(lg_done, 1)
                        dve.wait_ge(lg_done, 1)
                    for t in range(T):
                        nc.vector.max(m8[:, t, :], lg[:, t, :]).then_inc(max_done, 1)
                    for t in range(T):
                        dve.wait_ge(max_done, t + 1)
                        nc.vector.max_index(i8[:, t, :], m8[:, t, :], lg[:, t, :]).then_inc(idx_done, 1)
                    dve.wait_ge(idx_done, T)
                    nc.vector.tensor_copy(i8f[:], i8[:]).then_inc(step, 1)
                    dve.wait_ge(step, 1)
                    for k in range(TOP):
                        nc.vector.tensor_tensor(oh[k][:], bcast(i8f[:, :, k], 2, NE), bcast(const("iota8"), 1, T),
                                                ALU.is_equal).then_inc(step, 1)
                    dve.wait_ge(step, 3)
                    nc.vector.tensor_tensor(both[:], oh[0][:], oh[1][:], ALU.add).then_inc(step, 1)
                    if bias is None:
                        nc.vector.tensor_tensor(diff[:], m8[:, :, 0], m8[:, :, 1], ALU.subtract).then_inc(weighed, 1)
                    else:
                        nc.vector.tensor_tensor(diff[:], m8[:, :, 0], m8[:, :, 1], ALU.add).then_inc(weighed, 1)
                        dve.wait_ge(weighed, 1)
                        nc.vector.reciprocal(tot[:], diff[:]).then_inc(weighed, 1)
                        dve.wait_ge(weighed, 2)
                        for k in range(TOP):
                            nc.vector.tensor_tensor(wt[k][:], m8[:, :, k], tot[:], ALU.mult)
                    dve.wait_ge(counted, 1)
                    nc.vector.tensor_copy(cnt[:], count[:]).then_inc(step, 1)
                    dve.wait_ge(step, 5)
                    nc.vector.tensor_tensor(over[:], bcast(cnt[:], 2, T), bcast(const("full"), 1, NE), ALU.is_gt).then_inc(step, 1)
                    dve.wait_ge(step, 6)
                    nc.vector.tensor_reduce(nb[:], over[:], AX_X, ALU.add).then_inc(step, 1)
                    dve.wait_ge(step, 7)
                    nc.vector.tensor_tensor(part[:], bcast(nb[:], 1, NE), const("tri8").rearrange("p (e f) -> p e f", e=NE),
                                            ALU.mult).then_inc(step, 1)
                    dve.wait_ge(step, 8)
                    nc.vector.tensor_reduce(first[:], part[:], AX_X, ALU.add).then_inc(step, 1)
                    dve.wait_ge(step, 9)
                    nc.vector.tensor_tensor(past[:, :, 0:E - 1], bcast(const("iotab"), 2, E - 1),
                                            bcast(first[:, 1:E], 1, ROUTED + SHARED), ALU.is_ge).then_inc(step, 1)
                    dve.wait_ge(step, 10)
                    nc.vector.tensor_reduce(own[:], past[:, :, 0:E - 1], AX_X, ALU.add).then_inc(step, 1)
                    dve.wait_ge(step, 11)
                    if E < NE:
                        nc.vector.memset(own[:, ROUTED:], float(E)).then_inc(step, 1)
                    else:
                        nc.vector.tensor_copy(own[:, ROUTED:], own[:, ROUTED:]).then_inc(step, 1)
                    dve.wait_ge(step, 12)
                    nc.vector.tensor_copy(owner[:], own[:]).then_inc(step, 1)
                    dve.wait_ge(ranked, 1)
                    nc.vector.scalar_tensor_tensor(base[:], bcast(first[:], 1, T), float(P), rank[:], ALU.mult, ALU.add)\
                        .then_inc(step, 1)
                    dve.wait_ge(step, 14)
                    for k in range(TOP):
                        nc.vector.tensor_tensor(pick[k][:], oh[k][:], base[:], ALU.mult).then_inc(step, 1)
                    dve.wait_ge(step, 16)
                    for k in range(TOP):
                        nc.vector.tensor_reduce(sf[k][:], pick[k][:], AX_X, ALU.add).then_inc(step, 1)
                    dve.wait_ge(step, 18)
                    for k in range(TOP):
                        nc.vector.tensor_copy(slot[k][:], sf[k][:])

    def blocks(tag, w_gate, w_up, w_down, F, NB, experts_n, owner):
        FC = -(-F // P)
        FW = [min(P, F - f * P) for f in range(FC)]
        HALVES = -(-F // 512)
        FH = F // HALVES
        FULL = F // P
        with ExitStack() as st:
            sem = Semaphores(nc, st, f"{tag}b")
            tmp = lambda n, s: st.enter_context(nc.sbuf_tensor(f"{tag}b_{n}", s, F32))
            ps = lambda n, s: st.enter_context(nc.psum_tensor(f"{tag}b_{n}", s, F32))
            xb = [tmp(f"xb{j}", [P, D]) for j in range(2)]
            wg, wu = ([tmp(f"{n}{j}", [P, KC, F]) for j in range(2)] for n in ("wg", "wu"))
            wd = [tmp(f"wd{j}", [P, FC, D]) for j in range(2)]
            xT, sg, hT = tmp("xT", [P, KC, P]), tmp("sg", [P, F]), tmp("hT", [P, FC, P])
            h, yb = ([tmp(f"{n}{j}", [P, m]) for j in range(2)] for n, m in (("h", F), ("yb", D)))
            gp, up = ([ps(f"{n}{k}", [P, FH]) for k in range(HALVES)] for n in ("gp", "up"))
            hp = [ps(f"hp{k}", [P, 4, P]) for k in range(-(-FC // 4))]
            xp, yp = ps("xp", [P, KC, P]), ps("yp", [P, D])
            x_in, gu_in, d_in = ([sem(f"{n}{j}") for j in range(2)] for n in ("xin", "guin", "din"))
            before = list(stored_before)
            stored_before[0] += NB // 2 + 1
            stored_before[1] += NB // 2
            x_turned, x_copied, gate_made, up_made, sg_done, h_done, h_turned, h_copied, y_made, y_copied = (
                sem(n) for n in ("xt", "xc", "gate", "up", "sg", "h", "ht", "hc", "ymade", "yc"))
            DN = 16 if F % P == 0 else 32
            groups = [list(range(g, min(g + 4, FC))) for g in range(0, FC, 4)]
            NG = len(groups)

            with nc.Block() as block:
                @block.sync
                def _(sp):
                    def load(n, j, e, peeled):
                        if not peeled:
                            sp.wait_ge(x_turned, n)
                        sp.dma_start(xb[j][:], x_slots[n * P:n * P + P, :] if peeled else
                                     x_slots.rearrange("(n p) d -> n p d", p=P)[n]).then_inc(x_in[j], 16)
                        if not peeled:
                            sp.wait_ge(up_made, n)
                        sp.dma_start(wg[j][:], w_gate[e].rearrange("(k p) f -> p k f", p=P)).then_inc(gu_in[j], 16)
                        sp.dma_start(wu[j][:], w_up[e].rearrange("(k p) f -> p k f", p=P)).then_inc(gu_in[j], 16)
                        if not peeled:
                            sp.wait_ge(y_made, n)
                        sp.dma_start(wd[j][:, 0:FULL, :],
                                     w_down[e, 0:FULL * P, :].rearrange("(f p) d -> p f d", p=P)).then_inc(d_in[j], 16)
                        if F % P:
                            sp.dma_start(wd[j][0:F % P, FULL, :], w_down[e, FULL * P:F, :]).then_inc(d_in[j], 16)

                    for used in (x_turned, up_made, y_made):
                        sp.sem_inc(used, 1)
                    load(0, 0, sp.value_load(owner[0:1, 0:1], min_val=0, max_val=experts_n - 1), True)
                    with sp.Fori(0, NB // 2) as i:
                        for j in (1, 0):
                            n = i * 2 + 2 - j
                            load(n, j, sp.value_load(owner[0:1, bass.ds(n, 1)], min_val=0, max_val=experts_n - 1), False)

                @block.gpsimd
                def _(pool):
                    def store(n, j):
                        pool.wait_ge(y_copied, n + 2)
                        pool.dma_start(y_slots.rearrange("(n p) d -> n p d", p=P)[n], yb[j][:]).then_inc(rows_out[j], 16)
                    pool.sem_inc(y_copied, 1)
                    store(0, 0)
                    with pool.Fori(0, NB // 2) as i:
                        for j in (1, 0):
                            store(i * 2 + 2 - j, j)
                    pool.wait_ge(rows_out[0], 16 * (before[0] + NB // 2 + 1))
                    pool.wait_ge(rows_out[1], 16 * (before[1] + NB // 2))

                @block.tensor
                def _(pe):
                    def turn_rows(n, j, count):
                        pe.wait_ge(x_in[j], 16 * count)
                        for k in range(KC):
                            last = nc.tensor.transpose(xp[:, k, :], xb[j][:, k * P:(k + 1) * P], ident)
                        last.then_inc(x_turned, 1)

                    def gate_up(n, j, count, peeled=False):
                        pe.wait_ge(x_copied, n + 1)
                        pe.wait_ge(gu_in[j], 32 * count)
                        if not peeled:
                            pe.wait_ge(h_done, n)
                        for wm, dst, done in ((wg, gp, gate_made), (wu, up, up_made)):
                            for v in range(HALVES):
                                for k in range(KC):
                                    last = nc.tensor.matmul(dst[v][:], xT[:, k, :], wm[j][:, k, v * FH:(v + 1) * FH],
                                                            start=(k == 0), stop=(k == KC - 1))
                            last.then_inc(done, 1)

                    def turn_hidden(n, j):
                        pe.wait_ge(h_done, n + 1)
                        for g, chunks in enumerate(groups):
                            for f in chunks:
                                last = nc.tensor.transpose(hp[g][0:FW[f], f % 4, :], h[j][:, f * P:f * P + FW[f]], ident)
                            last.then_inc(h_turned, 1)

                    def down(n, j, count):
                        pe.wait_ge(d_in[j], DN * count)
                        pe.wait_ge(y_copied, n + 1)
                        for g, chunks in enumerate(groups):
                            pe.wait_ge(h_copied, n * NG + g + 1)
                            for f in chunks:
                                last = nc.tensor.matmul(yp[:], hT[0:FW[f], f, :], wd[j][0:FW[f], f, :], start=(f == 0),
                                                        stop=(f == FC - 1))
                        last.then_inc(y_made, 1)

                    turn_rows(0, 0, 1)
                    gate_up(0, 0, 1, peeled=True)
                    turn_rows(1, 1, 1)
                    def body(i, last_block=False):
                        for j in (1, 0):
                            n = i * 2 + 2 - j
                            gate_up(n, j, i + 2 - j)
                            turn_hidden(n - 1, 1 - j)
                            if not (last_block and j == 0):
                                turn_rows(n + 1, 1 - j, i + 2)
                            down(n - 1, 1 - j, i + 1)
                    with pe.Fori(0, NB // 2 - 1) as i:
                        body(i)
                    body(NB // 2 - 1, last_block=True)
                    turn_hidden(NB - 1, 0)
                    down(NB - 1, 0, NB // 2 + 1)

                @block.scalar
                def _(act):
                    def silu(n, peeled=False):
                        act.wait_ge(gate_made, n + 1)
                        if not peeled:
                            act.wait_ge(h_done, n)
                        for v in range(HALVES):
                            last = nc.scalar.activation(sg[:, v * FH:(v + 1) * FH], gp[v][:], ACT.Silu)
                        last.then_inc(sg_done, 1)

                    def copy_hidden(n):
                        act.wait_ge(y_made, n + 1)
                        for g, chunks in enumerate(groups):
                            act.wait_ge(h_turned, n * NG + g + 1)
                            full = [f for f in chunks if FW[f] == P]
                            last = nc.scalar.copy(hT[:, full[0]:full[-1] + 1, :], hp[g][:, 0:len(full), :])
                            for f in chunks:
                                if FW[f] < P:
                                    last = nc.scalar.copy(hT[0:FW[f], f, :], hp[g][0:FW[f], f % 4, :])
                            last.then_inc(h_copied, 1)

                    silu(0, peeled=True)
                    with act.Fori(1, NB) as n:
                        silu(n)
                        copy_hidden(n - 1)
                    copy_hidden(NB - 1)

                @block.vector
                def _(dve):
                    def copy_rows(n):
                        dve.wait_ge(x_turned, n + 2)
                        dve.wait_ge(up_made, n + 1)
                        nc.vector.tensor_copy(xT[:], xp[:]).then_inc(x_copied, 1)

                    def hidden(n, j):
                        dve.wait_ge(sg_done, n + 1)
                        dve.wait_ge(up_made, n + 2)
                        for v in range(HALVES):
                            last = nc.vector.tensor_tensor(h[j][:, v * FH:(v + 1) * FH], up[v][:],
                                                           sg[:, v * FH:(v + 1) * FH], ALU.mult)
                        last.then_inc(h_done, 1)

                    def copy_out(n, j, count):
                        dve.wait_ge(y_made, n + 2)
                        if positive(count):
                            dve.wait_ge(rows_out[j], 16 * before[j] + 16 * count)
                        nc.vector.tensor_copy(yb[j][:], yp[:]).then_inc(y_copied, 1)

                    copy_rows(0)
                    copy_rows(1)
                    hidden(0, 0)
                    def body(i, last_block=False):
                        for j in (1, 0):
                            n = i * 2 + 2 - j
                            if not (last_block and j == 0):
                                copy_rows(n + 1)
                            hidden(n, j)
                            copy_out(n - 1, 1 - j, i)
                    body(0)
                    with dve.Fori(1, NB // 2 - 1) as i:
                        body(i)
                    body(NB // 2 - 1, last_block=True)
                    copy_out(NB - 1, 0, NB // 2)

    def nearest_context(tag):
        with ExitStack() as st:
            sem = Semaphores(nc, st, tag)
            tmp = lambda n, s, dt=F32: st.enter_context(nc.sbuf_tensor(f"{tag}_{n}", s, dt))
            ps = lambda n, s: st.enter_context(nc.psum_tensor(f"{tag}_{n}", s, F32))
            sq, sqc = tmp("sq", [P, T, D]), tmp("sqc", [L, B, D])
            ss, rt, ri = tmp("ss", [P, T]), tmp("rt", [P, T]), tmp("ri", [P, T])
            ssc, rtc, ric = tmp("ssc", [L, B]), tmp("rtc", [L, B]), tmp("ric", [L, B])
            cn, cnT = tmp("cn", [L, B, D]), tmp("cnT", [P, KC, B, L])
            xs, sim = ([tmp(f"{n}{j}", s) for j in range(2)] for n, s in (("xs", [P, KC, P]), ("sim", [P, L])))
            m8, i8, i8f = [tmp(f"m8{j}", [P, 8]) for j in range(2)], [tmp(f"i8{j}", [P, 8], U32) for j in range(2)], \
                [tmp(f"if{j}", [P, 8]) for j in range(2)]
            oh, ohT = [tmp(f"oh{j}", [P, L]) for j in range(2)], [tmp(f"ohT{j}", [L, P]) for j in range(2)]
            sp_, tp_, yp = ([ps(f"{n}{j}", s) for j in range(2)] for n, s in
                            (("sp", [P, L]), ("tp", [L, P]), ("yp", [P, D])))
            cp = ps("cp", [P, KC, B, L])
            squared, summed, rooted, ready, c_turned, c_copied, staged, sim_made, scaled, max_done, idx_done, num_done, \
                hot, hot_turned, hot_copied, picked = (sem(n) for n in (
                    "sq", "sum", "root", "ready", "ct", "cc", "st", "sim", "sc", "max", "idx", "num", "hot", "ht", "hc", "p"))
            added = [sem(f"added{j}") for j in range(2)]
            with nc.Block() as block:
                @block.gpsimd
                def _(pool):
                    nc.gpsimd.tensor_tensor(sqc[:], ctx_tok[:], ctx_tok[:], ALU.mult).then_inc(squared, 1)

                @block.scalar
                def _(act):
                    act.wait_ge(summed, 2)
                    nc.scalar.activation(rt[:], ss[:], ACT.Sqrt).then_inc(rooted, 1)
                    nc.scalar.activation(rtc[:], ssc[:], ACT.Sqrt).then_inc(rooted, 1)
                    act.wait_ge(c_turned, 1)
                    nc.scalar.copy(cnT[:], cp[:]).then_inc(c_copied, 1)
                    for j in range(2):
                        act.sem_inc(added[j], 1)
                    with act.Fori(0, T // 2) as i:
                        for j in range(2):
                            act.wait_ge(added[j], i + 1)
                            nc.scalar.copy(xs[j][:], xnT[:, :, bass.ts(i * 2 + j, P)]).then_inc(staged, 1)
                        for j in range(2):
                            act.wait_ge(hot_turned, i * 2 + j + 1)
                            nc.scalar.copy(ohT[j][:], tp_[j][:]).then_inc(hot_copied, 1)

                @block.vector
                def _(dve):
                    nc.vector.tensor_tensor(sq[:], xn[:], xn[:], ALU.mult).then_inc(squared, 1)
                    dve.wait_ge(squared, 2)
                    nc.vector.tensor_reduce(ss[:], sq[:], AX_X, ALU.add).then_inc(summed, 1)
                    nc.vector.tensor_reduce(ssc[:], sqc[:], AX_X, ALU.add).then_inc(summed, 1)
                    dve.wait_ge(rooted, 2)
                    nc.vector.tensor_scalar(rt[:], rt[:], L2_EPS, None, ALU.max).then_inc(ready, 1)
                    nc.vector.tensor_scalar(rtc[:], rtc[:], L2_EPS, None, ALU.max).then_inc(ready, 1)
                    dve.wait_ge(ready, 2)
                    nc.vector.reciprocal(ri[:], rt[:]).then_inc(ready, 1)
                    nc.vector.reciprocal(ric[:], rtc[:]).then_inc(ready, 1)
                    dve.wait_ge(ready, 4)
                    nc.vector.tensor_tensor(cn[:], ctx_tok[:], bcast(ric[:], 2, D), ALU.mult).then_inc(ready, 1)
                    with dve.Fori(0, T // 2) as i:
                        for j in range(2):
                            t = i * 2 + j
                            dve.wait_ge(sim_made, t + 1)
                            nc.vector.tensor_scalar(sim[j][:], sp_[j][:], ri[:, bass.ds(t, 1)], None, ALU.mult).then_inc(scaled, 1)
                            dve.wait_ge(ready, 5)
                            dve.wait_ge(scaled, t + 1)
                            nc.vector.max(m8[j][:], sim[j][:]).then_inc(max_done, 1)
                            dve.wait_ge(ready, 5)
                            dve.wait_ge(max_done, t + 1)
                            nc.vector.max_index(i8[j][:], m8[j][:], sim[j][:]).then_inc(idx_done, 1)
                            dve.wait_ge(idx_done, t + 1)
                            nc.vector.tensor_copy(i8f[j][:], i8[j][:]).then_inc(num_done, 1)
                            dve.wait_ge(num_done, t + 1)
                            nc.vector.tensor_scalar(oh[j][:], const("iota64"), i8f[j][:, 0:1], None, ALU.is_equal)\
                                .then_inc(hot, 1)
                        for j in range(2):
                            dve.wait_ge(picked, i * 2 + j + 1)
                            nc.vector.tensor_tensor(x[:, i * 2 + j, :], yp[j][:], x[:, i * 2 + j, :], ALU.add)\
                                .then_inc(added[j], 1)

                @block.tensor
                def _(pe):
                    pe.wait_ge(ready, 5)
                    for b in range(B):
                        for k in range(KC):
                            last = nc.tensor.transpose(cp[:, k, b, :], cn[:, b, k * P:(k + 1) * P], ident[0:L, 0:L])
                    last.then_inc(c_turned, 1)
                    pe.wait_ge(c_copied, 1)
                    with pe.Fori(0, B) as b:
                        with pe.Fori(0, TB // 2) as p2:
                            i = b * (TB // 2) + p2
                            for j in range(2):
                                pe.wait_ge(staged, i * 2 + j + 1)
                                for k in range(KC):
                                    last = nc.tensor.matmul(sp_[j][:], xs[j][:, k, :], cnT[:, k, b, :], start=(k == 0),
                                                            stop=(k == KC - 1))
                                last.then_inc(sim_made, 1)
                            for j in range(2):
                                pe.wait_ge(c_copied, 1)
                                pe.wait_ge(hot, i * 2 + j + 1)
                                nc.tensor.transpose(tp_[j][:], oh[j][:], ident).then_inc(hot_turned, 1)
                            for j in range(2):
                                pe.wait_ge(c_copied, 1)
                                pe.wait_ge(hot_copied, i * 2 + j + 1)
                                nc.tensor.matmul(yp[j][:], ohT[j][:], ctx_tok[:, b, :], start=True, stop=True)\
                                    .then_inc(picked, 1)

    C_HALF, C_ONE, C_TWO = 1.5 * 2.0 ** 22, 1.5 * 2.0 ** 23, 1.5 * 2.0 ** 24
    QUANT_STEPS = 14

    def quantise(dve, dst, src, n, bufs, done, base, free=None):
        am, sc, a, m, u1, u2, u3 = bufs
        nb = n // FP4_BLOCK
        v3 = lambda ap: ap.rearrange("p (b i) -> p b i", i=FP4_BLOCK)
        am, sc, a, m, u1, u2, u3 = am[:, 0:nb], sc[:, 0:nb], a[:, 0:n], m[:, 0:n], u1[:, 0:n], u2[:, 0:n], u3[:, 0:n]
        after = lambda k: dve.wait_ge(done, base + k)
        nc.vector.tensor_reduce(am, v3(src), AX_X, ALU.max, apply_absolute_value=True).then_inc(done, 1)
        after(1)
        nc.vector.tensor_scalar(sc, am, 1.0 / 6.0, 1e-12, ALU.mult, ALU.max).then_inc(done, 1)
        after(2)
        nc.vector.reciprocal(am, sc).then_inc(done, 1)
        after(3)
        nc.vector.tensor_scalar(am, am, 1.0 - 2.0 ** -23, None, ALU.mult).then_inc(done, 1)
        after(4)
        nc.vector.tensor_tensor(v3(a), v3(src), bcast(am, 2, FP4_BLOCK), ALU.mult).then_inc(done, 1)
        after(5)
        nc.vector.tensor_scalar(m.bitcast(U32), a.bitcast(U32), 0x7FFFFFFF, None, ALU.bitwise_and).then_inc(done, 1)
        after(6)
        nc.vector.tensor_scalar(u1, m, 2.0, C_HALF, ALU.min, ALU.add).then_inc(done, 1)
        nc.vector.tensor_scalar(u2, m, 2.0, 4.0, ALU.max, ALU.min).then_inc(done, 1)
        nc.vector.tensor_scalar(u3, m, 4.0, C_TWO, ALU.max, ALU.add).then_inc(done, 1)
        after(8)
        nc.vector.tensor_scalar(u2, u2, C_ONE, C_ONE + 2.0, ALU.add, ALU.subtract).then_inc(done, 1)
        after(10)
        nc.vector.scalar_tensor_tensor(u1, u1, C_HALF, u2, ALU.subtract, ALU.add).then_inc(done, 1)
        after(11)
        nc.vector.scalar_tensor_tensor(u1, u3, C_TWO + 4.0, u1, ALU.subtract, ALU.add).then_inc(done, 1)
        after(12)
        nc.vector.scalar_tensor_tensor(u2.bitcast(U32), a.bitcast(U32), 0x80000000, u1.bitcast(U32), ALU.bitwise_and,
                                       ALU.bitwise_or).then_inc(done, 1)
        after(13)
        if free is not None:
            dve.wait_ge(*free)
        return nc.vector.tensor_tensor(v3(dst), v3(u2), bcast(sc, 2, FP4_BLOCK), ALU.mult)

    def fp4_feed_forward(tag, F):
        FC = -(-F // P)
        FW = [min(P, F - f * P) for f in range(FC)]
        FULL = F // P
        HALVES, FH = 2, F // 2
        with ExitStack() as st:
            tmp = lambda n, s: st.enter_context(nc.sbuf_tensor(f"{tag}_{n}", s, F32))
            bufs = [tmp(f"qb{k}", [P, FC * D if k > 1 else FC * D // FP4_BLOCK]) for k in range(7)]
            gT, uT, dT = tmp("gT", [P, KC, F]), tmp("uT", [P, KC, F]), tmp("dT", [P, FC, D])
            with ExitStack() as s2:
                sem = Semaphores(nc, s2, f"{tag}w")
                wn = [s2.enter_context(nc.sbuf_tensor(f"{tag}w_{n}", s, F32)) for n, s in
                      (("gate", [P, FC, D]), ("up", [P, FC, D]), ("down", [P, KC, F]))]
                tp = [s2.enter_context(nc.psum_tensor(f"{tag}w_tp{k}", [P, 512], F32)) for k in range(2)]
                cleared, loaded, steps, quantised, turned, copied = (sem(n) for n in ("clr", "ld", "q", "qd", "t", "tc"))
                jobs = []
                for m, dst in ((0, gT), (1, uT)):
                    for k in range(KC):
                        jobs.append((m, [(f, k) for f in range(4)], dst[:, k, 0:4 * P]))
                        jobs.append((m, [(f, k) for f in range(4, FC)], dst[:, k, 4 * P:F]))
                for f in range(0, FULL, 2):
                    fs = range(f, min(f + 2, FULL))
                    jobs.append((2, [(k, g) for g in fs for k in range(KC)],
                                 dT[:, fs[0]:fs[-1] + 1, :].rearrange("p f d -> p (f d)")))
                jobs.append((2, [(k, FULL) for k in range(KC)], dT[0:FW[FULL], FULL, :]))
                with nc.Block() as block:
                    @block.sync
                    def _(sp):
                        sp.wait_ge(cleared, 2)
                        for m, name in ((0, "L2_ffn_w_gate"), (1, "L2_ffn_w_up")):
                            sp.dma_start(wn[m][:, 0:FULL, :], ins[name][0:FULL * P, :].rearrange("(f p) k -> p f k", p=P))\
                                .then_inc(loaded, 16)
                            sp.dma_start(wn[m][0:F % P, FULL, :], ins[name][FULL * P:F, :]).then_inc(loaded, 16)
                        sp.dma_start(wn[2][:], ins["L2_ffn_w_down"].rearrange("(k p) f -> p k f", p=P)).then_inc(loaded, 16)

                    @block.vector
                    def _(dve):
                        for m in range(2):
                            nc.vector.memset(wn[m][:, FULL, :], 0.0).then_inc(cleared, 1)
                        dve.wait_ge(loaded, 16 * 5)
                        for m in range(3):
                            flat = wn[m][:].rearrange("p a b -> p (a b)")
                            quantise(dve, flat, flat, flat.shape[1], bufs, steps, m * (QUANT_STEPS - 1)).then_inc(quantised, 1)

                    @block.tensor
                    def _(pe):
                        for n, (m, parts, dst) in enumerate(jobs):
                            pe.wait_ge(quantised, m + 1)
                            if n >= 2:
                                pe.wait_ge(copied, n - 1)
                            at = 0
                            for r, c in parts:
                                if m < 2:
                                    last = nc.tensor.transpose(tp[n % 2][:, at:at + FW[r]],
                                                               wn[m][0:FW[r], r, c * P:(c + 1) * P], ident[0:FW[r], 0:FW[r]])
                                    at += FW[r]
                                else:
                                    last = nc.tensor.transpose(tp[n % 2][0:FW[c], at:at + P],
                                                               wn[m][:, r, c * P:c * P + FW[c]], ident)
                                    at += P
                            last.then_inc(turned, 1)

                    @block.scalar
                    def _(act):
                        for n, (m, parts, dst) in enumerate(jobs):
                            act.wait_ge(turned, n + 1)
                            nc.scalar.copy(dst, tp[n % 2][0:dst.shape[0], 0:dst.shape[1]]).then_inc(copied, 1)

            with ExitStack() as s2:
                sem = Semaphores(nc, s2, tag)
                tmp2 = lambda n, s: s2.enter_context(nc.sbuf_tensor(f"{tag}_{n}", s, F32))
                ps = lambda n, s: s2.enter_context(nc.psum_tensor(f"{tag}_{n}", s, F32))
                xq, xT, sg, h, hq, hT = tmp2("xq", [P, D]), tmp2("xT", [P, KC, P]), tmp2("sg", [P, F]), tmp2("h", [P, F]), \
                    tmp2("hq", [P, F]), tmp2("hT", [P, FC, P])
                gp, up = ([ps(f"{n}{k}", [P, FH]) for k in range(HALVES)] for n in ("gp", "up"))
                hp = [ps(f"hp{k}", [P, 4, P]) for k in range(2)]
                xp, yp = ps("xp", [P, KC, P]), ps("yp", [P, D])
                groups = [list(range(g, min(g + 4, FC))) for g in range(0, FC, 4)]
                NG = len(groups)
                xsteps, hsteps, x_quant, x_turned, x_copied, gate_made, up_made, sg_done, h_done, h_quant, h_turned, h_copied, \
                    y_made, added = (sem(n) for n in ("xs", "hs", "xq", "xt", "xc", "gate", "up", "sg", "h", "hq", "ht", "hc",
                                                      "y", "added"))
                with nc.Block() as block:
                    @block.vector
                    def _(dve):
                        def rows(n):
                            quantise(dve, xq[:], xn[:, n, :], D, bufs, xsteps, n * (QUANT_STEPS - 1),
                                     (x_turned, n) if positive(n) else None).then_inc(x_quant, 1)

                        def hidden(n):
                            dve.wait_ge(sg_done, n + 1)
                            dve.wait_ge(up_made, n + 1)
                            for v in range(HALVES):
                                last = nc.vector.tensor_tensor(h[:, v * FH:(v + 1) * FH], up[v][:], sg[:, v * FH:(v + 1) * FH],
                                                               ALU.mult)
                            last.then_inc(h_done, 1)
                            dve.wait_ge(h_done, n + 1)
                            quantise(dve, hq[:], h[:], F, bufs, hsteps, n * (QUANT_STEPS - 1),
                                     (h_turned, n * NG) if positive(n) else None).then_inc(h_quant, 1)

                        def add(n):
                            dve.wait_ge(y_made, n + 2)
                            nc.vector.tensor_tensor(x[:, n, :], yp[:], x[:, n, :], ALU.add).then_inc(added, 1)

                        rows(0)
                        rows(1)
                        hidden(0)
                        with dve.Fori(1, T - 1) as n:
                            rows(n + 1)
                            hidden(n)
                            add(n - 1)
                        hidden(T - 1)
                        add(T - 2)
                        add(T - 1)

                    @block.scalar
                    def _(act):
                        def copy_rows(n):
                            act.wait_ge(x_turned, n + 1)
                            if positive(n):
                                act.wait_ge(up_made, n)
                            nc.scalar.copy(xT[:], xp[:]).then_inc(x_copied, 1)

                        def silu(n):
                            act.wait_ge(gate_made, n + 1)
                            if positive(n):
                                act.wait_ge(h_done, n)
                            for v in range(HALVES):
                                last = nc.scalar.activation(sg[:, v * FH:(v + 1) * FH], gp[v][:], ACT.Silu)
                            last.then_inc(sg_done, 1)

                        def copy_hidden(n):
                            act.wait_ge(y_made, n + 1)
                            for g, chunks in enumerate(groups):
                                act.wait_ge(h_turned, n * NG + g + 1)
                                full = [f for f in chunks if FW[f] == P]
                                last = nc.scalar.copy(hT[:, full[0]:full[-1] + 1, :], hp[g][:, 0:len(full), :])
                                for f in chunks:
                                    if FW[f] < P:
                                        last = nc.scalar.copy(hT[0:FW[f], f, :], hp[g][0:FW[f], f % 4, :])
                                last.then_inc(h_copied, 1)

                        copy_rows(0)
                        silu(0)
                        copy_rows(1)
                        with act.Fori(1, T - 1) as n:
                            silu(n)
                            copy_rows(n + 1)
                            copy_hidden(n - 1)
                        silu(T - 1)
                        copy_hidden(T - 2)
                        copy_hidden(T - 1)

                    @block.tensor
                    def _(pe):
                        def turn_rows(n):
                            pe.wait_ge(x_quant, n + 1)
                            if positive(n):
                                pe.wait_ge(x_copied, n)
                            for k in range(KC):
                                last = nc.tensor.transpose(xp[:, k, :], xq[:, k * P:(k + 1) * P], ident)
                            last.then_inc(x_turned, 1)

                        def gate_up(n):
                            pe.wait_ge(x_copied, n + 1)
                            if positive(n):
                                pe.wait_ge(h_done, n)
                            for wm, dst, done in ((gT, gp, gate_made), (uT, up, up_made)):
                                for v in range(HALVES):
                                    for k in range(KC):
                                        last = nc.tensor.matmul(dst[v][:], xT[:, k, :], wm[:, k, v * FH:(v + 1) * FH],
                                                                start=(k == 0), stop=(k == KC - 1))
                                last.then_inc(done, 1)

                        def turn_hidden(n):
                            pe.wait_ge(h_quant, n + 1)
                            for g, chunks in enumerate(groups):
                                for f in chunks:
                                    last = nc.tensor.transpose(hp[g][0:FW[f], f % 4, :], hq[:, f * P:f * P + FW[f]], ident)
                                last.then_inc(h_turned, 1)

                        def down(n):
                            pe.wait_ge(added, n + 1)
                            for g, chunks in enumerate(groups):
                                pe.wait_ge(h_copied, n * NG + g + 1)
                                for f in chunks:
                                    last = nc.tensor.matmul(yp[:], hT[0:FW[f], f, :], dT[0:FW[f], f, :], start=(f == 0),
                                                            stop=(f == FC - 1))
                            last.then_inc(y_made, 1)

                        pe.sem_inc(added, 1)
                        pe.sem_inc(y_made, 1)
                        turn_rows(0)
                        gate_up(0)
                        turn_rows(1)
                        with pe.Fori(1, T - 1) as n:
                            gate_up(n)
                            turn_rows(n + 1)
                            turn_hidden(n - 1)
                            down(n - 1)
                        gate_up(T - 1)
                        turn_hidden(T - 2)
                        down(T - 2)
                        turn_hidden(T - 1)
                        down(T - 1)

    stages = [
        lambda: (normalise("n0", x, xn),
                 cross_attention("a0", w.q0, w.kv0[:, :, 0:D], w.kv0[:, :, D:2 * D], w.o0, w.bq0, w.bk0, w.bv0, w.bo0)),
        lambda: (normalise("n1", x, xn),
                 experts("e0", 0, x, w.router[0], ins["L0_ffn_gate_proj"], ins["L0_ffn_up_proj"], ins["L0_ffn_down_proj"], 704)),
        lambda: (normalise("n2", x, xn), cross_attention("a1", None, None, None, w.fc1, None, None, None, w.bo1, features=True)),
        lambda: (normalise("n3", x, inner), normalise("r3", inner, xn, w.ln1[:]), latent_attention("l1", inner)),
        lambda: (normalise("n4", inner, xn, w.ln2[:]),
                 experts("e1", 1, inner, w.router[1], ins["L1_ffn_Wg"], ins["L1_ffn_Wu"], ins["L1_ffn_Wd"], 256, shared=True,
                         bias=w.rbias, outer=x)),
        lambda: (normalise("n5", x, xn), nearest_context("c2")),
        lambda: (normalise("n6", x, xn), fp4_feed_forward("f2", 704)),
        lambda: (normalise("n7", x, xn), cross_attention("a3", w.q3, w.k3, w.v3, w.o3, w.bq3, w.bk3, w.bv3, w.bo3)),
        lambda: (normalise("n8", x, xn),
                 experts("e3", 2, x, w.router[2], ins["L3_ffn_W1"], ins["L3_ffn_W2"], ins["L3_ffn_W3"], 512)),
    ]
    for stage in stages:
        stage()

    with ExitStack() as st:
        stored = st.enter_context(nc.semaphore("stored"))
        with nc.Block() as block:
            @block.sync
            def _(sp):
                sp.dma_start(out.rearrange("b (t p) d -> p (b t) d", p=P), x[:]).then_inc(stored, 16)
                sp.wait_ge(stored, 16)


def kernel(**inputs):
    import numpy as _np
    import concourse.bacc as _bacc
    from concourse import mybir as _mybir
    from concourse.bass_utils import run_bass_kernel_spmd as _run

    a = {k: _np.asarray(v) for k, v in inputs.items()}
    D_ = a["x"].shape[-1]
    bkv = a.pop("L0_xattn_bkv")
    a["L0_xattn_bk"], a["L0_xattn_bv"] = bkv[:D_], bkv[D_:]
    for k in ("w_q", "w_k", "w_v", "w_o"):
        a[f"L3_xattn_{k}T"] = a.pop(f"L3_xattn_{k}").T
    a["L1_xattn_fm_wT"] = a.pop("L1_xattn_fm_w").T
    a["L1_xattn_fc_wT"] = a.pop("L1_xattn_fc_w").T
    for k in "gud":
        a[f"L1_ffn_W{k}"] = _np.concatenate([a.pop(f"L1_ffn_W{k}_r"), a.pop(f"L1_ffn_W{k}_s")[None]], axis=0)
    a["consts"] = _constants()

    nc = _bacc.Bacc("TRN2", target_bir_lowering=False, num_devices=1)
    arrays, ins = {}, {}
    for name, v in a.items():
        v = _np.ascontiguousarray(v)
        arrays[f"in_{name}"] = v
        ins[name] = nc.dram_tensor(f"in_{name}", v.shape, _mybir.dt.from_np(v.dtype), kind="ExternalInput").ap()
    out = nc.dram_tensor("out_x", a["x"].shape, F32, kind="ExternalOutput").ap()
    program(nc, ins, out)
    r = _run(nc, [arrays], core_ids=[0])
    return r.results[0]["out_x"]
```
